# Optimizing a Trainium2 kernel written in Bass

```python
import numpy as np
import jax
import jax.numpy as jnp

def _softmax(x, axis=-1):
    return jax.nn.softmax(x, axis=axis)

def _gelu(x):
    return jax.nn.gelu(x, approximate=True)

def _silu(x):
    return jax.nn.silu(x)

def _sigmoid(x):
    return jax.nn.sigmoid(x)

def _layernorm(x, axis=-1, eps=1e-05):
    m = jnp.mean(x, axis=axis, keepdims=True)
    v = jnp.var(x, axis=axis, keepdims=True)
    return (x - m) / jnp.sqrt(v + eps)

def _scatter_add(tgt, idx, src, axis=0):
    return tgt.at[idx].add(src)

def _segment_sum(src, seg, n):
    return jax.ops.segment_sum(src, seg, n)
kernel_name = 'mk_seq_preln_d1_jaxref_r4_13ca23'

def setup_inputs(seed: int=0):
    np.random.seed(seed)
    _w = jnp.asarray

    def _L0_attn_setup():
        import jax, jax.numpy as jnp
        import numpy as np
        EMBED = 256
        EXPAND = 128
        B, T = (4, 512)
        PI = 3.141592653589793
        EPS = 1e-05

        def _gla_scan(q, k, v, g):
            Bq, Tq, H, Dk = q.shape
            Dv = v.shape[-1]
            scale = Dk ** (-0.5)

            def step(S, inp):
                qt, kt, vt, gt = inp
                S = S * jnp.exp(gt)[..., None] + kt[..., None] * vt[..., None, :]
                o = jnp.einsum('bhk,bhkv->bhv', qt * scale, S)
                return (S, o)
            S0 = jnp.zeros((Bq, H, Dk, Dv), q.dtype)
            seq = tuple((jnp.moveaxis(a, 1, 0) for a in (q, k, v, g)))
            _, out = jax.lax.scan(step, S0, seq)
            return jnp.moveaxis(out, 0, 1)
        key = jax.random.key(seed)
        ks = jax.random.split(key, 8)
        std = 0.02
        return {'x': jax.random.normal(ks[0], (B, T, EMBED), jnp.float32), 'wq': jax.random.normal(ks[1], (EMBED, EMBED), jnp.float32) * std, 'wk': jax.random.normal(ks[2], (EMBED, EMBED), jnp.float32) * std, 'wv': jax.random.normal(ks[3], (EMBED, EMBED), jnp.float32) * std, 'wo': jax.random.normal(ks[4], (EMBED, EMBED), jnp.float32) * std, 'wg1': jax.random.normal(ks[5], (EMBED, EXPAND), jnp.float32) * std, 'wg2': jax.random.normal(ks[6], (EXPAND, EMBED), jnp.float32) * std, 'norm_w': jnp.ones((EMBED,), jnp.float32)}
    _L0_attn_in = _L0_attn_setup()

    def _L0_ffn_setup():
        import jax, jax.numpy as jnp
        import numpy as np
        E, D, F = (8, 256, 1024)
        B, S = (4, 512)

        def _layernorm(x, g, b, eps=1e-05):
            mu = jnp.mean(x, axis=-1, keepdims=True)
            var = jnp.var(x, axis=-1, keepdims=True)
            return (x - mu) * jax.lax.rsqrt(var + eps) * g + b
        key = jax.random.key(seed)
        ks = jax.random.split(key, 5)
        return {'input_features': jax.random.normal(ks[0], (B, S, D), jnp.float32), 'centroids': jax.random.normal(ks[1], (E, D), jnp.float32) * 0.1, 'ln_g': jnp.ones((E, D), jnp.float32), 'ln_b': jnp.zeros((E, D), jnp.float32), 'w1': jax.random.normal(ks[2], (E, F, D), jnp.float32) * (1.0 / np.sqrt(D).astype(np.float32)), 'b1': jnp.zeros((E, F), jnp.float32), 'w2': jax.random.normal(ks[3], (E, D, F), jnp.float32) * (1.0 / np.sqrt(F).astype(np.float32)), 'b2': jnp.zeros((E, D), jnp.float32)}
    _L0_ffn_in = _L0_ffn_setup()
    _d = {'L0_attn_x': _L0_attn_in['x'], 'L0_attn_wq': _L0_attn_in['wq'], 'L0_attn_wk': _L0_attn_in['wk'], 'L0_attn_wv': _L0_attn_in['wv'], 'L0_attn_wo': _L0_attn_in['wo'], 'L0_attn_wg1': _L0_attn_in['wg1'], 'L0_attn_wg2': _L0_attn_in['wg2'], 'L0_attn_norm_w': _L0_attn_in['norm_w'], 'L0_ffn_centroids': _L0_ffn_in['centroids'], 'L0_ffn_ln_g': _L0_ffn_in['ln_g'], 'L0_ffn_ln_b': _L0_ffn_in['ln_b'], 'L0_ffn_w1': _L0_ffn_in['w1'], 'L0_ffn_b1': _L0_ffn_in['b1'], 'L0_ffn_w2': _L0_ffn_in['w2'], 'L0_ffn_b2': _L0_ffn_in['b2']}
    _x0 = _d['L0_attn_x']
    _d['L0_attn_x'] = jax.random.normal(jax.random.fold_in(jax.random.key(seed), 1), (8, 512, 256), dtype=_x0.dtype)
    del _x0
    return _d

def reference(L0_attn_x, L0_attn_wq, L0_attn_wk, L0_attn_wv, L0_attn_wo, L0_attn_wg1, L0_attn_wg2, L0_attn_norm_w, L0_ffn_centroids, L0_ffn_ln_g, L0_ffn_ln_b, L0_ffn_w1, L0_ffn_b1, L0_ffn_w2, L0_ffn_b2):

    def _L0_attn_ref(x, wq, wk, wv, wo, wg1, wg2, norm_w):
        import jax, jax.numpy as jnp
        import numpy as np
        EMBED = 256
        EXPAND = 128
        B, T = (4, 512)
        PI = 3.141592653589793
        EPS = 1e-05

        def _gla_scan(q, k, v, g):
            Bq, Tq, H, Dk = q.shape
            Dv = v.shape[-1]
            scale = Dk ** (-0.5)

            def step(S, inp):
                qt, kt, vt, gt = inp
                S = S * jnp.exp(gt)[..., None] + kt[..., None] * vt[..., None, :]
                o = jnp.einsum('bhk,bhkv->bhv', qt * scale, S)
                return (S, o)
            S0 = jnp.zeros((Bq, H, Dk, Dv), q.dtype)
            seq = tuple((jnp.moveaxis(a, 1, 0) for a in (q, k, v, g)))
            _, out = jax.lax.scan(step, S0, seq)
            return jnp.moveaxis(out, 0, 1)
        Bx, Tx, E = x.shape
        d = EXPAND
        H = E // d
        q = jax.nn.silu(x @ wq)
        k = jax.nn.sigmoid(x @ wk)
        v = x @ wv
        f = 1.0 - k
        log_f = jnp.log(f)
        q4 = q.reshape(Bx, Tx, H, d)
        k4 = k.reshape(Bx, Tx, H, d)
        v4 = v.reshape(Bx, Tx, H, d)
        f4 = f.reshape(Bx, Tx, H, d)
        g4 = log_f.reshape(Bx, Tx, H, d)
        sign_f = jnp.sign(f4 - 0.5)
        theta = jnp.cumsum(sign_f, axis=1) * PI
        sin, cos = (jnp.sin(theta), jnp.cos(theta))
        qr = jnp.concatenate([q4 * cos, q4 * sin], axis=-1)
        kr = jnp.concatenate([k4 * cos, k4 * sin], axis=-1)
        g = jnp.concatenate([g4, g4], axis=-1)
        out = _gla_scan(qr, kr, v4, g)
        out = out.reshape(Bx, Tx, E)
        gate = jax.nn.sigmoid(x @ wg1 @ wg2)
        out = out * gate
        mu = jnp.mean(out, axis=-1, keepdims=True)
        var = jnp.mean(jnp.square(out - mu), axis=-1, keepdims=True)
        out = (out - mu) * jax.lax.rsqrt(var + EPS) * norm_w
        return out @ wo

    def _L0_ffn_ref(input_features, centroids, ln_g, ln_b, w1, b1, w2, b2):
        import jax, jax.numpy as jnp
        import numpy as np
        E, D, F = (8, 256, 1024)
        B, S = (4, 512)

        def _layernorm(x, g, b, eps=1e-05):
            mu = jnp.mean(x, axis=-1, keepdims=True)
            var = jnp.var(x, axis=-1, keepdims=True)
            return (x - mu) * jax.lax.rsqrt(var + eps) * g + b
        Bf, Sf, Df = input_features.shape
        x = input_features.reshape(-1, Df)
        aff = x @ centroids.T
        assign = jnp.argmax(aff, axis=1)
        order = jnp.argsort(assign)
        xs = x[order]
        es = assign[order]
        alpha = jax.nn.sigmoid(jnp.take_along_axis(aff[order], es[:, None], axis=1))
        nE = centroids.shape[0]
        y = jnp.zeros_like(xs)
        for e in range(nE):
            h = _layernorm(xs, ln_g[e], ln_b[e])
            h = jax.nn.relu(h @ w1[e].T + b1[e])
            ye = xs + h @ w2[e].T + b2[e]
            y = y + jnp.where((es == e)[:, None], ye, 0.0)
        out_sorted = alpha * y + (1.0 - alpha) * xs
        inv = jnp.argsort(order)
        return out_sorted[inv].reshape(Bf, Sf, Df)
    x = L0_attn_x
    x = x + _L0_attn_ref(_layernorm(x, axis=-1), L0_attn_wq, L0_attn_wk, L0_attn_wv, L0_attn_wo, L0_attn_wg1, L0_attn_wg2, L0_attn_norm_w)
    x = x + _L0_ffn_ref(_layernorm(x, axis=-1), L0_ffn_centroids, L0_ffn_ln_g, L0_ffn_ln_b, L0_ffn_w1, L0_ffn_b1, L0_ffn_w2, L0_ffn_b2)
    return x

_drawn_inputs = setup_inputs


def setup_inputs(seed=0):
    import zlib

    import numpy as np

    out = dict(_drawn_inputs(seed))
    spreads = {'L0_attn_norm_w': (1.0, 0.2),
     'L0_ffn_ln_g': (1.0, 0.2),
     'L0_ffn_ln_b': (0.0, 0.277),
     'L0_ffn_b1': (0.0, 0.273),
     'L0_ffn_b2': (0.0, 0.1)}
    factors = {}
    for name, (base, spread) in spreads.items():
        noise = np.random.default_rng([zlib.crc32(name.encode()), seed]).standard_normal(out[name].shape)
        drawn = base * np.exp(spread * noise) if base else spread * noise
        out[name] = jnp.asarray(drawn.astype(out[name].dtype))
    for name, factor in factors.items():
        out[name] = (out[name] * factor).astype(out[name].dtype)
    return out
```

```python
from contextlib import ExitStack
from collections import namedtuple

import numpy as np
import concourse.bass as bass
from concourse import mybir

ALU = mybir.AluOpType
ACT = mybir.ActivationFunctionType
F32 = mybir.dt.float32
BF16 = mybir.dt.bfloat16
I32 = mybir.dt.int32
U8 = mybir.dt.uint8
AX_X = mybir.AxisListType.X

P = 128
EPS = 1e-5

Seq = namedtuple("Seq", "half par")


def before(s, n):
    v = s.par - n
    return Seq(s.half + v // 2, v % 2)


def number(s):
    return s.half * 2 + s.par


def need(eng, sem, per, s, k):
    base = per * s.par + k
    if isinstance(s.half, int):
        if 2 * per * s.half + base > 0:
            eng.wait_ge(sem, 2 * per * s.half + base)
    else:
        eng.wait_ge(sem, s.half * (2 * per) + base)


def build_program(nc, x, wq, wk, wv, wo, wg1, wg2, norm_w, centroids_t, ln_g, ln_b, w1_t, b1, w2_t, b2, out):
    NSEQ, T, D = x.shape
    G1 = wg1.shape[1]
    E, F = b1.shape
    TJ = T // P
    DC = D // P
    H = D // P
    NCH = H * TJ
    FC = F // P
    N = NSEQ * T
    NT = N // P
    TILES = NT + E - 1
    TS = TILES + 1
    LEVELS = 7
    HALF = P // 2
    QSCALE = (2.0 * P) ** -0.5
    RW = 2 * D + 1
    SKIP = 2 * N
    assert D == 2 * P and T == 4 * P and G1 == P and NSEQ % 2 == 0 and E == 8

    rows = nc.dram_tensor("routed_rows", (N, RW), F32, kind="Internal").ap()

    ctx = ExitStack()
    with ctx:
        def sb(name, shape, dt):
            return ctx.enter_context(nc.sbuf_tensor(name, shape, dt))

        def sem(name):
            return ctx.enter_context(nc.semaphore(name))

        w1_sb = sb("w1_sb", [P, E * DC * F], F32)
        PHASE1_AB = 24576
        ARENA = 33408
        arena = sb("arena", [P, ARENA], F32)

        class Layout:
            def __init__(self, at, end):
                self.at, self.end = at, end

            def take(self, n):
                self.at += n
                assert self.at <= self.end, (self.at, self.end)
                return arena[:, self.at - n:self.at]

        lay = Layout(0, PHASE1_AB)
        x_sb = [lay.take(TJ * D) for _ in range(2)]
        xn = lay.take(TJ * D)
        xn_t = lay.take(DC * T)
        q_raw = lay.take(H * T)
        qk = lay.take(H * T)
        g1_t = lay.take(T)
        k_dec = [lay.take(H * T) for _ in range(2)]
        q_dec = [lay.take(H * T) for _ in range(2)]
        decay = [lay.take(2 * H * T) for _ in range(2)]
        v_sb = [lay.take(TJ * D) for _ in range(2)]
        gate = [lay.take(TJ * D) for _ in range(2)]
        attn_t = [lay.take(NCH * P) for _ in range(2)]
        k_tok = lay.take((TJ - 1) * D)
        state = lay.take((TJ - 1) * D)
        wq_sb = lay.take(DC * D)
        wk_sb = lay.take(DC * D)
        wv_sb = lay.take(DC * D)
        wg1_sb = lay.take(DC * G1)
        wg2_sb = lay.take(D)
        lay = Layout(PHASE1_AB, ARENA)
        o_sb = lay.take(TJ * D)
        o_t = lay.take(DC * T)
        x_res = lay.take(TJ * D)
        x1 = lay.take(TJ * D)
        xn2 = lay.take(TJ * D)
        xn2_t = lay.take(DC * T)
        row_sb = lay.take(TJ * RW + 4)[:, 0:TJ * RW]
        wo_sb = lay.take(DC * D)
        mask_f = xn2[:, 0:NCH * HALF]
        lay3 = Layout(0, PHASE1_AB)
        w2_sb = lay3.take(E * FC * D)
        b1_sb = lay3.take(E * F)
        lay3 = Layout(PHASE1_AB, ARENA)
        gathered = [lay3.take(RW + 3)[:, 0:RW] for _ in range(2)]
        xl_t = [lay3.take(DC * P) for _ in range(2)]
        h_sb = lay3.take(F)
        h_t = lay3.take(F)
        y_sb = lay3.take(D)
        y_out = [lay3.take(D) for _ in range(2)]
        b2_sb = lay3.take(E * D)
        lay2 = Layout(PHASE1_AB, ARENA)
        WIDE = NT * E
        aff_max = lay2.take(NT)
        is_max = lay2.take(WIDE)
        first = lay2.take(NT)
        onehot = lay2.take(WIDE)
        count_e = lay2.take(WIDE)
        cum_e = lay2.take(WIDE)
        place = lay2.take(WIDE)
        slot = lay2.take(NT)
        slot_i = lay2.take(NT).bitcast(I32)
        hi_i = lay2.take(NT).bitcast(I32)
        lo_i = lay2.take(NT).bitcast(I32)
        hi_f = lay2.take(NT)
        lo_f = lay2.take(NT)
        small = lay2.take(12 * E)
        ntile_i = lay2.take(2 * E).bitcast(I32)
        ge_f = lay2.take(TS * E)
        texp_f = lay2.take(TS)
        slot_f = lay2.take(4 * TS)
        lo_hot = lay2.take(NT * P // 2).bitcast(BF16)
        hi_hot = lay2.take(NT * 3 * TS // 2).bitcast(BF16)

        ident = sb("ident", [P, P], F32)
        ones = sb("ones", [P, P], F32)
        below = sb("below", [P, P], F32)
        masks = sb("masks", [P, LEVELS * NCH * HALF], U8)
        norm_col = sb("norm_col", [P, DC], F32)
        cent_sb = sb("cent_sb", [P, DC * E], F32)
        g_col = sb("g_col", [P, E * DC], F32)
        b_col = sb("b_col", [P, E * DC], F32)
        aff = sb("aff", [P, NT * E], F32)
        iota_e = sb("iota_e", [P, E], F32)
        iota_t = sb("iota_t", [P, TS], F32)
        iota_r = sb("iota_r", [P, P], F32)
        iota_p = sb("iota_p", [P, 1], F32)
        minus_half = sb("minus_half", [P, TJ], F32)
        tile_expert = sb("tile_expert", [P, TS], I32)
        take_idx = sb("take_idx", [P, TS], I32)
        put_idx = sb("put_idx", [P, TS], I32)
        take_now = sb("take_now", [P, 2], I32)
        put_now = sb("put_now", [P, 2], I32)
        diag = sb("diag", [P, NCH], F32)
        aff_best = sb("aff_best", [P, TJ], F32)
        stat = {n: sb(f"{n}_stat", [P, TJ, 6], F32) for n in "xouz"}
        mom = {n: sb(f"{n}_mom", [P, TJ, 2], F32) for n in "xouz"}
        var_eps = {n: sb(f"{n}_vareps", [P, TJ], F32) for n in "xouz"}
        rstd = {n: sb(f"{n}_rstd", [P, TJ], F32) for n in "xouz"}
        shift = {n: sb(f"{n}_shift", [P, TJ], F32) for n in "uz"}

        bank_a = [ctx.enter_context(nc.psum_tensor(f"bank_a{i}", [P, 512], F32)) for i in range(2)]
        bank_l = [ctx.enter_context(nc.psum_tensor(f"bank_l{i}", [P, 512], F32)) for i in range(2)]
        bank_b = [ctx.enter_context(nc.psum_tensor(f"bank_b{i}", [P, 512], F32)) for i in range(2)]
        bank_c = [ctx.enter_context(nc.psum_tensor(f"bank_c{i}", [P, 512], F32)) for i in range(2)]

        s_x = [sem(f"x_loaded{i}") for i in range(2)]
        s_xres = sem("xres_loaded")
        s_row_out = sem("rows_stored")
        s_wqk = sem("wqk_loaded")
        s_wvg = sem("wvg_loaded")
        s_wo_in = sem("wo_loaded")
        s_small = sem("small_loaded")
        s_w1 = sem("w1_loaded")
        s_w2 = sem("w2_loaded")
        s_b1 = sem("b1_loaded")
        s_b2 = sem("b2_loaded")
        s_const = sem("constants_ready")
        s_setup = sem("setup_step")
        s_held = sem("wait_held")
        s_wo = sem("wo_scaled")
        s_stat = {n: sem(f"{n}_stats") for n in "xouz"}
        s_mom = {n: sem(f"{n}_moments") for n in "xouz"}
        s_ve = {n: sem(f"{n}_var_eps") for n in "xouz"}
        s_rstd = {n: sem(f"{n}_rstd_ready") for n in "xouz"}
        s_shift = {n: sem(f"{n}_shift_ready") for n in "uz"}
        s_xn = sem("xn_ready")
        s_tp = sem("xn_transposed")
        s_xnt = sem("xnt_ready")
        s_kz = sem("kz_done")
        s_k = sem("k_ready")
        s_f = sem("f_ready")
        s_f0 = sem("decay0_ready")
        s_qz = sem("qz_done")
        s_qs = sem("q_sigmoid_ready")
        s_q = sem("q_ready")
        s_g1z = sem("g1z_done")
        s_g1 = sem("g1_ready")
        s_vz = sem("vz_done")
        s_v = sem("v_ready")
        s_gz = sem("gatez_done")
        s_gate = sem("gate_ready")
        s_qk = sem("qk_ready")
        s_tree = sem("decay_tree")
        s_q0 = sem("q0_ready")
        s_dz = sem("diag_summed")
        s_diag = sem("diag_ready")
        s_at0 = sem("attn_diag_set")
        s_lev = sem("level_scores")
        s_up = sem("level_update")
        s_pick = sem("level_picked")
        s_k7 = sem("k_transposed")
        s_kt = sem("k_tok_ready")
        s_kv = sem("kv_done")
        s_state = sem("state_ready")
        s_o = sem("o_done")
        s_og = sem("o_gated")
        s_on = sem("on_ready")
        s_ot = sem("on_transposed")
        s_ont = sem("ont_ready")
        s_y = sem("proj_done")
        s_x1 = sem("x1_ready")
        s_xn2 = sem("xn2_ready")
        s_t2 = sem("xn2_transposed")
        s_xn2t = sem("xn2t_ready")
        s_affz = sem("aff_done")
        s_best = sem("best_ready")
        s_aff = sem("aff_ready")
        s_alpha = sem("alpha_ready")
        s_base = sem("base_ready")
        s_zn = sem("zn_ready")
        s_r = sem("route_step")
        s_rank = sem("ranks_done")
        s_hot = sem("onehots_ready")
        s_inv = sem("inverse_done")
        s_idx = sem("indices_ready")
        s_take = sem("take_idx_ready")
        s_rows = [sem(f"rows_gathered{i}") for i in range(2)]
        s_zt = sem("z_transposed")
        s_xl = sem("xl_ready")
        s_h = sem("h_done")
        s_hb = sem("h_biased")
        s_ht = sem("h_transposed")
        s_hr = sem("h_relu")
        s_ye = sem("y_done")
        s_yb = sem("y_biased")
        s_yo = sem("y_ready")
        s_put = sem("put_idx_ready")
        s_out = [sem(f"rows_out{i}") for i in range(2)]

        def tiles(buf, w=D):
            return buf.rearrange("p (j d) -> p j d", d=w)

        def tree(buf, l):
            n = H * T
            at = 0 if l == 0 else 2 * n - (2 * n >> l)
            return buf[:, at:at + (n >> l)]

        def halves(ap, l):
            return ap.rearrange("p (n two h) -> p n two h", two=2, h=2 ** l)

        def factor(buf, l, which):
            n = H * T >> (l + 1)
            f = tree(buf, l).rearrange("p (n two) -> p n two", two=2)[:, :, which:which + 1]
            return f.broadcast_to([P, n, 2 ** l])

        def packed(ap, l):
            return ap.rearrange("p (n h) -> p n h", h=2 ** l)

        x_t = x.rearrange("b (j p) d -> b p j d", p=P)
        rows_t = rows.rearrange("(b j p) r -> b p j r", p=P, j=TJ)

        def seq_rows(ap, s):
            if isinstance(s.half, int):
                return ap[number(s)]
            return ap[bass.ds(number(s), 1)].squeeze(0)

        def need_apart(eng, sem, per, s, k):
            need(eng, sem, per, s, k)
            eng.sem_inc(s_held, 1)

        def column(buf, t):
            if isinstance(t.half, int):
                return buf[:, number(t):number(t) + 1]
            return buf[:, bass.ds(number(t), 1)]

        def aff_of(c):
            if isinstance(c.half, int):
                return aff[:, number(c) * TJ * E:(number(c) + 1) * TJ * E]
            return aff[:, bass.ds(number(c) * (TJ * E), TJ * E)]

        def expert_of(t):
            if isinstance(t.half, int):
                return tile_expert[0:1, number(t):number(t) + 1]
            return tile_expert[0:1, bass.ds(number(t), 1)]

        def ones_wide():
            return ones[:, 0:1].broadcast_to([P, WIDE])

        block = ctx.enter_context(nc.Block())

        def pipeline(eng, step):
            for i in range(2):
                a = Seq(0, i)
                step(a, before(a, 1) if i > 0 else None, None, before(a, -1))
            with eng.Fori(1, NSEQ // 2 - 1) as half:
                for par in range(2):
                    a = Seq(half, par)
                    step(a, before(a, 1), before(a, 2), before(a, -1))
            for i in range(NSEQ - 2, NSEQ + 2):
                a = Seq(i // 2, i % 2)
                step(a if i < NSEQ else None, before(a, 1) if i <= NSEQ else None, before(a, 2),
                     before(a, -1) if i + 1 < NSEQ else None)

        @block.sync
        def _(sp):
            sp.dma_start(tiles(x_sb[0]), x_t[0]).then_inc(s_x[0], 16)
            sp.dma_start(wk_sb.rearrange("p (c n) -> p c n", c=DC), wk.rearrange("(c p) n -> p c n", p=P)).then_inc(s_wqk, 16)
            sp.dma_start(wq_sb.rearrange("p (c n) -> p c n", c=DC), wq.rearrange("(c p) n -> p c n", p=P)).then_inc(s_wqk, 16)
            sp.dma_start(tiles(x_sb[1]), x_t[1]).then_inc(s_x[1], 16)

            def step(a, b, c, nxt):
                if nxt is not None and b is not None:
                    need_apart(sp, s_xn, TJ, b, TJ)
                    sp.dma_start(tiles(x_sb[nxt.par]), seq_rows(x_t, nxt)).then_inc(s_x[nxt.par], 16)
                if b is not None:
                    need_apart(sp, s_x1, 2, b, 0)
                    sp.dma_start(tiles(x_res), seq_rows(x_t, b)).then_inc(s_xres, 16)
                if c is not None:
                    need_apart(sp, s_zn, TJ, c, TJ)
                    need_apart(sp, s_base, 1, c, 1)
                    need_apart(sp, s_alpha, 1, c, 1)
                    sp.dma_start(seq_rows(rows_t, c), tiles(row_sb, RW)).then_inc(s_row_out, 16)

                if a is None and b is not None:
                    need(sp, s_o, 2, b, 2)
                    need(sp, s_og, 2, b, 2)
                    for e in range(E):
                        w = slice(e * FC * D, (e + 1) * FC * D)
                        sp.dma_start(w2_sb[:, w], w2_t[:, w]).then_inc(s_w2, 16)
                    sp.dma_start(b1_sb, b1.rearrange("e f -> (e f)").partition_broadcast(P)).then_inc(s_b1, 16)

            pipeline(sp, step)
            need(sp, s_y, 2, Seq(NSEQ // 2 - 1, 1), 2)
            sp.wait_ge(s_row_out, 16 * NSEQ)
            sp.wait_ge(s_idx, 3)
            sp.dma_start(b2_sb, b2.rearrange("e f -> (e f)").partition_broadcast(P)).then_inc(s_b2, 16)

        @block.gpsimd
        def _(pool):
            made = 0

            def own(ins):
                nonlocal made
                made += 1
                ins.then_inc(s_setup, 1)
                pool.wait_ge(s_setup, made)

            own(pool.memset(ident[:, :], 0.0))
            own(pool.affine_select(out=ident[:, :], in_=ident[:, :], compare_op=ALU.not_equal, fill=1.0, base=0,
                                   pattern=[[-1, P]], channel_multiplier=1))
            pool.memset(minus_half[:, :], -0.5)
            own(pool.memset(ones[:, :], 1.0))
            pool.iota(iota_e[:, :], pattern=[[1, E]], base=0, channel_multiplier=0, allow_small_or_imprecise_dtypes=True)
            pool.iota(iota_t[:, :], pattern=[[1, TS]], base=0, channel_multiplier=0, allow_small_or_imprecise_dtypes=True)
            pool.iota(iota_r[:, :], pattern=[[1, P]], base=0, channel_multiplier=0, allow_small_or_imprecise_dtypes=True)
            own(pool.iota(iota_p[:, :], pattern=[[0, 1]], base=0, channel_multiplier=1, allow_small_or_imprecise_dtypes=True))
            own(pool.affine_select(out=below[:, :], in_=ones[:, :], compare_op=ALU.is_gt, fill=0.0, base=0,
                                   pattern=[[1, P]], channel_multiplier=-1))
            pool.sem_inc(s_const, 1)
            for l in range(LEVELS):
                h = 2 ** l
                own(pool.memset(mask_f, 1.0))
                view = mask_f.rearrange("p (c n h) -> p c n h", c=NCH, h=h)
                own(pool.affine_select(out=view, in_=view, compare_op=ALU.is_ge, fill=0.0, base=0,
                                       pattern=[[0, NCH], [-2 * h, HALF // h], [0, h]], channel_multiplier=1))
                own(pool.affine_select(out=view, in_=view, compare_op=ALU.is_ge, fill=0.0, base=h - 1,
                                       pattern=[[0, NCH], [2 * h, HALF // h], [0, h]], channel_multiplier=-1))
                own(pool.tensor_copy(masks[:, l * NCH * HALF:(l + 1) * NCH * HALF], mask_f))
            pool.sem_inc(s_const, 1)

            def norm(n, s):
                need_apart(pool, s_mom[n], TJ, s, TJ)
                pool.tensor_scalar(var_eps[n][:, :], mom[n][:, :, 1], EPS, None, ALU.add).then_inc(s_ve[n], 1)
                need(pool, s_ve[n], 1, s, 1)
                pool.tensor_tensor(rstd[n][:, :], var_eps[n][:, :], minus_half[:, :], ALU.pow).then_inc(s_rstd[n], 1)

            def step(a, b, c, nxt):
                if a is not None:
                    dec = decay[a.par]
                    need(pool, s_f0, 1, a, 1)
                    need(pool, s_state, 5, before(a, 2), 5)
                    for l in range(1, LEVELS + 1):
                        if l > 1:
                            need(pool, s_tree, LEVELS, a, l - 1)
                        two = tree(dec, l - 1).rearrange("p (n two) -> p n two", two=2)
                        pool.tensor_tensor(tree(dec, l), two[:, :, 0], two[:, :, 1], ALU.mult).then_inc(s_tree, 1)
                if c is not None:
                    need(pool, s_xn2, TJ, c, 0)
                    norm("u", c)
                if a is not None:
                    need(pool, s_q, H, a, H)
                    need(pool, s_k, H, a, H)
                    need(pool, s_dz, 1, a, 0)
                    pool.tensor_tensor(qk, q_raw, k_dec[a.par], ALU.mult).then_inc(s_qk, 1)
                    need(pool, s_o, 2, before(a, 2), 2)
                    pool.tensor_tensor(q_dec[a.par], q_raw, tree(dec, 0), ALU.mult).then_inc(s_q0, 1)
                if c is not None:
                    need(pool, s_xn2, TJ, c, TJ)
                    need(pool, s_row_out, 16, c, 0)
                    pool.tensor_tensor(tiles(row_sb, RW)[:, :, D:2 * D], tiles(x1), tiles(xn2), ALU.add).then_inc(s_base, 1)
                    need(pool, s_zn, TJ, c, 0)
                    norm("z", c)
                if nxt is not None:
                    norm("x", nxt)
                if a is not None:
                    need(pool, s_diag, 1, a, 1)
                    need(pool, s_o, 2, before(a, 2), 2)
                    pool.tensor_tensor(attn_t[a.par].rearrange("p (n t) -> p n t", t=P),
                                       ident[:, :].unsqueeze(1).broadcast_to([P, NCH, P]),
                                       diag[:, :].unsqueeze(2).broadcast_to([P, NCH, P]), ALU.mult).then_inc(s_at0, 1)
                if b is not None:
                    norm("o", b)

            norm("x", Seq(0, 0))
            pipeline(pool, step)

            pool.wait_ge(s_row_out, 16 * NSEQ)
            pool.wait_ge(s_idx, 3)

            def gather(t, p):
                need(pool, s_yo, 1, before(t, 2), 1)
                pool.tensor_copy(take_now[:, p:p + 1], column(take_idx, t)).then_inc(s_take, 1)
                need_apart(pool, s_take, 1, t, 1)
                pool.indirect_dma_start(out=gathered[p], out_offset=None, in_=rows,
                                        in_offset=bass.IndirectOffsetOnAxis(ap=take_now[:, p:p + 1], axis=0)).then_inc(s_rows[p], 16)

            def scatter(t, p):
                if not isinstance(t.half, int):
                    pool.wait_ge(s_out[p], t.half * 16)
                elif t.half > 0:
                    pool.wait_ge(s_out[p], 16 * t.half)
                pool.tensor_copy(put_now[:, p:p + 1], column(put_idx, t)).then_inc(s_put, 1)
                need(pool, s_put, 1, t, 1)
                need_apart(pool, s_yo, 1, t, 1)
                pool.indirect_dma_start(out=out, out_offset=bass.IndirectOffsetOnAxis(ap=put_now[:, p:p + 1], axis=0),
                                        in_=y_out[p], in_offset=None, bounds_check=N - 1, oob_is_err=False).then_inc(s_out[p], 16)

            gather(Seq(0, 0), 0)
            gather(Seq(0, 1), 1)
            with pool.Fori(0, (TILES - 3) // 2) as half:
                for p in range(2):
                    t = Seq(half, p)
                    scatter(t, p)
                    gather(before(t, -2), p)
            for i in range(TILES - 3, TILES):
                t = Seq(i // 2, i % 2)
                scatter(t, t.par)
                if i + 2 < TILES:
                    gather(before(t, -2), t.par)
            for p in range(2):
                pool.wait_ge(s_out[p], 16 * ((TILES + 1 - p) // 2))

        @block.scalar
        def _(act):
            act.dma_start(wg1_sb.rearrange("p (c n) -> p c n", c=DC), wg1.rearrange("(c p) n -> p c n", p=P)).then_inc(s_wvg, 16)
            act.dma_start(wv_sb.rearrange("p (c n) -> p c n", c=DC), wv.rearrange("(c p) n -> p c n", p=P)).then_inc(s_wvg, 16)
            act.dma_start(wg2_sb, wg2).then_inc(s_wvg, 16)
            act.dma_start(wo_sb.rearrange("p (c n) -> p c n", c=DC), wo.rearrange("(c p) n -> p c n", p=P)).then_inc(s_wo_in, 16)
            act.dma_start(norm_col[:, :], norm_w).then_inc(s_wo_in, 16)
            act.dma_start(cent_sb[:, :], centroids_t).then_inc(s_small, 16)
            act.dma_start(g_col[:, :], ln_g).then_inc(s_small, 16)
            act.dma_start(b_col[:, :], ln_b).then_inc(s_small, 16)
            for e in range(E):
                act.dma_start(w1_sb[:, e * DC * F:(e + 1) * DC * F], w1_t[:, e * DC * F:(e + 1) * DC * F]).then_inc(s_w1, 16)

            def copy(dst, src):
                return act.activation(dst, src, ACT.Copy)

            def step(a, b, c, nxt):
                if a is not None:
                    for i in range(DC):
                        need(act, s_tp, DC, a, i + 1)
                        if i == 0:
                            need(act, s_gz, 2, a, 0)
                        copy(xn_t[:, i * T:(i + 1) * T], bank_a[i][:, :]).then_inc(s_xnt, 1)
                    for h in range(H):
                        need(act, s_kz, H, a, h + 1)
                        if h == 0:
                            need(act, s_k7, 1, before(a, 2), 1)
                        act.activation(k_dec[a.par][:, h * T:(h + 1) * T], bank_a[h][:, :], ACT.Sigmoid).then_inc(s_k, 1)
                if c is not None:
                    for i in range(DC):
                        need(act, s_ot, DC, c, i + 1)
                        if i == 0:
                            need(act, s_y, 2, c, 0)
                        copy(o_t[:, i * T:(i + 1) * T], bank_c[i][:, :]).then_inc(s_ont, 1)
                if a is not None:
                    for h in range(H):
                        need(act, s_qz, H, a, h + 1)
                        if h == 0:
                            need(act, s_qk, 1, a, 0)
                            need(act, s_q0, 1, a, 0)
                        act.activation(q_raw[:, h * T:(h + 1) * T], bank_a[h][:, :], ACT.Sigmoid).then_inc(s_qs, 1)
                if c is not None:
                    need(act, s_shift["u"], 1, c, 1)
                    need(act, s_base, 1, c, 0)
                    need(act, s_stat["z"], TJ, c, 0)
                    need(act, s_t2, DC, c, 0)
                    for j in range(TJ):
                        act.activation(tiles(xn2)[:, j], tiles(x1)[:, j], ACT.Identity, bias=shift["u"][:, j:j + 1],
                                       scale=rstd["u"][:, j:j + 1]).then_inc(s_xn2, 1)
                if b is not None:
                    need(act, s_k7, 1, b, 1)
                    need(act, s_kv, 2, b, 0)
                    copy(k_tok[:, 0:512], bank_b[0][:, :]).then_inc(s_kt, 1)
                    copy(k_tok[:, 512:768], bank_b[1][:, 0:256]).then_inc(s_kt, 1)
                if a is not None:
                    need(act, s_g1z, 1, a, 1)
                    copy(g1_t, bank_a[0][:, :]).then_inc(s_g1, 1)
                if c is not None:
                    need(act, s_affz, 1, c, 0)
                    for i in range(DC):
                        need(act, s_t2, DC, c, i + 1)
                        copy(xn2_t[:, i * T:(i + 1) * T], bank_c[i][:, :]).then_inc(s_xn2t, 1)
                if a is not None:
                    need(act, s_o, 2, before(a, 2), 2)
                    for i in range(2):
                        need(act, s_vz, 2, a, i + 1)
                        copy(v_sb[a.par][:, i * 512:(i + 1) * 512], bank_a[1 - i][:, :]).then_inc(s_v, 1)
                    need(act, s_og, 2, before(a, 2), 2)
                    for i in range(2):
                        need(act, s_gz, 2, a, i + 1)
                        act.activation(gate[a.par][:, i * 512:(i + 1) * 512], bank_a[1 - i][:, :], ACT.Sigmoid).then_inc(s_gate, 1)
                    need(act, s_dz, 1, a, 1)
                    need(act, s_at0, 1, a, 0)
                    copy(diag[:, :], bank_a[1][:, 0:NCH]).then_inc(s_diag, 1)
                if c is not None:
                    need(act, s_affz, 1, c, 1)
                    need(act, s_best, 1, c, 1)
                    copy(aff_of(c), bank_c[0][:, 0:TJ * E]).then_inc(s_aff, 1)
                    need(act, s_row_out, 16, c, 0)
                    act.activation(tiles(row_sb, RW)[:, :, 2 * D], aff_best[:, :], ACT.Sigmoid).then_inc(s_alpha, 1)
                    need(act, s_shift["z"], 1, c, 1)
                    for j in range(TJ):
                        act.activation(tiles(row_sb, RW)[:, j, 0:D], tiles(xn2)[:, j], ACT.Identity, bias=shift["z"][:, j:j + 1],
                                       scale=rstd["z"][:, j:j + 1]).then_inc(s_zn, 1)

            pipeline(act, step)

            act.wait_ge(s_small, 48)
            act.wait_ge(s_idx, 3)

            def tile(t, p):
                if t is not None:
                    e = act.value_load(expert_of(t), min_val=0, max_val=E - 1)
                    need(act, s_zt, 1, t, 1)
                    need(act, s_h, 2, before(t, 2), 2)
                    for i in range(DC):
                        act.activation(xl_t[p][:, i * P:(i + 1) * P], bank_b[0][:, i * P:(i + 1) * P], ACT.Identity,
                                       bias=b_col[:, bass.ds(e * DC + i, 1)], scale=g_col[:, bass.ds(e * DC + i, 1)]).then_inc(s_xl, 1)

            def relu(t):
                need(act, s_ye, 1, t, 0)
                for i in range(2):
                    need(act, s_ht, 2, t, i + 1)
                    act.activation(h_t[:, i * 512:(i + 1) * 512], bank_l[i][:, :], ACT.Relu).then_inc(s_hr, 1)

            tile(Seq(0, 0), 0)
            with act.Fori(0, (TILES - 1) // 2) as half:
                for p in range(2):
                    t = Seq(half, p)
                    tile(before(t, -1), 1 - p)
                    relu(t)
            relu(Seq((TILES - 1) // 2, 0))

        @block.tensor
        def _(pe):
            def level(b, l):
                kb, qb = k_dec[b.par], q_dec[b.par]
                if l == 0:
                    need(pe, s_q0, 1, b, 1)
                    need(pe, s_k, H, b, H)
                else:
                    need(pe, s_up, 2 * LEVELS, b, 2 * l)
                need(pe, s_pick, LEVELS, b, max(l - 1, 0))
                for n in range(NCH):
                    m = pe.matmul(packed(bank_l[l % 2][:, n * HALF:(n + 1) * HALF], l), kb[:, n * P:(n + 1) * P],
                                  halves(qb[:, n * P:(n + 1) * P], l)[:, :, 1, :], start=True, stop=True)
                m.then_inc(s_lev, 1)

            def transposes(a):
                need(pe, s_xn, TJ, a, TJ)
                for i in range(DC):
                    need(pe, s_gate if i == 0 else s_diag, 2 if i == 0 else 1, a, 0)
                    for j in range(TJ):
                        m = pe.transpose(bank_a[i][:, j * P:(j + 1) * P], tiles(xn)[:, j, i * P:(i + 1) * P], ident[:, :])
                    m.then_inc(s_tp, 1)

            def channels(a, w, h, bank, done):
                for i in range(DC):
                    m = pe.matmul(bank[:, :], w[:, i * D + h * P:i * D + (h + 1) * P], xn_t[:, i * T:(i + 1) * T],
                                  start=(i == 0), stop=(i == DC - 1))
                m.then_inc(done, 1)

            def k_proj(a, h):
                need(pe, s_xnt, DC, a, DC)
                channels(a, wk_sb, h, bank_a[h], s_kz)

            def q_proj(a, h):
                need(pe, s_k, H, a, h + 1)
                channels(a, wq_sb, h, bank_a[h], s_qz)

            def g1_proj(a):
                need(pe, s_q, H, a, 1)
                need(pe, s_gz, 2, a, 0)
                for i in range(DC):
                    m = pe.matmul(bank_a[0][:, :], wg1_sb[:, i * G1:(i + 1) * G1], xn_t[:, i * T:(i + 1) * T],
                                  start=(i == 0), stop=(i == DC - 1))
                m.then_inc(s_g1z, 1)

            def v_proj(a, half):
                if half == 0:
                    need(pe, s_q, H, a, 2)
                else:
                    need(pe, s_g1, 1, a, 1)
                for j in range(2):
                    for i in range(DC):
                        t0 = i * T + (2 * half + j) * P
                        m = pe.matmul(bank_a[1 - half][:, j * D:(j + 1) * D], xn_t[:, t0:t0 + P], wv_sb[:, i * D:(i + 1) * D],
                                      start=(i == 0), stop=(i == DC - 1))
                m.then_inc(s_vz, 1)

            def gate_proj(a, half):
                need(pe, s_g1, 1, a, 1)
                need(pe, s_v, 2, a, half + 1)
                for j in range(2):
                    t0 = (2 * half + j) * P
                    m = pe.matmul(bank_a[1 - half][:, j * D:(j + 1) * D], g1_t[:, t0:t0 + P], wg2_sb[:, :], start=True, stop=True)
                m.then_inc(s_gz, 1)

            def diagonal(a):
                need(pe, s_qk, 1, a, 1)
                need(pe, s_gate, 2, a, 1)
                for n in range(NCH):
                    m = pe.matmul(bank_a[1][:, n:n + 1], qk[:, n * P:(n + 1) * P], ones[:, 0:1], start=True, stop=True)
                m.then_inc(s_dz, 1)

            def k_transposes(b):
                need(pe, s_up, 2 * LEVELS, b, 2 * LEVELS)
                need(pe, s_og, 2, b, 0)
                for c in range(TJ - 1):
                    for h in range(H):
                        n = c * H + h
                        m = pe.transpose(bank_b[n // 4][:, n % 4 * P:(n % 4 + 1) * P],
                                         k_dec[b.par][:, h * T + c * P:h * T + (c + 1) * P], ident[:, :])
                m.then_inc(s_k7, 1)

            def key_values(b):
                need(pe, s_v, 2, b, 2)
                for c in range(TJ - 1):
                    for h in range(H):
                        n = c * H + h
                        if n % 4 == 0:
                            need(pe, s_kt, 2, b, n // 4 + 1)
                        if n == 4:
                            m.then_inc(s_kv, 1)
                        m = pe.matmul(bank_b[n // 4][:, n % 4 * P:(n % 4 + 1) * P], k_tok[:, n * P:(n + 1) * P],
                                      v_sb[b.par][:, n * P:(n + 1) * P], start=True, stop=True)
                m.then_inc(s_kv, 1)

            def outputs(b):
                need(pe, s_pick, LEVELS, b, LEVELS)
                need(pe, s_state, 5, b, 5)
                for c in range(TJ):
                    for h in range(H):
                        dst = bank_b[c // 2][:, c % 2 * D + h * P:c % 2 * D + (h + 1) * P]
                        t0 = h * T + c * P
                        if c > 0:
                            n = (c - 1) * H + h
                            pe.matmul(dst, q_dec[b.par][:, t0:t0 + P], state[:, n * P:(n + 1) * P], start=True, stop=False)
                        m = pe.matmul(dst, attn_t[b.par][:, t0:t0 + P], v_sb[b.par][:, c * D + h * P:c * D + (h + 1) * P],
                                      start=(c == 0), stop=True)
                    if c % 2:
                        m.then_inc(s_o, 1)

            def o_transposes(c):
                need(pe, s_on, TJ, c, TJ)
                for i in range(DC):
                    if i == 0:
                        need(pe, s_aff, 1, c, 0)
                        need(pe, s_best, 1, c, 0)
                    else:
                        need(pe, s_xn2t, DC, c, 0)
                    for j in range(TJ):
                        m = pe.transpose(bank_c[i][:, j * P:(j + 1) * P], tiles(o_sb)[:, j, i * P:(i + 1) * P], ident[:, :])
                    m.then_inc(s_ot, 1)

            def out_proj(c, half):
                need(pe, s_ont, DC, c, DC)
                for j in range(2):
                    for i in range(DC):
                        t0 = i * T + (2 * half + j) * P
                        m = pe.matmul(bank_c[half][:, j * D:(j + 1) * D], o_t[:, t0:t0 + P], wo_sb[:, i * D:(i + 1) * D],
                                      start=(i == 0), stop=(i == DC - 1))
                m.then_inc(s_y, 1)

            def xn2_transposes(c):
                need(pe, s_xn2, TJ, c, TJ)
                need(pe, s_x1, 2, c, 2)
                for i in range(DC):
                    for j in range(TJ):
                        m = pe.transpose(bank_c[i][:, j * P:(j + 1) * P], tiles(xn2)[:, j, i * P:(i + 1) * P], ident[:, :])
                    m.then_inc(s_t2, 1)

            def affinities(c):
                need(pe, s_xn2t, DC, c, DC)
                for j in range(TJ):
                    for i in range(DC):
                        m = pe.matmul(bank_c[0][:, j * E:(j + 1) * E], xn2_t[:, i * T + j * P:i * T + (j + 1) * P],
                                      cent_sb[:, i * E:(i + 1) * E], start=(i == 0), stop=(i == DC - 1))
                m.then_inc(s_affz, 1)

            def step(a, b, c, nxt):
                if b is not None:
                    level(b, 0)
                if a is not None:
                    transposes(a)
                if b is not None:
                    level(b, 1)
                if a is not None:
                    k_proj(a, 0)
                if b is not None:
                    level(b, 2)
                if a is not None:
                    k_proj(a, 1)
                if c is not None:
                    o_transposes(c)
                if b is not None:
                    level(b, 3)
                if c is not None:
                    out_proj(c, 0)
                if b is not None:
                    level(b, 4)
                if c is not None:
                    out_proj(c, 1)
                if b is not None:
                    level(b, 5)
                if a is not None:
                    q_proj(a, 0)
                if b is not None:
                    level(b, 6)
                if a is not None:
                    q_proj(a, 1)
                if b is not None:
                    k_transposes(b)
                if a is not None:
                    g1_proj(a)
                if c is not None:
                    xn2_transposes(c)
                if b is not None:
                    key_values(b)
                if a is not None:
                    v_proj(a, 0)
                    v_proj(a, 1)
                    gate_proj(a, 0)
                    gate_proj(a, 1)
                if c is not None:
                    affinities(c)
                if a is not None:
                    diagonal(a)
                if b is not None:
                    outputs(b)

            pe.wait_ge(s_const, 1)
            pe.wait_ge(s_wqk, 32)
            pe.wait_ge(s_wvg, 48)
            pe.wait_ge(s_wo, DC)
            pe.wait_ge(s_small, 48)
            pipeline(pe, step)

            pe.wait_ge(s_r, 5)
            pe.matmul(bank_a[0][:, 0:WIDE], below[:, :], onehot, start=True, stop=True)
            pe.matmul(bank_a[1][:, 0:WIDE], ones[:, :], onehot, start=True, stop=True).then_inc(s_rank, 1)
            for g in range(4):
                pe.wait_ge(s_hot, g + 4)
                for t in range(g * NT // 4, (g + 1) * NT // 4):
                    m = pe.matmul(bank_b[1][:, 0:3 * TS], lo_hot[:, t * P:(t + 1) * P], hi_hot[:, t * 3 * TS:(t + 1) * 3 * TS],
                                  start=(t == 0), stop=(t == NT - 1))
            m.then_inc(s_inv, 1)

            def z_transposes(t, p):
                pe.wait_ge(s_rows[p], t.half * 16 + 16)
                need(pe, s_xl, DC, t, 0)
                for i in range(DC):
                    m = pe.transpose(bank_b[0][:, i * P:(i + 1) * P], gathered[p][:, i * P:(i + 1) * P], ident[:, :])
                m.then_inc(s_zt, 1)

            def up(t, p, e):
                need(pe, s_xl, DC, t, DC)
                for n in range(2):
                    need(pe, s_hb, 2, t, 0)
                    for i in range(DC):
                        m = pe.matmul(bank_a[n][:, :], xl_t[p][:, i * P:(i + 1) * P],
                                      w1_sb[:, bass.ds(e * (DC * F) + (i * F + n * 512), 512)], start=(i == 0), stop=(i == DC - 1))
                    m.then_inc(s_h, 1)

            def h_transposes(t):
                for n in range(2):
                    need(pe, s_hb, 2, t, n + 1)
                    need(pe, s_hr, 2, t, 0)
                    for j in range(4):
                        k = 4 * n + j
                        m = pe.transpose(bank_l[n][:, j * P:(j + 1) * P], h_sb[:, k * P:(k + 1) * P], ident[:, :])
                    m.then_inc(s_ht, 1)

            def down(t, p, e):
                need(pe, s_yb, 1, before(t, 2), 1)
                for k in range(FC):
                    if k % 4 == 0:
                        need(pe, s_hr, 2, t, k // 4 + 1)
                    m = pe.matmul(bank_c[p][:, 0:D], h_t[:, k * P:(k + 1) * P],
                                  w2_sb[:, bass.ds(e * (FC * D) + k * D, D)], start=(k == 0), stop=(k == FC - 1))
                m.then_inc(s_ye, 1)

            pe.wait_ge(s_idx, 3)
            pe.wait_ge(s_w1, 16 * E)

            def expert(t):
                return pe.value_load(expert_of(t), min_val=0, max_val=E - 1)

            first_t = Seq(0, 0)
            z_transposes(first_t, 0)
            up(first_t, 0, expert(first_t))
            z_transposes(Seq(0, 1), 1)
            pe.wait_ge(s_w2, 16 * E)

            def turn(t):
                h_transposes(t)
                if not (isinstance(t.half, int) and number(t) + 1 >= TILES):
                    up(before(t, -1), 1 - t.par, expert(before(t, -1)))
                down(t, t.par, expert(t))
                if not (isinstance(t.half, int) and number(t) + 2 >= TILES):
                    z_transposes(before(t, -2), t.par)

            for p in range(2):
                turn(Seq(0, p))
            with pe.Fori(1, (TILES - 3) // 2) as half:
                for p in range(2):
                    turn(Seq(half, p))
            for i in range(TILES - 3, TILES):
                turn(Seq(i // 2, i % 2))

        @block.vector
        def _(dve):
            def stats(n, src, s):
                for j in range(TJ):
                    dve.bn_stats(stat[n][:, j, :], tiles(src)[:, j]).then_inc(s_stat[n], 1)
                for j in range(TJ):
                    need_apart(dve, s_stat[n], TJ, s, j + 1)
                    dve.bn_aggr(mom[n][:, j, :], stat[n][:, j, :]).then_inc(s_mom[n], 1)

            def apply_norm(n, src, dst, s, done):
                need(dve, s_rstd[n], 1, s, 1)
                for j in range(TJ):
                    dve.tensor_scalar(tiles(dst)[:, j], tiles(src)[:, j], mom[n][:, j, 0:1], rstd[n][:, j:j + 1],
                                      ALU.subtract, ALU.mult).then_inc(done, 1)

            def shifts(n, s):
                need(dve, s_rstd[n], 1, s, 1)
                dve.scalar_tensor_tensor(out=shift[n][:, :], in0=mom[n][:, :, 0], scalar=-1.0, in1=rstd[n][:, :],
                                         op0=ALU.mult, op1=ALU.mult).then_inc(s_shift[n], 1)

            def x_stats(a):
                dve.wait_ge(s_x[a.par], a.half * 16 + 16)
                stats("x", x_sb[a.par], a)

            def x_norm(a):
                need(dve, s_tp, DC, a, 0)
                apply_norm("x", x_sb[a.par], xn, a, s_xn)

            def update(b, l):
                kb, qb, dec = halves(k_dec[b.par], l), halves(q_dec[b.par], l), decay[b.par]
                need(dve, s_lev, LEVELS, b, l + 1)
                if l > 0:
                    need(dve, s_tree, LEVELS, b, l)
                    need(dve, s_up, 2 * LEVELS, b, 2 * l)
                dve.tensor_tensor(kb[:, :, 0, :], kb[:, :, 0, :], factor(dec, l, 1), ALU.mult).then_inc(s_up, 1)
                dve.tensor_tensor(qb[:, :, 1, :], qb[:, :, 1, :], factor(dec, l, 0), ALU.mult).then_inc(s_up, 1)

            def pick(b, l):
                if l == 0:
                    need_apart(dve, s_at0, 1, b, 1)
                else:
                    need_apart(dve, s_pick, LEVELS, b, l)
                m0 = l * NCH * HALF
                dve.copy_predicated(halves(attn_t[b.par], l)[:, :, 1, :], packed(masks[:, m0:m0 + NCH * HALF], l),
                                    packed(bank_l[l % 2][:, :], l)).then_inc(s_pick, 1)

            def decays(a):
                need(dve, s_k, H, a, H)
                need(dve, s_up, 2 * LEVELS, before(a, 2), 2 * LEVELS)
                f0 = tree(decay[a.par], 0)
                dve.tensor_scalar(f0, k_dec[a.par], -1.0, 1.0, ALU.mult, ALU.add).then_inc(s_f, 1)
                need(dve, s_f, 1, a, 1)
                dve.scalar_tensor_tensor(out=f0, in0=f0, scalar=0.5, in1=f0, op0=ALU.is_equal,
                                         op1=ALU.subtract).then_inc(s_f0, 1)

            def q_mult(a, h):
                need(dve, s_qs, H, a, h + 1)
                dve.tensor_tensor(q_raw[:, h * T:(h + 1) * T], bank_a[h][:, :], q_raw[:, h * T:(h + 1) * T],
                                  ALU.mult).then_inc(s_q, 1)

            def residual(c, half):
                need(dve, s_y, 2, c, half + 1)
                if half == 0:
                    need(dve, s_xres, 16, c, 16)
                    need(dve, s_base, 1, c, 0)
                w = slice(half * 512, half * 512 + 512)
                dve.tensor_tensor(x1[:, w], bank_c[half][:, :], x_res[:, w], ALU.add).then_inc(s_x1, 1)

            def states(b):
                need(dve, s_kv, 2, b, 1)
                f7 = tree(decay[b.par], LEVELS)
                dve.tensor_copy(state[:, 0:D], bank_b[0][:, 0:D]).then_inc(s_state, 1)
                for c in range(1, TJ - 1):
                    for h in range(H):
                        n = c * H + h
                        if h == 0:
                            need(dve, s_state, 5, b, 2 * c - 1)
                        if n == 4:
                            need(dve, s_kv, 2, b, 2)
                        dve.scalar_tensor_tensor(out=state[:, n * P:(n + 1) * P], in0=state[:, (n - H) * P:(n - H + 1) * P],
                                                 scalar=f7[:, h * TJ + c:h * TJ + c + 1],
                                                 in1=bank_b[n // 4][:, n % 4 * P:(n % 4 + 1) * P],
                                                 op0=ALU.mult, op1=ALU.add).then_inc(s_state, 1)

            def gating(b):
                need(dve, s_gate, 2, b, 2)
                need(dve, s_ot, DC, b, 0)
                for i in range(2):
                    need(dve, s_o, 2, b, i + 1)
                    w = slice(i * 512, i * 512 + 512)
                    dve.scalar_tensor_tensor(out=o_sb[:, w], in0=bank_b[i][:, :], scalar=QSCALE, in1=gate[b.par][:, w],
                                             op0=ALU.mult, op1=ALU.mult).then_inc(s_og, 1)

            def step(a, b, c, nxt):
                if b is not None:
                    update(b, 0)
                    pick(b, 0)
                    update(b, 1)
                    pick(b, 1)
                    update(b, 2)
                    pick(b, 2)
                if a is not None:
                    decays(a)
                if b is not None:
                    update(b, 3)
                    pick(b, 3)
                if c is not None:
                    residual(c, 0)
                if b is not None:
                    update(b, 4)
                    pick(b, 4)
                if c is not None:
                    residual(c, 1)
                    need(dve, s_x1, 2, c, 2)
                    stats("u", x1, c)
                if b is not None:
                    update(b, 5)
                    pick(b, 5)
                if a is not None:
                    q_mult(a, 0)
                if c is not None:
                    shifts("u", c)
                if b is not None:
                    update(b, 6)
                    pick(b, 6)
                if a is not None:
                    q_mult(a, 1)
                if c is not None:
                    need(dve, s_xn2, TJ, c, TJ)
                    stats("z", xn2, c)
                if nxt is not None:
                    x_stats(nxt)
                if b is not None:
                    states(b)
                if nxt is not None:
                    x_norm(nxt)
                if c is not None:
                    need(dve, s_zn, TJ, c, 0)
                    shifts("z", c)
                    need(dve, s_affz, 1, c, 1)
                    need(dve, s_alpha, 1, c, 0)
                    dve.tensor_reduce(aff_best[:, :], bank_c[0][:, 0:TJ * E].rearrange("p (j e) -> p j e", e=E), AX_X,
                                      ALU.max).then_inc(s_best, 1)
                if b is not None:
                    gating(b)
                    need(dve, s_og, 2, b, 2)
                    stats("o", o_sb, b)
                    apply_norm("o", o_sb, o_sb, b, s_on)

            dve.wait_ge(s_wo_in, 32)
            for i in range(DC):
                dve.tensor_scalar(wo_sb[:, i * D:(i + 1) * D], wo_sb[:, i * D:(i + 1) * D], norm_col[:, i:i + 1], None,
                                  ALU.mult).then_inc(s_wo, 1)
            x_stats(Seq(0, 0))
            x_norm(Seq(0, 0))
            dve.wait_ge(s_const, 2)
            pipeline(dve, step)

            done = 0

            def own(ins):
                nonlocal done
                done += 1
                ins.then_inc(s_r, 1)
                dve.wait_ge(s_r, done)

            def te(ap):
                return ap.rearrange("p (t e) -> p t e", e=E)

            def over_t(ap):
                return ap.unsqueeze(1).broadcast_to([P, NT, E])

            def over_e(ap):
                return ap.unsqueeze(2).broadcast_to([P, NT, E])

            dve.wait_ge(s_aff, NSEQ)
            dve.wait_ge(s_row_out, 16 * NSEQ)
            own(dve.tensor_reduce(aff_max, te(aff[:, :]), AX_X, ALU.max))
            own(dve.tensor_tensor(te(is_max), te(aff[:, :]), over_e(aff_max), ALU.is_equal))
            own(dve.scalar_tensor_tensor(out=te(is_max), in0=te(is_max), scalar=-float(E), in1=over_t(iota_e[:, :]),
                                         op0=ALU.mult, op1=ALU.add))
            own(dve.tensor_reduce(first, te(is_max), AX_X, ALU.min))
            own(dve.scalar_tensor_tensor(out=te(onehot), in0=over_t(iota_e[:, :]), scalar=-float(E), in1=over_e(first),
                                         op0=ALU.add, op1=ALU.is_equal))
            dve.wait_ge(s_rank, 1)
            own(dve.tensor_copy(count_e.rearrange("p (e t) -> p t e", e=E), te(bank_a[1][:, 0:WIDE])))
            own(dve.tensor_tensor_scan(out=cum_e, data0=ones_wide(), data1=count_e, initial=0.0, op0=ALU.mult, op1=ALU.add))
            upto = small[:, 0:E]
            n_e = small[:, E:2 * E]
            prior = small[:, 2 * E:3 * E]
            n_up = small[:, 3 * E:4 * E]
            nt_e = small[:, 4 * E:5 * E]
            t_upto = small[:, 5 * E:6 * E]
            off = small[:, 6 * E:7 * E]
            own(dve.tensor_copy(upto, cum_e.rearrange("p (e t) -> p e t", e=E)[:, :, NT - 1]))
            own(dve.tensor_reduce(n_e, count_e.rearrange("p (e t) -> p e t", e=E), AX_X, ALU.add))
            own(dve.tensor_tensor(prior, upto, n_e, ALU.subtract))
            own(dve.tensor_scalar(n_up, n_e, float(P - 1), None, ALU.add))
            own(dve.tensor_copy(ntile_i[:, 0:E], n_up))
            own(dve.tensor_scalar(ntile_i[:, E:2 * E], ntile_i[:, 0:E], 7, None, ALU.arith_shift_right))
            own(dve.tensor_copy(nt_e, ntile_i[:, E:2 * E]))
            own(dve.tensor_tensor_scan(out=t_upto, data0=ones[:, 0:E], data1=nt_e, initial=0.0, op0=ALU.mult, op1=ALU.add))
            own(dve.tensor_tensor(off, t_upto, nt_e, ALU.subtract))
            own(dve.scalar_tensor_tensor(out=off, in0=off, scalar=float(P), in1=prior, op0=ALU.mult, op1=ALU.subtract))
            own(dve.tensor_tensor(cum_e, cum_e, count_e, ALU.subtract))
            own(dve.tensor_tensor(te(place), te(bank_a[0][:, 0:WIDE]), cum_e.rearrange("p (e t) -> p t e", e=E), ALU.add))
            own(dve.tensor_tensor(te(place), te(place), over_t(off), ALU.add))
            own(dve.tensor_tensor(place, place, onehot, ALU.mult))
            own(dve.tensor_reduce(slot, te(place), AX_X, ALU.add))
            own(dve.tensor_copy(slot_i, slot))
            own(dve.tensor_scalar(hi_i, slot_i, 7, None, ALU.arith_shift_right))
            own(dve.tensor_scalar(lo_i, slot_i, P - 1, None, ALU.bitwise_and))
            own(dve.tensor_copy(hi_f, hi_i))
            own(dve.tensor_copy(lo_f, lo_i))
            hot = hi_hot.rearrange("p (t k s) -> p t k s", k=3, s=TS)
            wide = [P, NT, TS]
            dve.tensor_tensor(hot[:, :, 0, :], iota_t[:, :].unsqueeze(1).broadcast_to(wide), hi_f.unsqueeze(2).broadcast_to(wide),
                              ALU.is_equal).then_inc(s_hot, 1)
            dve.wait_ge(s_hot, 1)
            dve.tensor_scalar(hot[:, :, 1, :], hot[:, :, 0, :], iota_p[:, 0:1], None, ALU.mult).then_inc(s_hot, 1)
            dve.tensor_tensor(hot[:, :, 2, :], hot[:, :, 0, :], iota_t[:, 0:NT].unsqueeze(2).broadcast_to(wide),
                              ALU.mult).then_inc(s_hot, 1)
            lo3 = lo_hot.rearrange("p (t r) -> p t r", r=P)
            for g in range(4):
                n = NT // 4
                dve.tensor_tensor(lo3[:, g * n:(g + 1) * n], iota_r[:, :].unsqueeze(1).broadcast_to([P, n, P]),
                                  lo_f[:, g * n:(g + 1) * n].unsqueeze(2).broadcast_to([P, n, P]), ALU.is_equal).then_inc(s_hot, 1)
            own(dve.tensor_tensor(ge_f[:, 0:TS * (E - 1)].rearrange("p (s e) -> p s e", e=E - 1),
                                  iota_t[:, :].unsqueeze(2).broadcast_to([P, TS, E - 1]),
                                  t_upto[:, 0:E - 1].unsqueeze(1).broadcast_to([P, TS, E - 1]), ALU.is_ge))
            own(dve.tensor_reduce(texp_f, ge_f[:, 0:TS * (E - 1)].rearrange("p (s e) -> p s e", e=E - 1), AX_X, ALU.add))
            dve.tensor_copy(tile_expert[:, :], texp_f).then_inc(s_idx, 1)
            dve.wait_ge(s_inv, 1)
            own(dve.tensor_copy(slot_f[:, 0:3 * TS], bank_b[1][:, 0:3 * TS]))
            own(dve.scalar_tensor_tensor(out=slot_f[:, 3 * TS:4 * TS], in0=slot_f[:, 2 * TS:3 * TS], scalar=float(P),
                                         in1=slot_f[:, TS:2 * TS], op0=ALU.mult, op1=ALU.add))
            own(dve.tensor_scalar(slot_f[:, 0:TS], slot_f[:, 0:TS], -float(SKIP), float(SKIP), ALU.mult, ALU.add))
            dve.tensor_copy(take_idx[:, :], slot_f[:, 3 * TS:4 * TS]).then_inc(s_idx, 1)
            dve.tensor_tensor(put_idx[:, :], slot_f[:, 0:TS], slot_f[:, 3 * TS:4 * TS], ALU.add).then_inc(s_idx, 1)

            dve.wait_ge(s_idx, 3)
            dve.wait_ge(s_b1, 16)
            dve.wait_ge(s_b2, 16)

            def bias_h(t, e):
                need(dve, s_ht, 2, t, 0)
                for n in range(2):
                    need(dve, s_h, 2, t, n + 1)
                    dve.tensor_tensor(h_sb[:, n * 512:(n + 1) * 512], bank_a[n][:, :],
                                      b1_sb[:, bass.ds(e * F + n * 512, 512)], ALU.add).then_inc(s_hb, 1)

            def finish(t, p, e):
                need(dve, s_ye, 1, t, 1)
                need(dve, s_yo, 1, t, 0)
                dve.tensor_tensor(y_sb, bank_c[p][:, 0:D], b2_sb[:, bass.ds(e * D, D)], ALU.add).then_inc(s_yb, 1)
                need(dve, s_yb, 1, t, 1)
                if not isinstance(t.half, int):
                    dve.wait_ge(s_out[p], t.half * 16)
                elif t.half > 0:
                    dve.wait_ge(s_out[p], 16 * t.half)
                dve.scalar_tensor_tensor(out=y_out[p], in0=y_sb, scalar=gathered[p][:, 2 * D:2 * D + 1],
                                         in1=gathered[p][:, D:2 * D], op0=ALU.mult, op1=ALU.add).then_inc(s_yo, 1)

            def expert(t):
                return dve.value_load(expert_of(t), min_val=0, max_val=E - 1)

            bias_h(Seq(0, 0), expert(Seq(0, 0)))
            with dve.Fori(0, (TILES - 1) // 2) as half:
                for p in range(2):
                    t = Seq(half, p)
                    bias_h(before(t, -1), expert(before(t, -1)))
                    finish(t, p, expert(t))
            last_t = Seq((TILES - 1) // 2, 0)
            finish(last_t, 0, expert(last_t))



def kernel(**inputs):
    import concourse.bacc as bacc
    from concourse.bass_utils import run_bass_kernel_spmd

    def columns(a):
        n, d = a.shape
        return a.reshape(n, d // P, P).transpose(2, 0, 1).reshape(P, -1)

    g = {k.replace("L0_", ""): np.asarray(v) for k, v in inputs.items()}
    E, F, D = g["ffn_w1"].shape
    arrays = {
        "x": g["attn_x"], "wq": g["attn_wq"], "wk": g["attn_wk"], "wv": g["attn_wv"], "wo": g["attn_wo"],
        "wg1": g["attn_wg1"], "wg2": g["attn_wg2"], "norm_w": columns(g["attn_norm_w"][None]),
        "centroids": g["ffn_centroids"].reshape(E, D // P, P).transpose(2, 1, 0).reshape(P, -1),
        "ln_g": columns(g["ffn_ln_g"]), "ln_b": columns(g["ffn_ln_b"]),
        "w1": g["ffn_w1"].reshape(E, F, D // P, P).transpose(3, 0, 2, 1).reshape(P, -1),
        "b1": g["ffn_b1"],
        "w2": g["ffn_w2"].reshape(E, D, F // P, P).transpose(3, 0, 2, 1).reshape(P, -1),
        "b2": g["ffn_b2"],
    }
    arrays = {k: np.ascontiguousarray(v) for k, v in arrays.items()}
    nc = bacc.Bacc("TRN2", target_bir_lowering=False, num_devices=1)
    args = [nc.dram_tensor(k, v.shape, mybir.dt.from_np(v.dtype), kind="ExternalInput").ap() for k, v in arrays.items()]
    shape = g["attn_x"].shape
    out = nc.dram_tensor("out", (shape[0] * shape[1], shape[2]), F32, kind="ExternalOutput").ap()
    build_program(nc, *args, out)
    got = run_bass_kernel_spmd(nc, [arrays], core_ids=[0])
    return got.results[0]["out"].reshape(shape)
```

```python
from contextlib import ExitStack
from collections import namedtuple

import numpy as np
import concourse.bass as bass
from concourse import mybir

ALU = mybir.AluOpType
ACT = mybir.ActivationFunctionType
F32 = mybir.dt.float32
BF16 = mybir.dt.bfloat16
I32 = mybir.dt.int32
U8 = mybir.dt.uint8
AX_X = mybir.AxisListType.X

P = 128
EPS = 1e-5

Step = namedtuple("Step", "half par of")


def before(s, n):
    v = s.par - n
    return Step(s.half + v // s.of, v % s.of, s.of)


def number(s):
    return s.half * s.of + s.par


def need(eng, sem, per, s, k):
    base = per * s.par + k + 1
    if not isinstance(s.half, int):
        eng.wait_ge(sem, s.half * (s.of * per) + base)
    elif s.of * per * s.half + base > 1:
        eng.wait_ge(sem, s.of * per * s.half + base)


def start_at_one(eng, sems):
    for s in sems:
        eng.sem_inc(s, 1)


def build_program(nc, x, wq, wk, wv, wo, wg1, wg2, norm_w, centroids_t, ln_g, ln_b, w1_t, b1, w2_t, b2, out):
    NSEQ, T, D = x.shape
    G1 = wg1.shape[1]
    E, F = b1.shape
    TJ = T // P
    DC = D // P
    H = D // P
    NCH = H * TJ
    FC = F // P
    N = NSEQ * T
    NT = N // P
    TILES = NT + E - 1
    TS = TILES + 1
    LEVELS = 7
    HALF = P // 2
    QSCALE = (2.0 * P) ** -0.5
    RW = 2 * D + 1
    SKIP = 2 * N
    SLOTS = 4
    PAIRS = NCH // 2
    LAST = (TILES - 1) // SLOTS
    assert D == 2 * P and T == 4 * P and G1 == P and NSEQ % 2 == 0 and E == 8

    rows = nc.dram_tensor("routed_rows", (N, RW), F32, kind="Internal").ap()

    ctx = ExitStack()
    with ctx:
        def sb(name, shape, dt):
            return ctx.enter_context(nc.sbuf_tensor(name, shape, dt))

        def sem(name):
            return ctx.enter_context(nc.semaphore(name))

        w1_sb = sb("w1_sb", [P, E * DC * F], F32)
        PHASE1_AB = 24576
        ARENA = 33408
        arena = sb("arena", [P, ARENA], F32)

        class Layout:
            def __init__(self, at, end):
                self.at, self.end = at, end

            def take(self, n):
                self.at += n
                assert self.at <= self.end, (self.at, self.end)
                return arena[:, self.at - n:self.at]

        lay = Layout(0, PHASE1_AB)
        x_sb = [lay.take(TJ * D) for _ in range(2)]
        xn = lay.take(TJ * D)
        xn_t = lay.take(DC * T)
        q_raw = lay.take(H * T)
        qk = lay.take(H * T)
        g1_t = lay.take(T)
        kq = [lay.take(2 * H * T) for _ in range(2)]
        decay = [lay.take(2 * H * T) for _ in range(2)]
        v_sb = [lay.take(TJ * D) for _ in range(2)]
        gate = [lay.take(TJ * D) for _ in range(2)]
        attn_t = [lay.take(NCH * P) for _ in range(2)]
        k_tok = lay.take((TJ - 1) * D)
        state = lay.take((TJ - 1) * D)
        wq_sb = lay.take(DC * D)
        wk_sb = lay.take(DC * D)
        wv_sb = lay.take(DC * D)
        wg1_sb = lay.take(DC * G1)
        wg2_sb = lay.take(D)
        lay = Layout(PHASE1_AB, ARENA)
        o_sb = lay.take(TJ * D)
        o_t = lay.take(DC * T)
        x_res = lay.take(TJ * D)
        x1 = lay.take(TJ * D)
        xn2 = lay.take(TJ * D)
        xn2_t = lay.take(DC * T)
        row_sb = lay.take(TJ * RW + 4)[:, 0:TJ * RW]
        wo_sb = lay.take(DC * D)
        mask_f = xn2[:, 0:LEVELS * 2 * HALF]
        lay3 = Layout(0, PHASE1_AB)
        w2_sb = lay3.take(E * FC * D)
        b1_sb = lay3.take(E * F)
        lay3 = Layout(PHASE1_AB, ARENA)
        gathered = [lay3.take(RW + 3)[:, 0:RW] for _ in range(SLOTS)]
        xl_t = [lay3.take(DC * P) for _ in range(SLOTS)]
        h_sb = lay3.take(F)
        h_t = lay3.take(F)
        y_sb = lay3.take(D)
        y_out = [lay3.take(D) for _ in range(SLOTS)]
        lay2 = Layout(PHASE1_AB, ARENA)
        WIDE = NT * E
        aff_max = lay2.take(NT)
        is_max = lay2.take(WIDE)
        first = lay2.take(NT)
        onehot = lay2.take(WIDE)
        count_e = lay2.take(WIDE)
        cum_e = lay2.take(WIDE)
        place = is_max
        slot = lay2.take(NT)
        slot_i = lay2.take(NT).bitcast(I32)
        hi_i = lay2.take(NT).bitcast(I32)
        lo_i = lay2.take(NT).bitcast(I32)
        hi_f = lay2.take(NT)
        lo_f = lay2.take(NT)
        small = lay2.take(12 * E)
        ntile_i = lay2.take(2 * E).bitcast(I32)
        ge_f = lay2.take(TS * E)
        texp_f = lay2.take(TS)
        slot_f = lay2.take(4 * TS)
        lo_hot = lay2.take(NT * P // 2).bitcast(BF16)
        hi_hot = lay2.take(NT * 3 * TS // 2).bitcast(BF16)

        k_mix = [sb(f"k_mix{i}", [P, PAIRS * P], F32)[:, :] for i in range(2)]
        b2_sb = Layout(max(lay2.at, lay3.at), ARENA).take(E * D)
        ident = sb("ident", [P, P], F32)
        ones = sb("ones", [P, P], F32)
        below = sb("below", [P, P], F32)
        masks = sb("masks", [P, LEVELS * NCH * HALF], U8)
        norm_col = sb("norm_col", [P, DC], F32)
        cent_sb = sb("cent_sb", [P, DC * E], F32)
        g_col = sb("g_col", [P, E * DC], F32)
        b_col = sb("b_col", [P, E * DC], F32)
        aff = sb("aff", [P, NT * E], F32)
        iota_e = sb("iota_e", [P, E], F32)
        iota_t = sb("iota_t", [P, TS], F32)
        iota_r = sb("iota_r", [P, P], F32)
        iota_p = sb("iota_p", [P, 1], F32)
        minus_half = sb("minus_half", [P, TJ], F32)
        tile_expert = sb("tile_expert", [P, TS], I32)
        take_idx = sb("take_idx", [P, TS], I32)
        put_idx = sb("put_idx", [P, TS], I32)
        take_now = sb("take_now", [P, SLOTS], I32)
        put_now = sb("put_now", [P, SLOTS], I32)
        aff_best = sb("aff_best", [P, TJ], F32)
        stat = {n: sb(f"{n}_stat", [P, TJ, 6], F32) for n in "xouz"}
        mom = {n: sb(f"{n}_mom", [P, TJ, 2], F32) for n in "xouz"}
        var_eps = {n: sb(f"{n}_vareps", [P, TJ], F32) for n in "xouz"}
        rstd = {n: sb(f"{n}_rstd", [P, TJ], F32) for n in "xouz"}
        shift = {n: sb(f"{n}_shift", [P, TJ], F32) for n in "uz"}

        bank_a = [ctx.enter_context(nc.psum_tensor(f"bank_a{i}", [P, 512], F32)) for i in range(2)]
        bank_l = [ctx.enter_context(nc.psum_tensor(f"bank_l{i}", [P, 512], F32)) for i in range(2)]
        bank_b = [ctx.enter_context(nc.psum_tensor(f"bank_b{i}", [P, 512], F32)) for i in range(2)]
        bank_c = [ctx.enter_context(nc.psum_tensor(f"bank_c{i}", [P, 512], F32)) for i in range(2)]


        s_x = [sem(f"x_loaded{i}") for i in range(2)]
        s_xres = sem("xres_loaded")
        s_row_out = sem("rows_stored")
        s_wqk = sem("wqk_loaded")
        s_wvg = sem("wvg_loaded")
        s_wo_in = sem("wo_loaded")
        s_small = sem("small_loaded")
        s_w1 = sem("w1_loaded")
        s_w2 = sem("w2_loaded")
        s_b1 = sem("b1_loaded")
        s_b2 = sem("b2_loaded")
        s_const = sem("constants_ready")
        s_setup = sem("setup_step")
        s_held = sem("wait_held")
        s_wo = sem("wo_scaled")
        s_stat = {n: sem(f"{n}_stats") for n in "xouz"}
        s_mom = {n: sem(f"{n}_moments") for n in "xouz"}
        s_ve = {n: sem(f"{n}_var_eps") for n in "xouz"}
        s_rstd = {n: sem(f"{n}_rstd_ready") for n in "xouz"}
        s_shift = {n: sem(f"{n}_shift_ready") for n in "uz"}
        s_xn = sem("xn_ready")
        s_tp = sem("xn_transposed")
        s_xnt = sem("xnt_ready")
        s_kz = sem("kz_done")
        s_k = sem("k_ready")
        s_f = sem("f_ready")
        s_f0 = sem("decay0_ready")
        s_qz = sem("qz_done")
        s_qs = sem("q_sigmoid_ready")
        s_q = sem("q_ready")
        s_g1z = sem("g1z_done")
        s_g1 = sem("g1_ready")
        s_vz = sem("vz_done")
        s_v = sem("v_ready")
        s_gz = sem("gatez_done")
        s_gate = sem("gate_ready")
        s_qk = sem("qk_ready")
        s_tree = sem("decay_tree")
        s_q0 = sem("q0_ready")
        s_dz = sem("diag_summed")
        s_at0 = sem("attn_diag_set")
        s_lev = sem("level_scores")
        s_up = sem("level_update")
        s_mix = sem("keys_mixed")
        s_pick = sem("level_picked")
        s_k7 = sem("k_transposed")
        s_kt = sem("k_tok_ready")
        s_kv = sem("kv_done")
        s_state = sem("state_ready")
        s_o = sem("o_done")
        s_og = sem("o_gated")
        s_on = sem("on_ready")
        s_ot = sem("on_transposed")
        s_ont = sem("ont_ready")
        s_y = sem("proj_done")
        s_x1 = sem("x1_ready")
        s_xn2 = sem("xn2_ready")
        s_t2 = sem("xn2_transposed")
        s_xn2t = sem("xn2t_ready")
        s_affz = sem("aff_done")
        s_best = sem("best_ready")
        s_aff = sem("aff_ready")
        s_alpha = sem("alpha_ready")
        s_base = sem("base_ready")
        s_zn = sem("zn_ready")
        s_r = sem("route_step")
        s_rank = sem("ranks_done")
        s_hot = sem("onehots_ready")
        s_inv = sem("inverse_done")
        s_idx = sem("indices_ready")
        s_take = sem("take_idx_ready")
        s_rows = [sem(f"rows_gathered{i}") for i in range(SLOTS)]
        s_zt = sem("z_transposed")
        s_xl = sem("xl_ready")
        s_h = sem("h_done")
        s_hb = sem("h_biased")
        s_ht = sem("h_transposed")
        s_hr = sem("h_relu")
        s_ye = sem("y_done")
        s_yb = sem("y_biased")
        s_yo = sem("y_ready")
        s_put = sem("put_idx_ready")
        s_out = [sem(f"rows_out{i}") for i in range(SLOTS)]
        s_mask = sem("mask_made")

        def tiles(buf, w=D):
            return buf.rearrange("p (j d) -> p j d", d=w)

        def tree(buf, l):
            n = H * T
            at = 0 if l == 0 else 2 * n - (2 * n >> l)
            return buf[:, at:at + (n >> l)]

        def halves(ap, l):
            return ap.rearrange("p (n two h) -> p n two h", two=2, h=2 ** l)

        def factor(buf, l, which):
            n = P >> (l + 1)
            return strided(tree(buf, l), which, [2 * n, NCH], [2, n], [0, 2 ** l])

        def strided(base, at, *dims):
            return bass.AP(base.tensor, base.offset + at, [list(base.ap[0]), *[list(d) for d in dims]])

        K_EVEN, Q_EVEN, Q_ODD, K_ODD = 0, P, 2 * P, 3 * P
        PAIR = 4 * P

        def keys(buf, h=None):
            n = PAIRS if h is None else PAIRS // H
            return strided(buf, 0 if h is None else h * n * PAIR, [PAIR, n], [K_ODD - K_EVEN, 2], [1, P])

        def queries(buf):
            return strided(buf, Q_EVEN, [PAIR, PAIRS], [1, 2 * P])

        def chunk(buf, h, c, which):
            at = (h * TJ // 2 + c // 2) * PAIR + which[c % 2]
            return buf[:, at:at + P]

        KEY, QUERY = (K_EVEN, K_ODD), (Q_EVEN, Q_ODD)

        def level_queries(buf, m, l):
            h = 2 ** l
            return strided(buf, m * PAIR + Q_EVEN + h, [Q_ODD - Q_EVEN - h, 2], [2 * h, P // (2 * h)], [1, h])

        def updated(buf, l, odd):
            h = 2 ** l
            return strided(buf, odd * (P + h), [2 * P, NCH], [2 * h, P // (2 * h)], [1, h])

        def mixed_from(buf, l, odd):
            h = 2 ** l
            return strided(buf, (K_ODD + h) if odd else K_EVEN, [PAIR, PAIRS], [2 * h, P // (2 * h)], [1, h])

        def mixed_to(buf, l, odd):
            h = 2 ** l
            return strided(buf, odd * h, [P, PAIRS], [2 * h, P // (2 * h)], [1, h])

        def picked(buf, l, odd):
            h = 2 ** l
            return strided(buf, P if odd else h, [2 * P, PAIRS], [2 * h, P // (2 * h)], [1, h])

        def split_chunks(ap):
            return ap.rearrange("p (m two s) -> p m two s", two=2, s=P)

        def packed(ap, l):
            return ap.rearrange("p (n h) -> p n h", h=2 ** l)

        x_t = x.rearrange("b (j p) d -> b p j d", p=P)
        rows_t = rows.rearrange("(b j p) r -> b p j r", p=P, j=TJ)

        def seq_rows(ap, s):
            if isinstance(s.half, int):
                return ap[number(s)]
            return ap[bass.ds(number(s), 1)].squeeze(0)

        def need_apart(eng, sem, per, s, k):
            need(eng, sem, per, s, k)
            eng.sem_inc(s_held, 1)

        def column(buf, t):
            if isinstance(t.half, int):
                return buf[:, number(t):number(t) + 1]
            return buf[:, bass.ds(number(t), 1)]

        def aff_of(c):
            if isinstance(c.half, int):
                return aff[:, number(c) * TJ * E:(number(c) + 1) * TJ * E]
            return aff[:, bass.ds(number(c) * (TJ * E), TJ * E)]

        def expert_of(t):
            if isinstance(t.half, int):
                return tile_expert[0:1, number(t):number(t) + 1]
            return tile_expert[0:1, bass.ds(number(t), 1)]

        def ones_wide():
            return ones[:, 0:1].broadcast_to([P, WIDE])

        block = ctx.enter_context(nc.Block())

        def pipeline(eng, step):
            def at(i):
                a = Step(i // 2, i % 2, 2)
                step(a if i < NSEQ else None, before(a, 1) if 0 < i <= NSEQ else None, before(a, 2) if i > 1 else None,
                     before(a, -1) if i + 1 < NSEQ else None)

            for i in range(2):
                at(i)
            with eng.Fori(1, NSEQ // 2 - 1) as half:
                for par in range(2):
                    a = Step(half, par, 2)
                    step(a, before(a, 1), before(a, 2), before(a, -1))
            for i in range(NSEQ - 2, NSEQ + 2):
                at(i)

        def rounds(eng, turn):
            for i in range(SLOTS):
                turn(Step(0, i, SLOTS))
            with eng.Fori(1, LAST - 1) as r:
                for i in range(SLOTS):
                    turn(Step(r, i, SLOTS))
            for i in range((LAST - 1) * SLOTS, TILES):
                turn(Step(i // SLOTS, i % SLOTS, SLOTS))

        def exists(t):
            return not isinstance(t.half, int) or number(t) < TILES

        @block.sync
        def _(sp):
            sp.sem_inc(s_row_out, 16)
            sp.dma_start(tiles(x_sb[0]), x_t[0]).then_inc(s_x[0], 16)
            sp.dma_start(wk_sb.rearrange("p (c n) -> p c n", c=DC), wk.rearrange("(c p) n -> p c n", p=P)).then_inc(s_wqk, 16)
            sp.dma_start(wq_sb.rearrange("p (c n) -> p c n", c=DC), wq.rearrange("(c p) n -> p c n", p=P)).then_inc(s_wqk, 16)
            sp.dma_start(tiles(x_sb[1]), x_t[1]).then_inc(s_x[1], 16)

            def step(a, b, c, nxt):
                if nxt is not None and b is not None:
                    need_apart(sp, s_xn, TJ, b, TJ)
                    sp.dma_start(tiles(x_sb[nxt.par]), seq_rows(x_t, nxt)).then_inc(s_x[nxt.par], 16)
                if b is not None:
                    need_apart(sp, s_x1, 2, b, 0)
                    sp.dma_start(tiles(x_res), seq_rows(x_t, b)).then_inc(s_xres, 16)
                if c is not None:
                    need_apart(sp, s_zn, TJ, c, TJ)
                    need_apart(sp, s_base, 1, c, 1)
                    need_apart(sp, s_alpha, 1, c, 1)
                    sp.dma_start(seq_rows(rows_t, c), tiles(row_sb, RW)).then_inc(s_row_out, 16)

                if a is None and b is not None:
                    need(sp, s_o, 2, b, 2)
                    need(sp, s_og, 2, b, 2)
                    for e in range(E):
                        w = slice(e * FC * D, (e + 1) * FC * D)
                        sp.dma_start(w2_sb[:, w], w2_t[:, w]).then_inc(s_w2, 16)

            pipeline(sp, step)
            sp.dma_start(b1_sb, b1.rearrange("e f -> (e f)").partition_broadcast(P)).then_inc(s_b1, 16)
            need(sp, s_y, 2, Step(NSEQ // 2 - 1, 1, 2), 2)
            sp.wait_ge(s_row_out, 16 * NSEQ + 16)
            sp.dma_start(b2_sb, b2.rearrange("e f -> (e f)").partition_broadcast(P)).then_inc(s_b2, 16)

        @block.gpsimd
        def _(pool):
            start_at_one(pool, [*s_ve.values(), *s_rstd.values(), s_tree, s_qk, s_q0, s_base, s_take, s_put])
            made = 0

            def own(ins):
                nonlocal made
                made += 1
                ins.then_inc(s_setup, 1)
                pool.wait_ge(s_setup, made)

            own(pool.memset(ident[:, :], 0.0))
            own(pool.affine_select(out=ident[:, :], in_=ident[:, :], compare_op=ALU.not_equal, fill=1.0, base=0,
                                   pattern=[[-1, P]], channel_multiplier=1))
            pool.memset(minus_half[:, :], -0.5)
            own(pool.memset(ones[:, :], 1.0))
            pool.iota(iota_e[:, :], pattern=[[1, E]], base=0, channel_multiplier=0, allow_small_or_imprecise_dtypes=True)
            pool.iota(iota_t[:, :], pattern=[[1, TS]], base=0, channel_multiplier=0, allow_small_or_imprecise_dtypes=True)
            pool.iota(iota_r[:, :], pattern=[[1, P]], base=0, channel_multiplier=0, allow_small_or_imprecise_dtypes=True)
            own(pool.iota(iota_p[:, :], pattern=[[0, 1]], base=0, channel_multiplier=1, allow_small_or_imprecise_dtypes=True))
            own(pool.affine_select(out=below[:, :], in_=ones[:, :], compare_op=ALU.is_gt, fill=0.0, base=0,
                                   pattern=[[1, P]], channel_multiplier=-1))
            pool.sem_inc(s_const, 1)

            def make_masks():
                pool.memset(mask_f, 1.0).then_inc(s_setup, 1)
                for side in range(2):
                    pool.wait_ge(s_setup, made + 1 + side * 2 * LEVELS)
                    for l in range(LEVELS):
                        h = 2 ** l
                        for odd in range(2):
                            at = (2 * l + odd) * HALF
                            view = mask_f[:, at:at + HALF].rearrange("p (n h) -> p n h", h=h)
                            sign = -1 if side else 1
                            pool.affine_select(out=view, in_=view, compare_op=ALU.is_ge, fill=0.0,
                                               base=(1 + odd) * h - 1 if side else -odd * h,
                                               pattern=[[-sign * 2 * h, HALF // h], [0, h]],
                                               channel_multiplier=sign).then_inc(s_setup, 1)
                pool.wait_ge(s_setup, made + 1 + 4 * LEVELS)
                pool.sem_inc(s_mask, 1)

            def norm(n, s):
                need_apart(pool, s_mom[n], TJ, s, TJ)
                pool.tensor_scalar(var_eps[n][:, :], mom[n][:, :, 1], EPS, None, ALU.add).then_inc(s_ve[n], 1)
                need(pool, s_ve[n], 1, s, 1)
                pool.tensor_tensor(rstd[n][:, :], var_eps[n][:, :], minus_half[:, :], ALU.pow).then_inc(s_rstd[n], 1)

            def step(a, b, c, nxt):
                if a is not None:
                    dec = decay[a.par]
                    need(pool, s_f0, 1, a, 1)
                    need(pool, s_state, 5, before(a, 2), 5)
                    for l in range(1, LEVELS + 1):
                        if l > 1:
                            need(pool, s_tree, LEVELS, a, l - 1)
                        two = tree(dec, l - 1).rearrange("p (n two) -> p n two", two=2)
                        pool.tensor_tensor(tree(dec, l), two[:, :, 0], two[:, :, 1], ALU.mult).then_inc(s_tree, 1)
                if c is not None:
                    need(pool, s_xn2, TJ, c, 0)
                    norm("u", c)
                if a is not None:
                    need(pool, s_q, H, a, H)
                    need(pool, s_k, H, a, H)
                    need(pool, s_dz, H, a, 0)
                    pool.tensor_tensor(split_chunks(qk), split_chunks(q_raw), keys(kq[a.par]), ALU.mult).then_inc(s_qk, 1)
                    need(pool, s_o, 2, before(a, 2), 2)
                    pool.tensor_tensor(queries(kq[a.par]), q_raw.rearrange("p (m s) -> p m s", s=2 * P),
                                       tree(dec, 0).rearrange("p (m s) -> p m s", s=2 * P), ALU.mult).then_inc(s_q0, 1)
                if nxt is not None:
                    norm("x", nxt)
                if c is not None:
                    need(pool, s_xn2, TJ, c, TJ)
                    pool.wait_ge(s_row_out, number(c) * 16 + 16)
                    pool.tensor_tensor(tiles(row_sb, RW)[:, :, D:2 * D], tiles(x1), tiles(xn2), ALU.add).then_inc(s_base, 1)
                    need(pool, s_zn, TJ, c, 0)
                    norm("z", c)
                if b is not None:
                    norm("o", b)

            norm("x", Step(0, 0, 2))
            make_masks()
            pipeline(pool, step)

            pool.wait_ge(s_row_out, 16 * NSEQ + 16)
            pool.wait_ge(s_idx, 3)

            def gather(t):
                p = t.par
                need(pool, s_yo, 1, before(t, SLOTS), 1)
                pool.tensor_copy(take_now[:, p:p + 1], column(take_idx, t)).then_inc(s_take, 1)
                need_apart(pool, s_take, 1, t, 1)
                pool.indirect_dma_start(out=gathered[p], out_offset=None, in_=rows,
                                        in_offset=bass.IndirectOffsetOnAxis(ap=take_now[:, p:p + 1], axis=0)).then_inc(s_rows[p], 16)

            def scatter(t):
                p = t.par
                if not isinstance(t.half, int) or t.half > 0:
                    pool.wait_ge(s_out[p], t.half * 16)
                pool.tensor_copy(put_now[:, p:p + 1], column(put_idx, t)).then_inc(s_put, 1)
                need_apart(pool, s_put, 1, t, 1)
                need_apart(pool, s_yo, 1, t, 1)
                pool.indirect_dma_start(out=out, out_offset=bass.IndirectOffsetOnAxis(ap=put_now[:, p:p + 1], axis=0),
                                        in_=y_out[p], in_offset=None, bounds_check=N - 1, oob_is_err=False).then_inc(s_out[p], 16)

            for p in range(SLOTS):
                gather(Step(0, p, SLOTS))

            def turn(t):
                if exists(before(t, -SLOTS)):
                    gather(before(t, -SLOTS))
                scatter(t)

            rounds(pool, turn)
            for p in range(SLOTS):
                pool.wait_ge(s_out[p], 16 * ((TILES - p + SLOTS - 1) // SLOTS))

        @block.scalar
        def _(act):
            start_at_one(act, [s_mix, s_xnt, s_k, s_qs, s_g1, s_v, s_gate, s_kt, s_ont, s_xn2, s_xn2t, s_aff, s_alpha, s_zn, s_xl, s_hr])
            act.dma_start(wg1_sb.rearrange("p (c n) -> p c n", c=DC), wg1.rearrange("(c p) n -> p c n", p=P)).then_inc(s_wvg, 16)
            act.dma_start(wv_sb.rearrange("p (c n) -> p c n", c=DC), wv.rearrange("(c p) n -> p c n", p=P)).then_inc(s_wvg, 16)
            act.dma_start(wg2_sb, wg2).then_inc(s_wvg, 16)
            act.dma_start(wo_sb.rearrange("p (c n) -> p c n", c=DC), wo.rearrange("(c p) n -> p c n", p=P)).then_inc(s_wo_in, 16)
            act.dma_start(norm_col[:, :], norm_w).then_inc(s_wo_in, 16)
            act.dma_start(cent_sb[:, :], centroids_t).then_inc(s_small, 16)
            act.dma_start(g_col[:, :], ln_g).then_inc(s_small, 16)
            act.dma_start(b_col[:, :], ln_b).then_inc(s_small, 16)
            for e in range(E):
                act.dma_start(w1_sb[:, e * DC * F:(e + 1) * DC * F], w1_t[:, e * DC * F:(e + 1) * DC * F]).then_inc(s_w1, 16)

            def copy(dst, src):
                return act.activation(dst, src, ACT.Copy)

            def mix(b, l):
                if l == 0:
                    need(act, s_k, H, b, H)
                    need(act, s_lev, LEVELS, b, 0)
                else:
                    need(act, s_lev, LEVELS, b, l - 1)
                for odd in range(2):
                    if l > 0:
                        need(act, s_up, 2 * LEVELS, b, 2 * l - 1 + odd)
                    copy(mixed_to(k_mix[l % 2], l, odd), mixed_from(kq[b.par], l, odd)).then_inc(s_mix, 1)

            def k_sigmoid(a, h):
                need(act, s_kz, H, a, h + 1)
                if h == 0:
                    need(act, s_k7, 1, before(a, 2), 1)
                act.activation(keys(kq[a.par], h), split_chunks(bank_a[h][:, :]), ACT.Sigmoid).then_inc(s_k, 1)

            def q_sigmoid(a, h):
                need(act, s_qz, H, a, h + 1)
                if h == 0:
                    need(act, s_qk, 1, a, 0)
                    need(act, s_q0, 1, a, 0)
                act.activation(q_raw[:, h * T:(h + 1) * T], bank_a[h][:, :], ACT.Sigmoid).then_inc(s_qs, 1)

            def step(a, b, c, nxt):
                if b is not None:
                    mix(b, 0)
                if a is not None:
                    for i in range(DC):
                        need(act, s_tp, DC, a, i + 1)
                        if i == 0:
                            need(act, s_gz, 2, a, 0)
                        copy(xn_t[:, i * T:(i + 1) * T], bank_a[i][:, :]).then_inc(s_xnt, 1)
                if b is not None:
                    mix(b, 1)
                if a is not None:
                    k_sigmoid(a, 0)
                if b is not None:
                    mix(b, 2)
                if a is not None:
                    k_sigmoid(a, 1)
                if c is not None:
                    for i in range(DC):
                        need(act, s_ot, DC, c, i + 1)
                        if i == 0:
                            need(act, s_y, 2, c, 0)
                        copy(o_t[:, i * T:(i + 1) * T], bank_c[i][:, :]).then_inc(s_ont, 1)
                if b is not None:
                    mix(b, 3)
                if a is not None:
                    q_sigmoid(a, 0)
                if b is not None:
                    mix(b, 4)
                    mix(b, 5)
                    mix(b, 6)
                if a is not None:
                    q_sigmoid(a, 1)
                if c is not None:
                    need(act, s_shift["u"], 1, c, 1)
                    need(act, s_base, 1, c, 0)
                    need(act, s_stat["z"], TJ, c, 0)
                    need(act, s_t2, DC, c, 0)
                    for j in range(TJ):
                        act.activation(tiles(xn2)[:, j], tiles(x1)[:, j], ACT.Identity, bias=shift["u"][:, j:j + 1],
                                       scale=rstd["u"][:, j:j + 1]).then_inc(s_xn2, 1)
                if b is not None:
                    need(act, s_k7, 1, b, 1)
                    need(act, s_kv, 2, b, 0)
                    copy(k_tok[:, 0:512], bank_b[0][:, :]).then_inc(s_kt, 1)
                    copy(k_tok[:, 512:768], bank_b[1][:, 0:256]).then_inc(s_kt, 1)
                if a is not None:
                    need(act, s_g1z, 1, a, 1)
                    copy(g1_t, bank_a[0][:, :]).then_inc(s_g1, 1)
                if c is not None:
                    need(act, s_affz, 1, c, 0)
                    for i in range(DC):
                        need(act, s_t2, DC, c, i + 1)
                        copy(xn2_t[:, i * T:(i + 1) * T], bank_c[i][:, :]).then_inc(s_xn2t, 1)
                if a is not None:
                    need(act, s_o, 2, before(a, 2), 2)
                    for i in range(2):
                        need(act, s_vz, 2, a, i + 1)
                        copy(v_sb[a.par][:, i * 512:(i + 1) * 512], bank_a[1 - i][:, :]).then_inc(s_v, 1)
                    need(act, s_og, 2, before(a, 2), 2)
                    for i in range(2):
                        need(act, s_gz, 2, a, i + 1)
                        act.activation(gate[a.par][:, i * 512:(i + 1) * 512], bank_a[1 - i][:, :], ACT.Sigmoid).then_inc(s_gate, 1)
                if c is not None:
                    need(act, s_affz, 1, c, 1)
                    need(act, s_best, 1, c, 1)
                    copy(aff_of(c), bank_c[0][:, 0:TJ * E]).then_inc(s_aff, 1)
                    act.wait_ge(s_row_out, number(c) * 16 + 16)
                    act.activation(tiles(row_sb, RW)[:, :, 2 * D], aff_best[:, :], ACT.Sigmoid).then_inc(s_alpha, 1)
                    need(act, s_shift["z"], 1, c, 1)
                    for j in range(TJ):
                        act.activation(tiles(row_sb, RW)[:, j, 0:D], tiles(xn2)[:, j], ACT.Identity, bias=shift["z"][:, j:j + 1],
                                       scale=rstd["z"][:, j:j + 1]).then_inc(s_zn, 1)

            pipeline(act, step)

            act.wait_ge(s_small, 48)
            act.wait_ge(s_idx, 3)

            def gains(t):
                p = t.par
                e = act.value_load(expert_of(t), min_val=0, max_val=E - 1)
                need(act, s_zt, 1, t, 1)
                need(act, s_h, 2, before(t, SLOTS), 2)
                for i in range(DC):
                    act.activation(xl_t[p][:, i * P:(i + 1) * P], bank_b[0][:, i * P:(i + 1) * P], ACT.Identity,
                                   bias=b_col[:, bass.ds(e * DC + i, 1)], scale=g_col[:, bass.ds(e * DC + i, 1)]).then_inc(s_xl, 1)

            def relu(t):
                need(act, s_ye, 1, t, 0)
                for i in range(2):
                    need(act, s_ht, 2, t, i + 1)
                    act.activation(h_t[:, i * 512:(i + 1) * 512], bank_l[i][:, :], ACT.Relu).then_inc(s_hr, 1)

            def turn(t):
                relu(t)
                if exists(before(t, -2)):
                    gains(before(t, -2))

            for i in range(2):
                gains(Step(0, i, SLOTS))
            rounds(act, turn)

        @block.tensor
        def _(pe):
            start_at_one(pe, [s_tp, s_kz, s_qz, s_g1z, s_vz, s_gz, s_dz, s_lev, s_k7, s_kv, s_o, s_ot, s_y, s_t2, s_affz, s_zt, s_h, s_ht, s_ye])
            def level(b, l):
                buf = kq[b.par]
                if l == 0:
                    need(pe, s_q0, 1, b, 1)
                need(pe, s_mix, 2 * LEVELS, b, 2 * l + 2)
                need(pe, s_pick, 2 * LEVELS, b, 2 * max(l - 1, 0))
                for m in range(PAIRS):
                    bank = bank_l[l % 2][:, m * P:(m + 1) * P].rearrange("p (two n h) -> p two n h", two=2, h=2 ** l)
                    ins = pe.matmul(bank, k_mix[l % 2][:, m * P:(m + 1) * P], level_queries(buf, m, l), start=True, stop=True)
                ins.then_inc(s_lev, 1)

            def transposes(a):
                need(pe, s_xn, TJ, a, TJ)
                for i in range(DC):
                    need(pe, s_at0, H, a, 0)
                    for j in range(TJ):
                        m = pe.transpose(bank_a[i][:, j * P:(j + 1) * P], tiles(xn)[:, j, i * P:(i + 1) * P], ident[:, :])
                    m.then_inc(s_tp, 1)

            def channels(a, w, h, bank, done):
                for i in range(DC):
                    m = pe.matmul(bank[:, :], w[:, i * D + h * P:i * D + (h + 1) * P], xn_t[:, i * T:(i + 1) * T],
                                  start=(i == 0), stop=(i == DC - 1))
                m.then_inc(done, 1)

            def k_proj(a, h):
                need(pe, s_xnt, DC, a, DC)
                channels(a, wk_sb, h, bank_a[h], s_kz)

            def q_proj(a, h):
                need(pe, s_k, H, a, h + 1)
                channels(a, wq_sb, h, bank_a[h], s_qz)

            def g1_proj(a):
                need(pe, s_q, H, a, 1)
                need(pe, s_gz, 2, a, 0)
                for i in range(DC):
                    m = pe.matmul(bank_a[0][:, :], wg1_sb[:, i * G1:(i + 1) * G1], xn_t[:, i * T:(i + 1) * T],
                                  start=(i == 0), stop=(i == DC - 1))
                m.then_inc(s_g1z, 1)

            def v_proj(a, half, between=None):
                if half == 0:
                    need(pe, s_q, H, a, 2)
                else:
                    need(pe, s_g1, 1, a, 1)
                for j in range(2):
                    for i in range(DC):
                        t0 = i * T + (2 * half + j) * P
                        m = pe.matmul(bank_a[1 - half][:, j * D:(j + 1) * D], xn_t[:, t0:t0 + P], wv_sb[:, i * D:(i + 1) * D],
                                      start=(i == 0), stop=(i == DC - 1))
                        if (j, i) == (1, DC - 1):
                            m.then_inc(s_vz, 1)
                        if between is not None:
                            between(DC * j + i)

            def gate_proj(a, half, between=None):
                need(pe, s_g1, 1, a, 1)
                need(pe, s_v, 2, a, half + 1)
                for j in range(2):
                    t0 = (2 * half + j) * P
                    m = pe.matmul(bank_a[1 - half][:, j * D:(j + 1) * D], g1_t[:, t0:t0 + P], wg2_sb[:, :], start=True, stop=True)
                    if j == 1:
                        m.then_inc(s_gz, 1)
                    if between is not None:
                        between(DC * TJ // 2 + 2 * half + j)

            def diagonal(a):
                for h in range(H):
                    need(pe, s_qk, 1, a, 1)
                    need(pe, s_gate, 2, a, h + 1)
                    pe.matmul(bank_a[1 - h][:, :], ones[:, :], qk[:, h * T:(h + 1) * T], start=True, stop=True).then_inc(s_dz, 1)

            def k_transposes(b):
                need(pe, s_up, 2 * LEVELS, b, 2 * LEVELS)
                need(pe, s_og, 2, b, 0)
                for c in range(TJ - 1):
                    for h in range(H):
                        n = c * H + h
                        m = pe.transpose(bank_b[n // 4][:, n % 4 * P:(n % 4 + 1) * P],
                                         chunk(kq[b.par], h, c, KEY), ident[:, :])
                m.then_inc(s_k7, 1)

            def key_values(b):
                need(pe, s_v, 2, b, 2)
                for c in range(TJ - 1):
                    for h in range(H):
                        n = c * H + h
                        if n % 4 == 0:
                            need(pe, s_kt, 2, b, n // 4 + 1)
                        if n == 4:
                            m.then_inc(s_kv, 1)
                        m = pe.matmul(bank_b[n // 4][:, n % 4 * P:(n % 4 + 1) * P], k_tok[:, n * P:(n + 1) * P],
                                      v_sb[b.par][:, n * P:(n + 1) * P], start=True, stop=True)
                m.then_inc(s_kv, 1)

            def outputs(b):
                need(pe, s_pick, 2 * LEVELS, b, 2 * LEVELS)
                need(pe, s_state, 5, b, 5)
                for c in range(TJ):
                    for h in range(H):
                        dst = bank_b[c // 2][:, c % 2 * D + h * P:c % 2 * D + (h + 1) * P]
                        t0 = h * T + c * P
                        if c > 0:
                            n = (c - 1) * H + h
                            pe.matmul(dst, chunk(kq[b.par], h, c, QUERY), state[:, n * P:(n + 1) * P], start=True, stop=False)
                        m = pe.matmul(dst, attn_t[b.par][:, t0:t0 + P], v_sb[b.par][:, c * D + h * P:c * D + (h + 1) * P],
                                      start=(c == 0), stop=True)
                    if c % 2:
                        m.then_inc(s_o, 1)

            def o_transposes(c):
                need(pe, s_on, TJ, c, TJ)
                for i in range(DC):
                    if i == 0:
                        need(pe, s_aff, 1, c, 0)
                        need(pe, s_best, 1, c, 0)
                    else:
                        need(pe, s_xn2t, DC, c, 0)
                    for j in range(TJ):
                        m = pe.transpose(bank_c[i][:, j * P:(j + 1) * P], tiles(o_sb)[:, j, i * P:(i + 1) * P], ident[:, :])
                    m.then_inc(s_ot, 1)

            def out_proj(c, half):
                need(pe, s_ont, DC, c, DC)
                for j in range(2):
                    for i in range(DC):
                        t0 = i * T + (2 * half + j) * P
                        m = pe.matmul(bank_c[half][:, j * D:(j + 1) * D], o_t[:, t0:t0 + P], wo_sb[:, i * D:(i + 1) * D],
                                      start=(i == 0), stop=(i == DC - 1))
                m.then_inc(s_y, 1)

            def xn2_transposes(c):
                need(pe, s_xn2, TJ, c, TJ)
                need(pe, s_x1, 2, c, 2)
                for i in range(DC):
                    for j in range(TJ):
                        m = pe.transpose(bank_c[i][:, j * P:(j + 1) * P], tiles(xn2)[:, j, i * P:(i + 1) * P], ident[:, :])
                    m.then_inc(s_t2, 1)

            def affinity(c, n):
                j, i = n // DC, n % DC
                if n == 0:
                    need(pe, s_xn2t, DC, c, DC)
                m = pe.matmul(bank_c[0][:, j * E:(j + 1) * E], xn2_t[:, i * T + j * P:i * T + (j + 1) * P],
                              cent_sb[:, i * E:(i + 1) * E], start=(i == 0), stop=(i == DC - 1))
                if n == DC * TJ - 1:
                    m.then_inc(s_affz, 1)

            def step(a, b, c, nxt):
                if b is not None:
                    level(b, 0)
                if a is not None:
                    transposes(a)
                    k_proj(a, 0)
                if b is not None:
                    level(b, 1)
                if a is not None:
                    k_proj(a, 1)
                if b is not None:
                    level(b, 2)
                if c is not None:
                    o_transposes(c)
                if a is not None:
                    q_proj(a, 0)
                if b is not None:
                    level(b, 3)
                if c is not None:
                    out_proj(c, 0)
                if b is not None:
                    level(b, 4)
                if c is not None:
                    out_proj(c, 1)
                if b is not None:
                    level(b, 5)
                if a is not None:
                    q_proj(a, 1)
                if b is not None:
                    level(b, 6)
                if a is not None:
                    g1_proj(a)
                if b is not None:
                    k_transposes(b)
                if c is not None:
                    xn2_transposes(c)
                if a is not None:
                    v_proj(a, 0)
                if b is not None:
                    key_values(b)
                if a is not None:
                    between = None if c is None else lambda n: affinity(c, n)
                    v_proj(a, 1, between)
                    gate_proj(a, 0, between)
                    gate_proj(a, 1, between)
                    diagonal(a)
                elif c is not None:
                    for n in range(DC * TJ):
                        affinity(c, n)
                if b is not None:
                    outputs(b)

            pe.wait_ge(s_const, 1)
            pe.wait_ge(s_wqk, 32)
            pe.wait_ge(s_wvg, 48)
            pe.wait_ge(s_wo, DC)
            pe.wait_ge(s_small, 48)
            pipeline(pe, step)

            pe.wait_ge(s_r, 5)
            pe.matmul(bank_a[0][:, 0:WIDE], below[:, :], onehot, start=True, stop=True)
            pe.matmul(bank_a[1][:, 0:WIDE], ones[:, :], onehot, start=True, stop=True).then_inc(s_rank, 1)
            for g in range(4):
                pe.wait_ge(s_hot, g + 4)
                for t in range(g * NT // 4, (g + 1) * NT // 4):
                    m = pe.matmul(bank_b[1][:, 0:3 * TS], lo_hot[:, t * P:(t + 1) * P], hi_hot[:, t * 3 * TS:(t + 1) * 3 * TS],
                                  start=(t == 0), stop=(t == NT - 1))
            m.then_inc(s_inv, 1)

            def z_transposes(t):
                p = t.par
                pe.wait_ge(s_rows[p], t.half * 16 + 16)
                need(pe, s_xl, DC, t, 0)
                for i in range(DC):
                    m = pe.transpose(bank_b[0][:, i * P:(i + 1) * P], gathered[p][:, i * P:(i + 1) * P], ident[:, :])
                m.then_inc(s_zt, 1)

            def up(t):
                e = pe.value_load(expert_of(t), min_val=0, max_val=E - 1)
                need(pe, s_xl, DC, t, DC)
                need(pe, s_hb, 2, t, 0)
                for n in range(2):
                    for i in range(DC):
                        m = pe.matmul(bank_a[n][:, :], xl_t[t.par][:, i * P:(i + 1) * P],
                                      w1_sb[:, bass.ds(e * (DC * F) + (i * F + n * 512), 512)], start=(i == 0), stop=(i == DC - 1))
                    m.then_inc(s_h, 1)

            def h_transposes(t):
                for n in range(2):
                    need(pe, s_hb, 2, t, n + 1)
                    need(pe, s_hr, 2, t, 0)
                    for j in range(4):
                        k = 4 * n + j
                        m = pe.transpose(bank_l[n][:, j * P:(j + 1) * P], h_sb[:, k * P:(k + 1) * P], ident[:, :])
                    m.then_inc(s_ht, 1)

            def down(t):
                e = pe.value_load(expert_of(t), min_val=0, max_val=E - 1)
                need(pe, s_yb, 1, before(t, 2), 1)
                for k in range(FC):
                    if k % 4 == 0:
                        need(pe, s_hr, 2, t, k // 4 + 1)
                    m = pe.matmul(bank_c[t.par % 2][:, 0:D], h_t[:, k * P:(k + 1) * P],
                                  w2_sb[:, bass.ds(e * (FC * D) + k * D, D)], start=(k == 0), stop=(k == FC - 1))
                m.then_inc(s_ye, 1)

            pe.wait_ge(s_idx, 3)
            pe.wait_ge(s_w1, 16 * E)
            z_transposes(Step(0, 0, SLOTS))
            z_transposes(Step(0, 1, SLOTS))
            up(Step(0, 0, SLOTS))
            pe.wait_ge(s_w2, 16 * E)

            def turn(t):
                h_transposes(t)
                if exists(before(t, -1)):
                    up(before(t, -1))
                if exists(before(t, -2)):
                    z_transposes(before(t, -2))
                down(t)

            rounds(pe, turn)

        @block.vector
        def _(dve):
            start_at_one(dve, [*s_stat.values(), *s_mom.values(), *s_shift.values(), s_xn, s_f, s_f0, s_q, s_up, s_pick, s_state, s_og,
                               s_on, s_x1, s_at0, s_best, s_hb, s_yb, s_yo])
            def stats(n, src, s):
                for j in range(TJ):
                    dve.bn_stats(stat[n][:, j, :], tiles(src)[:, j]).then_inc(s_stat[n], 1)
                for j in range(TJ):
                    need_apart(dve, s_stat[n], TJ, s, j + 1)
                    dve.bn_aggr(mom[n][:, j, :], stat[n][:, j, :]).then_inc(s_mom[n], 1)

            def apply_norm(n, src, dst, s, done):
                need(dve, s_rstd[n], 1, s, 1)
                for j in range(TJ):
                    dve.tensor_scalar(tiles(dst)[:, j], tiles(src)[:, j], mom[n][:, j, 0:1], rstd[n][:, j:j + 1],
                                      ALU.subtract, ALU.mult).then_inc(done, 1)

            def shifts(n, s):
                need(dve, s_rstd[n], 1, s, 1)
                dve.scalar_tensor_tensor(out=shift[n][:, :], in0=mom[n][:, :, 0], scalar=-1.0, in1=rstd[n][:, :],
                                         op0=ALU.mult, op1=ALU.mult).then_inc(s_shift[n], 1)

            def x_stats(a):
                dve.wait_ge(s_x[a.par], a.half * 16 + 16)
                stats("x", x_sb[a.par], a)

            def x_norm(a):
                need(dve, s_tp, DC, a, 0)
                apply_norm("x", x_sb[a.par], xn, a, s_xn)

            def update(b, l):
                buf, dec = kq[b.par], decay[b.par]
                need(dve, s_lev, LEVELS, b, l + 1)
                if l > 0:
                    need(dve, s_tree, LEVELS, b, l)
                    need(dve, s_up, 2 * LEVELS, b, 2 * l)
                for odd in range(2):
                    half = updated(buf, l, odd)
                    dve.tensor_tensor(half, half, factor(dec, l, 1 - odd), ALU.mult).then_inc(s_up, 1)

            def pick(b, l):
                if l == 0:
                    need_apart(dve, s_at0, H, b, H)
                else:
                    need_apart(dve, s_pick, 2 * LEVELS, b, 2 * l)
                for odd in range(2):
                    m0 = (2 * l + odd) * PAIRS * HALF
                    mask = masks[:, m0:m0 + PAIRS * HALF].rearrange("p (m n h) -> p m n h", m=PAIRS, h=2 ** l)
                    scores = bank_l[l % 2][:, :].rearrange("p (m two s) -> p m two s", m=PAIRS, two=2)[:, :, odd, :]
                    dve.copy_predicated(picked(attn_t[b.par], l, odd), mask, scores.rearrange("p m (n h) -> p m n h", h=2 ** l)).then_inc(s_pick, 1)

            def attn_diagonal(a):
                need(dve, s_o, 2, before(a, 2), 2)
                for h in range(H):
                    need(dve, s_dz, H, a, h + 1)
                    dve.tensor_tensor(attn_t[a.par][:, h * T:(h + 1) * T].rearrange("p (n t) -> p n t", t=P),
                                      bank_a[1 - h][:, :].rearrange("p (n t) -> p n t", t=P),
                                      ident[:, :].unsqueeze(1).broadcast_to([P, TJ, P]), ALU.mult).then_inc(s_at0, 1)

            def decays(a):
                need(dve, s_k, H, a, H)
                need(dve, s_up, 2 * LEVELS, before(a, 2), 2 * LEVELS)
                f0 = tree(decay[a.par], 0)
                dve.tensor_scalar(split_chunks(f0), keys(kq[a.par]), -1.0, 1.0, ALU.mult, ALU.add).then_inc(s_f, 1)
                need(dve, s_f, 1, a, 1)
                dve.scalar_tensor_tensor(out=f0, in0=f0, scalar=0.5, in1=f0, op0=ALU.is_equal,
                                         op1=ALU.subtract).then_inc(s_f0, 1)

            def q_mult(a, h):
                need(dve, s_qs, H, a, h + 1)
                dve.tensor_tensor(q_raw[:, h * T:(h + 1) * T], bank_a[h][:, :], q_raw[:, h * T:(h + 1) * T],
                                  ALU.mult).then_inc(s_q, 1)

            def residual(c, half):
                need(dve, s_y, 2, c, half + 1)
                if half == 0:
                    dve.wait_ge(s_xres, number(c) * 16 + 16)
                    need(dve, s_base, 1, c, 0)
                w = slice(half * 512, half * 512 + 512)
                dve.tensor_tensor(x1[:, w], bank_c[half][:, :], x_res[:, w], ALU.add).then_inc(s_x1, 1)

            def states(b):
                need(dve, s_kv, 2, b, 1)
                f7 = tree(decay[b.par], LEVELS)
                dve.tensor_copy(state[:, 0:D], bank_b[0][:, 0:D]).then_inc(s_state, 1)
                for c in range(1, TJ - 1):
                    for h in range(H):
                        n = c * H + h
                        if h == 0:
                            need(dve, s_state, 5, b, 2 * c - 1)
                        if n == 4:
                            need(dve, s_kv, 2, b, 2)
                        dve.scalar_tensor_tensor(out=state[:, n * P:(n + 1) * P], in0=state[:, (n - H) * P:(n - H + 1) * P],
                                                 scalar=f7[:, h * TJ + c:h * TJ + c + 1],
                                                 in1=bank_b[n // 4][:, n % 4 * P:(n % 4 + 1) * P],
                                                 op0=ALU.mult, op1=ALU.add).then_inc(s_state, 1)

            def gating(b):
                need(dve, s_gate, 2, b, 2)
                need(dve, s_ot, DC, b, 0)
                for i in range(2):
                    need(dve, s_o, 2, b, i + 1)
                    w = slice(i * 512, i * 512 + 512)
                    dve.scalar_tensor_tensor(out=o_sb[:, w], in0=bank_b[i][:, :], scalar=QSCALE, in1=gate[b.par][:, w],
                                             op0=ALU.mult, op1=ALU.mult).then_inc(s_og, 1)

            def step(a, b, c, nxt):
                def level(l):
                    if b is not None:
                        update(b, l)
                        pick(b, l)

                level(0)
                if c is not None:
                    apply_norm("o", o_sb, o_sb, c, s_on)
                level(1)
                level(2)
                if a is not None:
                    decays(a)
                level(3)
                if a is not None:
                    q_mult(a, 0)
                level(4)
                if c is not None:
                    residual(c, 0)
                level(5)
                if c is not None:
                    residual(c, 1)
                    need(dve, s_x1, 2, c, 2)
                    stats("u", x1, c)
                level(6)
                if a is not None:
                    q_mult(a, 1)
                if c is not None:
                    shifts("u", c)
                if nxt is not None:
                    x_stats(nxt)
                if c is not None:
                    need(dve, s_xn2, TJ, c, TJ)
                    stats("z", xn2, c)
                if b is not None:
                    states(b)
                if nxt is not None:
                    x_norm(nxt)
                if c is not None:
                    need(dve, s_zn, TJ, c, 0)
                    shifts("z", c)
                    need(dve, s_affz, 1, c, 1)
                    need(dve, s_alpha, 1, c, 0)
                    dve.tensor_reduce(aff_best[:, :], bank_c[0][:, 0:TJ * E].rearrange("p (j e) -> p j e", e=E), AX_X,
                                      ALU.max).then_inc(s_best, 1)
                if a is not None:
                    attn_diagonal(a)
                if b is not None:
                    gating(b)
                    need(dve, s_og, 2, b, 2)
                    stats("o", o_sb, b)

            dve.wait_ge(s_wo_in, 32)
            for i in range(DC):
                dve.tensor_scalar(wo_sb[:, i * D:(i + 1) * D], wo_sb[:, i * D:(i + 1) * D], norm_col[:, i:i + 1], None,
                                  ALU.mult).then_inc(s_wo, 1)
            x_stats(Step(0, 0, 2))
            x_norm(Step(0, 0, 2))
            dve.wait_ge(s_mask, 1)
            dve.tensor_copy(masks[:, :].rearrange("p (l m s) -> p l m s", m=PAIRS, s=HALF),
                            mask_f.rearrange("p (l s) -> p l s", s=HALF).unsqueeze(2).broadcast_to([P, 2 * LEVELS, PAIRS, HALF])).then_inc(s_mask, 1)
            dve.wait_ge(s_mask, 2)
            pipeline(dve, step)

            done = 0

            def own(ins):
                nonlocal done
                done += 1
                ins.then_inc(s_r, 1)
                dve.wait_ge(s_r, done)

            def te(ap):
                return ap.rearrange("p (t e) -> p t e", e=E)

            def over_t(ap):
                return ap.unsqueeze(1).broadcast_to([P, NT, E])

            def over_e(ap):
                return ap.unsqueeze(2).broadcast_to([P, NT, E])

            dve.wait_ge(s_aff, NSEQ + 1)
            dve.wait_ge(s_zn, TJ * NSEQ + 1)
            dve.wait_ge(s_base, NSEQ + 1)
            own(dve.tensor_reduce(aff_max, te(aff[:, :]), AX_X, ALU.max))
            own(dve.tensor_tensor(te(is_max), te(aff[:, :]), over_e(aff_max), ALU.is_equal))
            own(dve.scalar_tensor_tensor(out=te(is_max), in0=te(is_max), scalar=-float(E), in1=over_t(iota_e[:, :]),
                                         op0=ALU.mult, op1=ALU.add))
            own(dve.tensor_reduce(first, te(is_max), AX_X, ALU.min))
            own(dve.scalar_tensor_tensor(out=te(onehot), in0=over_t(iota_e[:, :]), scalar=-float(E), in1=over_e(first),
                                         op0=ALU.add, op1=ALU.is_equal))
            dve.wait_ge(s_rank, 1)
            own(dve.tensor_copy(count_e.rearrange("p (e t) -> p t e", e=E), te(bank_a[1][:, 0:WIDE])))
            own(dve.tensor_tensor_scan(out=cum_e, data0=ones_wide(), data1=count_e, initial=0.0, op0=ALU.mult, op1=ALU.add))
            upto = small[:, 0:E]
            n_e = small[:, E:2 * E]
            prior = small[:, 2 * E:3 * E]
            n_up = small[:, 3 * E:4 * E]
            nt_e = small[:, 4 * E:5 * E]
            t_upto = small[:, 5 * E:6 * E]
            off = small[:, 6 * E:7 * E]
            own(dve.tensor_copy(upto, cum_e.rearrange("p (e t) -> p e t", e=E)[:, :, NT - 1]))
            own(dve.tensor_reduce(n_e, count_e.rearrange("p (e t) -> p e t", e=E), AX_X, ALU.add))
            own(dve.tensor_tensor(prior, upto, n_e, ALU.subtract))
            own(dve.tensor_scalar(n_up, n_e, float(P - 1), None, ALU.add))
            own(dve.tensor_copy(ntile_i[:, 0:E], n_up))
            own(dve.tensor_scalar(ntile_i[:, E:2 * E], ntile_i[:, 0:E], 7, None, ALU.arith_shift_right))
            own(dve.tensor_copy(nt_e, ntile_i[:, E:2 * E]))
            own(dve.tensor_tensor_scan(out=t_upto, data0=ones[:, 0:E], data1=nt_e, initial=0.0, op0=ALU.mult, op1=ALU.add))
            own(dve.tensor_tensor(off, t_upto, nt_e, ALU.subtract))
            own(dve.scalar_tensor_tensor(out=off, in0=off, scalar=float(P), in1=prior, op0=ALU.mult, op1=ALU.subtract))
            own(dve.tensor_tensor(cum_e, cum_e, count_e, ALU.subtract))
            own(dve.tensor_tensor(te(place), te(bank_a[0][:, 0:WIDE]), cum_e.rearrange("p (e t) -> p t e", e=E), ALU.add))
            own(dve.tensor_tensor(te(place), te(place), over_t(off), ALU.add))
            own(dve.tensor_tensor(place, place, onehot, ALU.mult))
            own(dve.tensor_reduce(slot, te(place), AX_X, ALU.add))
            own(dve.tensor_copy(slot_i, slot))
            own(dve.tensor_scalar(hi_i, slot_i, 7, None, ALU.arith_shift_right))
            own(dve.tensor_scalar(lo_i, slot_i, P - 1, None, ALU.bitwise_and))
            own(dve.tensor_copy(hi_f, hi_i))
            own(dve.tensor_copy(lo_f, lo_i))
            hot = hi_hot.rearrange("p (t k s) -> p t k s", k=3, s=TS)
            wide = [P, NT, TS]
            dve.tensor_tensor(hot[:, :, 0, :], iota_t[:, :].unsqueeze(1).broadcast_to(wide), hi_f.unsqueeze(2).broadcast_to(wide),
                              ALU.is_equal).then_inc(s_hot, 1)
            dve.wait_ge(s_hot, 1)
            dve.tensor_scalar(hot[:, :, 1, :], hot[:, :, 0, :], iota_p[:, 0:1], None, ALU.mult).then_inc(s_hot, 1)
            dve.tensor_tensor(hot[:, :, 2, :], hot[:, :, 0, :], iota_t[:, 0:NT].unsqueeze(2).broadcast_to(wide),
                              ALU.mult).then_inc(s_hot, 1)
            lo3 = lo_hot.rearrange("p (t r) -> p t r", r=P)
            for g in range(4):
                n = NT // 4
                dve.tensor_tensor(lo3[:, g * n:(g + 1) * n], iota_r[:, :].unsqueeze(1).broadcast_to([P, n, P]),
                                  lo_f[:, g * n:(g + 1) * n].unsqueeze(2).broadcast_to([P, n, P]), ALU.is_equal).then_inc(s_hot, 1)
            own(dve.tensor_tensor(ge_f[:, 0:TS * (E - 1)].rearrange("p (s e) -> p s e", e=E - 1),
                                  iota_t[:, :].unsqueeze(2).broadcast_to([P, TS, E - 1]),
                                  t_upto[:, 0:E - 1].unsqueeze(1).broadcast_to([P, TS, E - 1]), ALU.is_ge))
            own(dve.tensor_reduce(texp_f, ge_f[:, 0:TS * (E - 1)].rearrange("p (s e) -> p s e", e=E - 1), AX_X, ALU.add))
            dve.tensor_copy(tile_expert[:, :], texp_f).then_inc(s_idx, 1)
            dve.wait_ge(s_inv, 1)
            own(dve.tensor_copy(slot_f[:, 0:3 * TS], bank_b[1][:, 0:3 * TS]))
            own(dve.scalar_tensor_tensor(out=slot_f[:, 3 * TS:4 * TS], in0=slot_f[:, 2 * TS:3 * TS], scalar=float(P),
                                         in1=slot_f[:, TS:2 * TS], op0=ALU.mult, op1=ALU.add))
            own(dve.tensor_scalar(slot_f[:, 0:TS], slot_f[:, 0:TS], -float(SKIP), float(SKIP), ALU.mult, ALU.add))
            dve.tensor_copy(take_idx[:, :], slot_f[:, 3 * TS:4 * TS]).then_inc(s_idx, 1)
            dve.tensor_tensor(put_idx[:, :], slot_f[:, 0:TS], slot_f[:, 3 * TS:4 * TS], ALU.add).then_inc(s_idx, 1)

            dve.wait_ge(s_idx, 3)
            dve.wait_ge(s_b1, 16)
            dve.wait_ge(s_b2, 16)

            def bias_h(t):
                e = dve.value_load(expert_of(t), min_val=0, max_val=E - 1)
                need(dve, s_ht, 2, t, 0)
                for n in range(2):
                    need(dve, s_h, 2, t, n + 1)
                    dve.tensor_tensor(h_sb[:, n * 512:(n + 1) * 512], bank_a[n][:, :],
                                      b1_sb[:, bass.ds(e * F + n * 512, 512)], ALU.add).then_inc(s_hb, 1)

            def finish(t):
                p = t.par
                e = dve.value_load(expert_of(t), min_val=0, max_val=E - 1)
                need(dve, s_ye, 1, t, 1)
                need(dve, s_yo, 1, t, 0)
                dve.tensor_tensor(y_sb, bank_c[p % 2][:, 0:D], b2_sb[:, bass.ds(e * D, D)], ALU.add).then_inc(s_yb, 1)
                need(dve, s_yb, 1, t, 1)
                if not isinstance(t.half, int) or t.half > 0:
                    dve.wait_ge(s_out[p], t.half * 16)
                dve.scalar_tensor_tensor(out=y_out[p], in0=y_sb, scalar=gathered[p][:, 2 * D:2 * D + 1],
                                         in1=gathered[p][:, D:2 * D], op0=ALU.mult, op1=ALU.add).then_inc(s_yo, 1)

            def turn(t):
                if exists(before(t, -1)):
                    bias_h(before(t, -1))
                finish(t)

            bias_h(Step(0, 0, SLOTS))
            rounds(dve, turn)


def kernel(**inputs):
    import concourse.bacc as bacc
    from concourse.bass_utils import run_bass_kernel_spmd

    def columns(a):
        n, d = a.shape
        return a.reshape(n, d // P, P).transpose(2, 0, 1).reshape(P, -1)

    def odd_reversed(a):
        a = a.reshape(-1, 2, P, a.shape[-1])
        return np.stack([a[:, 0], a[:, 1, ::-1]], axis=1)

    g = {k.replace("L0_", ""): np.asarray(v) for k, v in inputs.items()}
    E, F, D = g["ffn_w1"].shape
    arrays = {
        "x": odd_reversed(g["attn_x"]).reshape(g["attn_x"].shape), "wq": g["attn_wq"], "wk": g["attn_wk"], "wv": g["attn_wv"], "wo": g["attn_wo"],
        "wg1": g["attn_wg1"], "wg2": g["attn_wg2"], "norm_w": columns(g["attn_norm_w"][None]),
        "centroids": g["ffn_centroids"].reshape(E, D // P, P).transpose(2, 1, 0).reshape(P, -1),
        "ln_g": columns(g["ffn_ln_g"]), "ln_b": columns(g["ffn_ln_b"]),
        "w1": g["ffn_w1"].reshape(E, F, D // P, P).transpose(3, 0, 2, 1).reshape(P, -1),
        "b1": g["ffn_b1"],
        "w2": g["ffn_w2"].reshape(E, D, F // P, P).transpose(3, 0, 2, 1).reshape(P, -1),
        "b2": g["ffn_b2"],
    }
    arrays = {k: np.ascontiguousarray(v) for k, v in arrays.items()}
    nc = bacc.Bacc("TRN2", target_bir_lowering=False, num_devices=1)
    args = [nc.dram_tensor(k, v.shape, mybir.dt.from_np(v.dtype), kind="ExternalInput").ap() for k, v in arrays.items()]
    shape = g["attn_x"].shape
    out = nc.dram_tensor("out", (shape[0] * shape[1], shape[2]), F32, kind="ExternalOutput").ap()
    build_program(nc, *args, out)
    got = run_bass_kernel_spmd(nc, [arrays], core_ids=[0])
    return odd_reversed(got.results[0]["out"]).reshape(shape)
```

```python
from contextlib import ExitStack
from collections import namedtuple

import numpy as np
import concourse.bass as bass
from concourse import mybir

ALU = mybir.AluOpType
ACT = mybir.ActivationFunctionType
F32 = mybir.dt.float32
BF16 = mybir.dt.bfloat16
F32R = mybir.dt.float32r
I32 = mybir.dt.int32
U8 = mybir.dt.uint8
AX_X = mybir.AxisListType.X

P = 128
EPS = 1e-5

Step = namedtuple("Step", "half par of")


def before(s, n):
    v = s.par - n
    return Step(s.half + v // s.of, v % s.of, s.of)


def number(s):
    return s.half * s.of + s.par


def need(eng, sem, per, s, k):
    base = per * s.par + k + 1
    if not isinstance(s.half, int):
        eng.wait_ge(sem, s.half * (s.of * per) + base)
    elif s.of * per * s.half + base > 1:
        eng.wait_ge(sem, s.of * per * s.half + base)


def start_at_one(eng, sems):
    for s in sems:
        eng.sem_inc(s, 1)


def build_program(nc, x, wq, wk, wv, wo, wg1, wg2, norm_w, centroids_t, ln_g, ln_b, w1_t, b1, w2_t, b2, out):
    NSEQ, T, D = x.shape
    G1 = wg1.shape[1]
    E = b2.shape[0]
    F = w1_t.shape[1] // (E * (D // P))
    TJ = T // P
    DC = D // P
    H = D // P
    NCH = H * TJ
    FC = F // P
    N = NSEQ * T
    NT = N // P
    TILES = NT + E - 1
    TS = TILES + 1
    LEVELS = 7
    HALF = P // 2
    QSCALE = (2.0 * P) ** -0.5
    RW = 2 * D + 1
    SKIP = 2 * N
    SLOTS = 4
    PAIRS = NCH // 2
    LAST = (TILES - 1) // SLOTS
    assert D == 2 * P and T == 4 * P and G1 == P and NSEQ % 2 == 0 and E == 8

    rows = nc.dram_tensor("routed_rows", (N, RW), F32, kind="Internal").ap()

    ctx = ExitStack()
    with ctx:
        def sb(name, shape, dt):
            return ctx.enter_context(nc.sbuf_tensor(name, shape, dt))

        def sem(name):
            return ctx.enter_context(nc.semaphore(name))

        w1_sb = sb("w1_sb", [P, E * DC * F], F32)
        PHASE1_AB = 24576
        ARENA = 33808
        arena_at = nc.sbuf_base
        arena = sb("arena", [P, ARENA], F32)

        class Layout:
            def __init__(self, at, end):
                self.at, self.end = at, end

            def take(self, n):
                self.at += n
                assert self.at <= self.end, (self.at, self.end)
                return arena[:, self.at - n:self.at]

            def take_rounded(self, name, n):
                self.take(n)
                return nc.alloc_sbuf_tensor_at(name, [P, n], F32R, offset=arena_at + 4 * (self.at - n))[:, :]

        lay = Layout(0, PHASE1_AB)
        x_sb = [lay.take(TJ * D) for _ in range(2)]
        xn = lay.take(TJ * D)
        xn_t = lay.take(DC * T)
        q_raw = lay.take(H * T)
        qk = lay.take(H * T)
        g1_t = lay.take(T)
        kq = [lay.take(2 * H * T) for _ in range(2)]
        decay = [lay.take(2 * H * T) for _ in range(2)]
        v_sb = [lay.take(TJ * D) for _ in range(2)]
        gate = [lay.take(TJ * D) for _ in range(2)]
        attn_t = [lay.take(NCH * P) for _ in range(2)]
        k_tok = lay.take((TJ - 1) * D)
        state = lay.take((TJ - 1) * D)
        wq_sb = lay.take(DC * D)
        wk_sb = lay.take(DC * D)
        wv_sb = lay.take(DC * D)
        wg1_sb = lay.take(DC * G1)
        wg2_sb = lay.take(D)
        lay = Layout(PHASE1_AB, ARENA)
        o_sb = lay.take(TJ * D)
        o_t = lay.take(DC * T)
        x_res = lay.take(TJ * D)
        x1 = lay.take(TJ * D)
        xn2 = lay.take(TJ * D)
        xn2_t = lay.take(DC * T)
        row_sb = lay.take(TJ * RW + 4)[:, 0:TJ * RW]
        wo_sb = lay.take(DC * D)
        mask_f = xn2[:, 0:LEVELS * 2 * HALF]
        lay3 = Layout(0, PHASE1_AB)
        w2_sb = lay3.take(E * FC * D)
        w2_high = [lay3.take_rounded(f"w2_high{i}", FC * D) for i in range(2)]
        w2_low = [lay3.take_rounded(f"w2_low{i}", FC * D) for i in range(2)]
        lay3 = Layout(PHASE1_AB, ARENA)
        gathered = [lay3.take(RW + 3)[:, 0:RW] for _ in range(SLOTS)]
        h_sb = lay3.take(F)
        h_high = lay3.take_rounded("h_high", F)
        h_low = lay3.take_rounded("h_low", F)
        w1_now = lay3.take(DC * F)
        lay2 = Layout(PHASE1_AB, ARENA)
        WIDE = NT * E
        aff_max = lay2.take(NT)
        is_max = lay2.take(WIDE)
        first = lay2.take(NT)
        onehot = lay2.take(WIDE)
        count_e = lay2.take(WIDE)
        cum_e = lay2.take(WIDE)
        place = is_max
        slot = lay2.take(NT)
        slot_i = lay2.take(NT).bitcast(I32)
        hi_i = lay2.take(NT).bitcast(I32)
        lo_i = lay2.take(NT).bitcast(I32)
        hi_f = lay2.take(NT)
        lo_f = lay2.take(NT)
        small = lay2.take(12 * E)
        ntile_i = lay2.take(2 * E).bitcast(I32)
        ge_f = lay2.take(TS * E)
        texp_f = lay2.take(TS)
        slot_f = lay2.take(4 * TS)
        lo_hot = lay2.take(NT * P // 2).bitcast(BF16)
        hi_hot = lay2.take(NT * 3 * TS // 2).bitcast(BF16)
        hot = hi_hot.rearrange("p (t k s) -> p t k s", k=3, s=TS)
        wide = [P, NT, TS]
        iota_r = lay2.take(P)

        k_mix = [sb(f"k_mix{i}", [P, PAIRS * P], F32)[:, :] for i in range(2)]
        b2_sb = Layout(max(lay2.at, lay3.at), ARENA).take(E * D)
        ident = sb("ident", [P, P], F32)
        ones = sb("ones", [P, P], F32)
        masks = sb("masks", [P, LEVELS * NCH * HALF], U8)
        y_out = [k_mix[i // 2][:, i % 2 * D:(i % 2 + 1) * D] for i in range(SLOTS)]
        over_masks = masks[:, :].bitcast(F32)
        xl_t = [over_masks[:, i * DC * P:(i + 1) * DC * P] for i in range(2)]
        y_sb = over_masks[:, 2 * DC * P:2 * DC * P + D]
        not_below = over_masks[:, 2 * DC * P + D:2 * DC * P + D + P]
        norm_col = sb("norm_col", [P, DC], F32)
        cent_sb = sb("cent_sb", [P, DC * E], F32)
        g_col = sb("g_col", [P, E * DC], F32)
        b_col = sb("b_col", [P, E * DC], F32)
        b1_col = sb("b1_col", [P, E * FC], F32)
        aff = sb("aff", [P, NT * E], F32)
        iota_e = sb("iota_e", [P, E], F32)
        iota_t = sb("iota_t", [P, TS], F32)
        iota_p = sb("iota_p", [P, 1], F32)
        minus_half = sb("minus_half", [P, TJ], F32)
        tile_expert = sb("tile_expert", [P, TS], I32)
        take_idx = sb("take_idx", [P, TS], I32)
        put_idx = sb("put_idx", [P, TS], I32)
        take_now = sb("take_now", [P, SLOTS], I32)
        put_now = sb("put_now", [P, SLOTS], I32)
        aff_best = sb("aff_best", [P, TJ], F32)
        stat = {n: sb(f"{n}_stat", [P, TJ, 6], F32) for n in "xouz"}
        mom = {n: sb(f"{n}_mom", [P, TJ, 2], F32) for n in "xouz"}
        var_eps = {n: sb(f"{n}_vareps", [P, TJ], F32) for n in "xouz"}
        rstd = {n: sb(f"{n}_rstd", [P, TJ], F32) for n in "xouz"}
        shift = {n: sb(f"{n}_shift", [P, TJ], F32) for n in "xouz"}

        bank_a = [ctx.enter_context(nc.psum_tensor(f"bank_a{i}", [P, 512], F32)) for i in range(2)]
        bank_l = [ctx.enter_context(nc.psum_tensor(f"bank_l{i}", [P, 512], F32)) for i in range(2)]
        bank_b = [ctx.enter_context(nc.psum_tensor(f"bank_b{i}", [P, 512], F32)) for i in range(2)]
        bank_c = [ctx.enter_context(nc.psum_tensor(f"bank_c{i}", [P, 512], F32)) for i in range(2)]

        s_x = [sem(f"x_loaded{i}") for i in range(2)]
        s_xres = sem("xres_loaded")
        s_row_out = sem("rows_stored")
        s_wqk = sem("wqk_loaded")
        s_wvg = sem("wvg_loaded")
        s_wo_in = sem("wo_loaded")
        s_small = sem("small_loaded")
        s_w1 = sem("w1_loaded")
        s_w2 = sem("w2_loaded")
        s_b2 = sem("b2_loaded")
        s_const = sem("constants_ready")
        s_setup = sem("setup_step")
        s_held = sem("wait_held")
        s_wo = sem("wo_scaled")
        s_stat = {n: sem(f"{n}_stats") for n in "xouz"}
        s_mom = {n: sem(f"{n}_moments") for n in "xouz"}
        s_ve = {n: sem(f"{n}_var_eps") for n in "xouz"}
        s_rstd = {n: sem(f"{n}_rstd_ready") for n in "xouz"}
        s_shift = {n: sem(f"{n}_shift_ready") for n in "xouz"}
        s_xn = sem("xn_ready")
        s_tp = sem("xn_transposed")
        s_xnt = sem("xnt_ready")
        s_kz = sem("kz_done")
        s_k = sem("k_ready")
        s_f = sem("f_ready")
        s_f0 = sem("decay0_ready")
        s_qz = sem("qz_done")
        s_qs = sem("q_sigmoid_ready")
        s_q = sem("q_ready")
        s_g1z = sem("g1z_done")
        s_g1 = sem("g1_ready")
        s_vz = sem("vz_done")
        s_v = sem("v_ready")
        s_gz = sem("gatez_done")
        s_gate = sem("gate_ready")
        s_qk = sem("qk_ready")
        s_tree = sem("decay_tree")
        s_q0 = sem("q0_ready")
        s_dz = sem("diag_summed")
        s_at0 = sem("attn_diag_set")
        s_lev = sem("level_scores")
        s_up = sem("level_update")
        s_mix = sem("keys_mixed")
        s_pick = sem("level_picked")
        s_k7 = sem("k_transposed")
        s_kt = sem("k_tok_ready")
        s_kv = sem("kv_done")
        s_state = sem("state_ready")
        s_o = sem("o_done")
        s_og = sem("o_gated")
        s_on = sem("on_ready")
        s_ot = sem("on_transposed")
        s_ont = sem("ont_ready")
        s_y = sem("proj_done")
        s_x1 = sem("x1_ready")
        s_xn2 = sem("xn2_ready")
        s_t2 = sem("xn2_transposed")
        s_xn2t = sem("xn2t_ready")
        s_affz = sem("aff_done")
        s_best = sem("best_ready")
        s_aff = sem("aff_ready")
        s_alpha = sem("alpha_ready")
        s_base = sem("base_ready")
        s_zn = sem("zn_ready")
        s_r = sem("route_step")
        s_rank = sem("ranks_done")
        s_hot = sem("onehots_ready")
        s_hot_t = sem("onehots_times_tile_ready")
        s_inv = sem("inverse_done")
        s_idx = sem("indices_ready")
        s_take = sem("take_idx_ready")
        s_rows = [sem(f"rows_gathered{i}") for i in range(SLOTS)]
        s_zt = sem("z_transposed")
        s_xl = sem("xl_ready")
        s_h = sem("h_done")
        s_hb = sem("h_biased")
        s_now = sem("w1_now_ready")
        s_wh = sem("w2_high_ready")
        s_wl = [sem(f"w2_low{i}_ready") for i in range(2)]
        s_hl = sem("h_low_ready")
        s_hr = sem("h_high_ready")
        s_ye = sem("y_done")
        s_yb = sem("y_biased")
        s_yo = sem("y_ready")
        s_put = sem("put_idx_ready")
        s_out = [sem(f"rows_out{i}") for i in range(SLOTS)]
        s_mask = sem("mask_made")

        def tiles(buf, w=D):
            return buf.rearrange("p (j d) -> p j d", d=w)

        def tree(buf, l):
            n = H * T
            at = 0 if l == 0 else 2 * n - (2 * n >> l)
            return buf[:, at:at + (n >> l)]

        def factor(buf, h, l, second):
            n = P >> (l + 1)
            return strided(tree(buf, l), h * TJ * 2 * n + 1 - second, [2 * n, TJ], [2, n], [0, 2 ** l])

        def strided(base, at, *dims):
            return bass.AP(base.tensor, base.offset + at, [list(base.ap[0]), *[list(d) for d in dims]])

        K_EVEN, Q_EVEN, Q_ODD, K_ODD = 0, P, 2 * P, 3 * P
        PAIR = 4 * P

        def keys(buf, h=None):
            n = PAIRS if h is None else PAIRS // H
            return strided(buf, 0 if h is None else h * n * PAIR, [PAIR, n], [K_ODD - K_EVEN, 2], [1, P])

        def queries(buf):
            return strided(buf, Q_EVEN, [PAIR, PAIRS], [1, 2 * P])

        def chunk(buf, h, c, which):
            at = (h * TJ // 2 + c // 2) * PAIR + which[c % 2]
            return buf[:, at:at + P]

        KEY, QUERY = (K_EVEN, K_ODD), (Q_EVEN, Q_ODD)

        def level_queries(buf, m, l):
            h = 2 ** l
            return strided(buf, m * PAIR + Q_EVEN + h, [Q_ODD - Q_EVEN - h, 2], [2 * h, P // (2 * h)], [1, h])

        def updated(buf, h, l, second):
            w = 2 ** l
            return strided(buf, h * TJ * 2 * P + second * (P + w), [2 * P, TJ], [2 * w, P // (2 * w)], [1, w])

        def mixed_from(buf, h, l, odd):
            w = 2 ** l
            return strided(buf, h * TJ * 2 * P + odd * (K_ODD + w), [PAIR, PAIRS // H], [2 * w, P // (2 * w)], [1, w])

        def mixed_to(buf, h, l, odd):
            w = 2 ** l
            return strided(buf, h * (PAIRS // H) * P + odd * w, [P, PAIRS // H], [2 * w, P // (2 * w)], [1, w])

        def picked(buf, l, odd):
            h = 2 ** l
            return strided(buf, P if odd else h, [2 * P, PAIRS], [2 * h, P // (2 * h)], [1, h])

        def split_chunks(ap):
            return ap.rearrange("p (m two s) -> p m two s", two=2, s=P)

        x_t = x.rearrange("b (j p) d -> b p j d", p=P)
        rows_t = rows.rearrange("(b j p) r -> b p j r", p=P, j=TJ)

        def seq_rows(ap, s):
            if isinstance(s.half, int):
                return ap[number(s)]
            return ap[bass.ds(number(s), 1)].squeeze(0)

        def need_apart(eng, sem, per, s, k):
            need(eng, sem, per, s, k)
            eng.sem_inc(s_held, 1)

        def column(buf, t):
            if isinstance(t.half, int):
                return buf[:, number(t):number(t) + 1]
            return buf[:, bass.ds(number(t), 1)]

        def aff_of(c):
            if isinstance(c.half, int):
                return aff[:, number(c) * TJ * E:(number(c) + 1) * TJ * E]
            return aff[:, bass.ds(number(c) * (TJ * E), TJ * E)]

        def expert_of(t):
            if isinstance(t.half, int):
                return tile_expert[0:1, number(t):number(t) + 1]
            return tile_expert[0:1, bass.ds(number(t), 1)]

        def ones_wide():
            return ones[:, 0:1].broadcast_to([P, WIDE])

        def low_w2(eng, t, n):
            e = eng.value_load(expert_of(t), min_val=0, max_val=E - 1)
            need(eng, s_ye, 1, before(t, 2), 1)
            need(eng, s_wh, 2, t, n + 1)
            w = FC * D // 2
            eng.tensor_tensor(w2_low[t.par % 2][:, n * w:(n + 1) * w], w2_sb[:, bass.ds(e * (FC * D) + n * w, w)],
                              w2_high[t.par % 2][:, n * w:(n + 1) * w], ALU.subtract).then_inc(s_wl[n], 1)

        block = ctx.enter_context(nc.Block())

        def pipeline(eng, step):
            def at(i):
                a = Step(i // 2, i % 2, 2)
                step(a if i < NSEQ else None, before(a, 1) if 0 < i <= NSEQ else None, before(a, 2) if i > 1 else None,
                     before(a, -1) if i + 1 < NSEQ else None)

            for i in range(2):
                at(i)
            with eng.Fori(1, NSEQ // 2 - 1) as half:
                for par in range(2):
                    a = Step(half, par, 2)
                    step(a, before(a, 1), before(a, 2), before(a, -1))
            for i in range(NSEQ - 2, NSEQ + 2):
                at(i)

        def rounds(eng, turn):
            for i in range(SLOTS):
                turn(Step(0, i, SLOTS))
            with eng.Fori(1, LAST - 1) as r:
                for i in range(SLOTS):
                    turn(Step(r, i, SLOTS))
            for i in range((LAST - 1) * SLOTS, TILES):
                turn(Step(i // SLOTS, i % SLOTS, SLOTS))

        def exists(t):
            return not isinstance(t.half, int) or number(t) < TILES

        @block.sync
        def _(sp):
            sp.sem_inc(s_row_out, 16)
            sp.dma_start(tiles(x_sb[0]), x_t[0]).then_inc(s_x[0], 16)
            sp.dma_start(wk_sb.rearrange("p (c n) -> p c n", c=DC), wk.rearrange("(c p) n -> p c n", p=P)).then_inc(s_wqk, 16)
            sp.dma_start(wq_sb.rearrange("p (c n) -> p c n", c=DC), wq.rearrange("(c p) n -> p c n", p=P)).then_inc(s_wqk, 16)
            sp.dma_start(tiles(x_sb[1]), x_t[1]).then_inc(s_x[1], 16)
            sp.dma_start(wo_sb.rearrange("p (c n) -> p c n", c=DC), wo.rearrange("(c p) n -> p c n", p=P)).then_inc(s_wo_in, 16)
            sp.dma_start(norm_col[:, :], norm_w).then_inc(s_wo_in, 16)
            sp.dma_start(cent_sb[:, :], centroids_t).then_inc(s_small, 16)
            sp.dma_start(g_col[:, :], ln_g).then_inc(s_small, 16)
            sp.dma_start(b_col[:, :], ln_b).then_inc(s_small, 16)
            sp.dma_start(b1_col[:, :], b1).then_inc(s_small, 16)
            for e in range(E):
                sp.dma_start(w1_sb[:, e * DC * F:(e + 1) * DC * F], w1_t[:, e * DC * F:(e + 1) * DC * F]).then_inc(s_w1, 16)

            def step(a, b, c, nxt):
                if nxt is not None and b is not None:
                    need_apart(sp, s_xn, TJ, b, TJ)
                    sp.dma_start(tiles(x_sb[nxt.par]), seq_rows(x_t, nxt)).then_inc(s_x[nxt.par], 16)
                if b is not None:
                    need_apart(sp, s_x1, 2, b, 0)
                    sp.dma_start(tiles(x_res), seq_rows(x_t, b)).then_inc(s_xres, 16)
                if c is not None:
                    need_apart(sp, s_zn, TJ, c, TJ)
                    need_apart(sp, s_base, 1, c, 1)
                    need_apart(sp, s_alpha, 1, c, 1)
                    sp.dma_start(seq_rows(rows_t, c), tiles(row_sb, RW)).then_inc(s_row_out, 16)

                if a is None and b is not None:
                    need(sp, s_o, 2, b, 2)
                    need(sp, s_og, 2, b, 2)
                    for e in range(E):
                        w = slice(e * FC * D, (e + 1) * FC * D)
                        sp.dma_start(w2_sb[:, w], w2_t[:, w]).then_inc(s_w2, 16)

            pipeline(sp, step)
            need(sp, s_y, 2, Step(NSEQ // 2 - 1, 1, 2), 2)
            sp.wait_ge(s_row_out, 16 * NSEQ + 16)
            sp.dma_start(b2_sb, b2.rearrange("e f -> (e f)").partition_broadcast(P)).then_inc(s_b2, 16)

        @block.gpsimd
        def _(pool):
            start_at_one(pool, [*s_ve.values(), *s_rstd.values(), s_tree, s_qk, s_q0, s_base, s_take, s_put, s_wl[1]])
            made = 0

            def own(ins):
                nonlocal made
                made += 1
                ins.then_inc(s_setup, 1)
                pool.wait_ge(s_setup, made)

            own(pool.memset(ident[:, :], 0.0))
            own(pool.affine_select(out=ident[:, :], in_=ident[:, :], compare_op=ALU.not_equal, fill=1.0, base=0,
                                   pattern=[[-1, P]], channel_multiplier=1))
            pool.memset(minus_half[:, :], -0.5)
            own(pool.memset(ones[:, :], 1.0))
            pool.iota(iota_e[:, :], pattern=[[1, E]], base=0, channel_multiplier=0, allow_small_or_imprecise_dtypes=True)
            pool.iota(iota_t[:, :], pattern=[[1, TS]], base=0, channel_multiplier=0, allow_small_or_imprecise_dtypes=True)
            own(pool.iota(iota_p[:, :], pattern=[[0, 1]], base=0, channel_multiplier=1, allow_small_or_imprecise_dtypes=True))
            pool.sem_inc(s_const, 1)

            def make_masks():
                pool.memset(mask_f, 1.0).then_inc(s_setup, 1)
                for side in range(2):
                    pool.wait_ge(s_setup, made + 1 + side * 2 * LEVELS)
                    for l in range(LEVELS):
                        h = 2 ** l
                        for odd in range(2):
                            at = (2 * l + odd) * HALF
                            view = mask_f[:, at:at + HALF].rearrange("p (n h) -> p n h", h=h)
                            sign = -1 if side else 1
                            pool.affine_select(out=view, in_=view, compare_op=ALU.is_ge, fill=0.0,
                                               base=(1 + odd) * h - 1 if side else -odd * h,
                                               pattern=[[-sign * 2 * h, HALF // h], [0, h]],
                                               channel_multiplier=sign).then_inc(s_setup, 1)
                pool.wait_ge(s_setup, made + 1 + 4 * LEVELS)
                pool.sem_inc(s_mask, 1)

            def norm(n, s):
                need_apart(pool, s_mom[n], TJ, s, TJ)
                pool.tensor_scalar(var_eps[n][:, :], mom[n][:, :, 1], EPS, None, ALU.add).then_inc(s_ve[n], 1)
                need(pool, s_ve[n], 1, s, 1)
                pool.tensor_tensor(rstd[n][:, :], var_eps[n][:, :], minus_half[:, :], ALU.pow).then_inc(s_rstd[n], 1)

            def step(a, b, c, nxt):
                if c is not None:
                    need(pool, s_on, TJ, c, 0)
                    norm("o", c)
                if a is not None:
                    dec = decay[a.par]
                    need(pool, s_f0, H, a, H)
                    need(pool, s_state, 5, before(a, 2), 5)
                    for l in range(1, LEVELS + 1):
                        if l > 1:
                            need(pool, s_tree, LEVELS, a, l - 1)
                        two = tree(dec, l - 1).rearrange("p (n two) -> p n two", two=2)
                        pool.tensor_tensor(tree(dec, l), two[:, :, 0], two[:, :, 1], ALU.mult).then_inc(s_tree, 1)
                if c is not None:
                    need(pool, s_xn2, TJ, c, 0)
                    norm("u", c)
                if a is not None:
                    need(pool, s_q, H, a, H)
                    need(pool, s_k, H, a, H)
                    need(pool, s_dz, H, a, 0)
                    pool.tensor_tensor(split_chunks(qk), split_chunks(q_raw), keys(kq[a.par]), ALU.mult).then_inc(s_qk, 1)
                    need(pool, s_o, 2, before(a, 2), 2)
                    pool.tensor_tensor(queries(kq[a.par]), q_raw.rearrange("p (m s) -> p m s", s=2 * P),
                                       tree(dec, 0).rearrange("p (m s) -> p m s", s=2 * P), ALU.mult).then_inc(s_q0, 1)
                if nxt is not None:
                    need(pool, s_xn, TJ, nxt, 0)
                    norm("x", nxt)
                if c is not None:
                    need(pool, s_zn, TJ, c, 0)
                    norm("z", c)
                    need(pool, s_xn2, TJ, c, TJ)
                    pool.wait_ge(s_row_out, number(c) * 16 + 16)
                    pool.tensor_tensor(tiles(row_sb, RW)[:, :, D:2 * D], tiles(x1), tiles(xn2), ALU.add).then_inc(s_base, 1)

            norm("x", Step(0, 0, 2))
            make_masks()
            pipeline(pool, step)

            pool.wait_ge(s_aff, NSEQ + 1)
            made += 1 + 4 * LEVELS
            own(pool.iota(iota_r, pattern=[[1, P]], base=0, channel_multiplier=0, allow_small_or_imprecise_dtypes=True))
            own(pool.memset(not_below, 0.0))
            own(pool.affine_select(out=not_below, in_=not_below, compare_op=ALU.is_gt, fill=-1.0, base=0,
                                   pattern=[[1, P]], channel_multiplier=-1))
            pool.sem_inc(s_const, 1)

            pool.wait_ge(s_hot, 1)
            pool.tensor_tensor(hot[:, :, 2, :], hot[:, :, 0, :], iota_t[:, 0:NT].unsqueeze(2).broadcast_to(wide),
                               ALU.mult).then_inc(s_hot_t, 1)

            pool.wait_ge(s_row_out, 16 * NSEQ + 16)
            pool.wait_ge(s_idx, 3)

            def gather(t):
                p = t.par
                need(pool, s_yo, 1, before(t, SLOTS), 1)
                pool.tensor_copy(take_now[:, p:p + 1], column(take_idx, t)).then_inc(s_take, 1)
                need_apart(pool, s_take, 1, t, 1)
                pool.indirect_dma_start(out=gathered[p], out_offset=None, in_=rows,
                                        in_offset=bass.IndirectOffsetOnAxis(ap=take_now[:, p:p + 1], axis=0)).then_inc(s_rows[p], 16)

            def scatter(t):
                p = t.par
                if not isinstance(t.half, int) or t.half > 0:
                    pool.wait_ge(s_out[p], t.half * 16)
                pool.tensor_copy(put_now[:, p:p + 1], column(put_idx, t)).then_inc(s_put, 1)
                need_apart(pool, s_put, 1, t, 1)
                need_apart(pool, s_yo, 1, t, 1)
                pool.indirect_dma_start(out=out, out_offset=bass.IndirectOffsetOnAxis(ap=put_now[:, p:p + 1], axis=0),
                                        in_=y_out[p], in_offset=None, bounds_check=N - 1, oob_is_err=False).then_inc(s_out[p], 16)

            for p in range(SLOTS):
                gather(Step(0, p, SLOTS))

            low_w2(pool, Step(0, 0, SLOTS), 1)

            def turn(t):
                if exists(before(t, -1)):
                    low_w2(pool, before(t, -1), 1)
                if exists(before(t, -SLOTS)):
                    gather(before(t, -SLOTS))
                scatter(t)

            rounds(pool, turn)
            for p in range(SLOTS):
                pool.wait_ge(s_out[p], 16 * ((TILES - p + SLOTS - 1) // SLOTS))

        @block.scalar
        def _(act):
            start_at_one(act, [s_mix, s_xn, s_f, s_on, s_xnt, s_k, s_qs, s_g1, s_v, s_gate, s_kt, s_ont, s_xn2, s_xn2t, s_aff, s_alpha, s_zn, s_xl, s_now, s_wh, s_hr])
            act.dma_start(wg1_sb.rearrange("p (c n) -> p c n", c=DC), wg1.rearrange("(c p) n -> p c n", p=P)).then_inc(s_wvg, 16)
            act.dma_start(wv_sb.rearrange("p (c n) -> p c n", c=DC), wv.rearrange("(c p) n -> p c n", p=P)).then_inc(s_wvg, 16)
            act.dma_start(wg2_sb, wg2).then_inc(s_wvg, 16)

            def copy(dst, src):
                return act.activation(dst, src, ACT.Copy)

            def mix(b, l, h):
                need(act, s_lev, H * LEVELS, b, H * (l - 1) + h + 1 if l > 0 else 0)
                if l == 0:
                    need(act, s_k, H, b, h + 1)
                for odd in range(2):
                    if l > 0:
                        need(act, s_up, 2 * H * LEVELS, b, 2 * (H * (l - 1) + h) + odd + 1)
                    copy(mixed_to(k_mix[l % 2], h, l, odd), mixed_from(kq[b.par], h, l, odd)).then_inc(s_mix, 1)

            def normed(n, dst, src, s, j, done):
                act.activation(dst, tiles(src)[:, j], ACT.Identity, bias=shift[n][:, j:j + 1],
                               scale=rstd[n][:, j:j + 1]).then_inc(done, 1)

            def x_norm(a):
                need(act, s_shift["x"], 1, a, 1)
                need(act, s_tp, DC, a, 0)
                for j in range(TJ):
                    normed("x", tiles(xn)[:, j], x_sb[a.par], a, j, s_xn)

            def xn_copy(a, i):
                need(act, s_tp, DC, a, i + 1)
                if i == 0:
                    need(act, s_gz, 2, a, 0)
                copy(xn_t[:, i * T:(i + 1) * T], bank_a[i][:, :]).then_inc(s_xnt, 1)

            def k_sigmoid(a, h):
                need(act, s_kz, H, a, h + 1)
                if h == 0:
                    need(act, s_k7, 1, before(a, 2), 1)
                act.activation(keys(kq[a.par], h), split_chunks(bank_a[h][:, :]), ACT.Sigmoid).then_inc(s_k, 1)

            def one_minus_k(a, h):
                if h == 0:
                    need(act, s_up, 2 * H * LEVELS, before(a, 2), 2 * H * LEVELS)
                need(act, s_k, H, a, h + 1)
                act.activation(split_chunks(tree(decay[a.par], 0)[:, h * T:(h + 1) * T]), keys(kq[a.par], h), ACT.Copy,
                               bias=1.0, scale=-1.0).then_inc(s_f, 1)

            def q_sigmoid(a, h):
                need(act, s_qz, H, a, h + 1)
                if h == 0:
                    need(act, s_qk, 1, a, 0)
                    need(act, s_q0, 1, a, 0)
                act.activation(q_raw[:, h * T:(h + 1) * T], bank_a[h][:, :], ACT.Sigmoid).then_inc(s_qs, 1)

            def o_norm(c, j):
                need(act, s_shift["o"], 1, c, 1)
                normed("o", tiles(o_sb)[:, j], o_sb, c, j, s_on)

            def o_copy(c, i):
                need(act, s_ot, DC, c, i + 1)
                if i == 0:
                    need(act, s_y, 2, c, 0)
                copy(o_t[:, i * T:(i + 1) * T], bank_c[i][:, :]).then_inc(s_ont, 1)

            def g1_copy(a):
                need(act, s_g1z, 1, a, 1)
                copy(g1_t, bank_a[0][:, :]).then_inc(s_g1, 1)

            def k_tok_copies(b):
                need(act, s_k7, 1, b, 1)
                need(act, s_kv, 2, b, 0)
                copy(k_tok[:, 0:512], bank_b[0][:, :]).then_inc(s_kt, 1)
                copy(k_tok[:, 512:768], bank_b[1][:, 0:256]).then_inc(s_kt, 1)

            def xn2_norm(c):
                need(act, s_shift["u"], 1, c, 1)
                need(act, s_base, 1, c, 0)
                need(act, s_stat["z"], TJ, c, 0)
                need(act, s_t2, DC, c, 0)
                for j in range(TJ):
                    normed("u", tiles(xn2)[:, j], x1, c, j, s_xn2)

            def xn2_copies(c):
                need(act, s_affz, 1, c, 0)
                for i in range(DC):
                    need(act, s_t2, DC, c, i + 1)
                    copy(xn2_t[:, i * T:(i + 1) * T], bank_c[i][:, :]).then_inc(s_xn2t, 1)

            def v_copy(a, i):
                if i == 0:
                    need(act, s_o, 2, before(a, 2), 2)
                need(act, s_vz, 2, a, i + 1)
                copy(v_sb[a.par][:, i * 512:(i + 1) * 512], bank_a[1 - i][:, :]).then_inc(s_v, 1)

            def gate_sigmoid(a, i):
                if i == 0:
                    need(act, s_og, 2, before(a, 2), 2)
                need(act, s_gz, 2, a, i + 1)
                act.activation(gate[a.par][:, i * 512:(i + 1) * 512], bank_a[1 - i][:, :], ACT.Sigmoid).then_inc(s_gate, 1)

            def affinities(c):
                need(act, s_affz, 1, c, 1)
                need(act, s_best, 1, c, 1)
                copy(aff_of(c), bank_c[0][:, 0:TJ * E]).then_inc(s_aff, 1)
                act.activation(tiles(row_sb, RW)[:, :, 2 * D], aff_best[:, :], ACT.Sigmoid).then_inc(s_alpha, 1)

            def zn_norm(c):
                need(act, s_shift["z"], 1, c, 1)
                act.wait_ge(s_row_out, number(c) * 16 + 16)
                for j in range(TJ):
                    normed("z", tiles(row_sb, RW)[:, j, 0:D], xn2, c, j, s_zn)

            def step(a, b, c, nxt):
                def of(s, f, *args):
                    if s is not None:
                        f(s, *args)

                of(a, xn_copy, 0)
                of(b, mix, 1, 0)
                of(a, xn_copy, 1)
                of(b, mix, 1, 1)
                of(a, k_sigmoid, 0)
                of(b, mix, 2, 0)
                of(b, mix, 2, 1)
                of(c, o_norm, 0)
                of(c, o_norm, 1)
                of(b, mix, 3, 0)
                of(c, o_norm, 2)
                of(c, o_norm, 3)
                of(b, mix, 3, 1)
                of(a, k_sigmoid, 1)
                of(a, one_minus_k, 0)
                of(b, mix, 4, 0)
                of(a, q_sigmoid, 0)
                of(c, o_copy, 0)
                of(b, mix, 4, 1)
                of(c, o_copy, 1)
                of(a, one_minus_k, 1)
                for l in (5, 6):
                    for h in range(H):
                        of(b, mix, l, h)
                of(a, q_sigmoid, 1)
                of(b, k_tok_copies)
                of(a, g1_copy)
                of(a, v_copy, 0)
                of(c, xn2_norm)
                of(a, v_copy, 1)
                of(a, gate_sigmoid, 0)
                of(c, xn2_copies)
                of(a, gate_sigmoid, 1)
                of(nxt, x_norm)
                of(a, mix, 0, 0)
                of(a, mix, 0, 1)
                of(c, zn_norm)
                of(c, affinities)

            x_norm(Step(0, 0, 2))
            pipeline(act, step)

            act.wait_ge(s_small, 64)
            act.wait_ge(s_idx, 3)

            def gains(t):
                e = act.value_load(expert_of(t), min_val=0, max_val=E - 1)
                need(act, s_zt, 1, t, 1)
                need(act, s_h, 2, before(t, 2), 2)
                for i in range(DC):
                    act.activation(xl_t[t.par % 2][:, i * P:(i + 1) * P], bank_b[0][:, i * P:(i + 1) * P], ACT.Identity,
                                   bias=b_col[:, bass.ds(e * DC + i, 1)], scale=g_col[:, bass.ds(e * DC + i, 1)]).then_inc(s_xl, 1)

            def copy_w1(t, n):
                e = act.value_load(expert_of(t), min_val=0, max_val=E - 1)
                need(act, s_h, 2, before(t, 1), n + 1)
                w = slice(n * F // 2, (n + 1) * F // 2)
                src = w1_sb[:, bass.ds(e * (DC * F), DC * F)].rearrange("p (c f) -> p c f", c=DC)
                copy(w1_now.rearrange("p (c f) -> p c f", c=DC)[:, :, w], src[:, :, w]).then_inc(s_now, 1)

            def high_w2(t, n):
                e = act.value_load(expert_of(t), min_val=0, max_val=E - 1)
                need(act, s_ye, 1, before(t, 2), 1)
                w = FC * D // 2
                copy(w2_high[t.par % 2][:, n * w:(n + 1) * w], w2_sb[:, bass.ds(e * (FC * D) + n * w, w)]).then_inc(s_wh, 1)

            def relu(t):
                need(act, s_ye, 1, t, 0)
                for i in range(2):
                    need(act, s_hb, 2, t, i + 1)
                    w = slice(i * F // 2, (i + 1) * F // 2)
                    act.activation(h_high[:, w], h_sb[:, w], ACT.Relu).then_inc(s_hr, 1)

            def turn(t):
                relu(t)
                one = before(t, -1) if exists(before(t, -1)) else None
                two = before(t, -2) if exists(before(t, -2)) else None
                if one is not None:
                    high_w2(one, 0)
                if two is not None:
                    copy_w1(two, 0)
                if one is not None:
                    high_w2(one, 1)
                if two is not None:
                    gains(two)
                    copy_w1(two, 1)

            act.wait_ge(s_w1, 16 * E)
            act.wait_ge(s_w2, 16 * E)
            act.wait_ge(s_row_out, 16 * NSEQ + 16)
            t0, t1 = Step(0, 0, SLOTS), Step(0, 1, SLOTS)
            for n in range(2):
                copy_w1(t0, n)
            gains(t0)
            gains(t1)
            for n in range(2):
                high_w2(t0, n)
            for n in range(2):
                copy_w1(t1, n)
            rounds(act, turn)

        @block.tensor
        def _(pe):
            start_at_one(pe, [s_tp, s_kz, s_qz, s_g1z, s_vz, s_gz, s_dz, s_lev, s_k7, s_kv, s_o, s_ot, s_y, s_t2, s_affz, s_zt, s_h, s_ye])
            def level(b, l, h):
                buf = kq[b.par]
                if l == 0:
                    need(pe, s_q0, 1, b, 1)
                need(pe, s_mix, 2 * H * LEVELS, b, 2 * (H * l + h + 1))
                need(pe, s_pick, 2 * LEVELS, b, 2 * max(l - 1, 0))
                for m in range(h * PAIRS // H, (h + 1) * PAIRS // H):
                    bank = bank_l[l % 2][:, m * P:(m + 1) * P].rearrange("p (two n h) -> p two n h", two=2, h=2 ** l)
                    ins = pe.matmul(bank, k_mix[l % 2][:, m * P:(m + 1) * P], level_queries(buf, m, l), start=True, stop=True)
                ins.then_inc(s_lev, 1)

            def transposes(a, i):
                need(pe, s_xn, TJ, a, TJ)
                need(pe, s_at0, H, a, 0)
                for j in range(TJ):
                    m = pe.transpose(bank_a[i][:, j * P:(j + 1) * P], tiles(xn)[:, j, i * P:(i + 1) * P], ident[:, :])
                m.then_inc(s_tp, 1)

            def channels(w, width, h, bank, i):
                return pe.matmul(bank[:, :], w[:, i * width + h * P:i * width + (h + 1) * P], xn_t[:, i * T:(i + 1) * T],
                                 start=(i == 0), stop=(i == DC - 1))

            def k_proj(a, h, i):
                need(pe, s_xnt, DC, a, max(h, i) + 1)
                m = channels(wk_sb, D, h, bank_a[h], i)
                if i == DC - 1:
                    m.then_inc(s_kz, 1)

            def q_proj(a, h, i):
                need(pe, s_k, H, a, h + 1)
                m = channels(wq_sb, D, h, bank_a[h], i)
                if i == DC - 1:
                    m.then_inc(s_qz, 1)

            def g1_proj(a, i):
                need(pe, s_q, H, a, 1)
                m = channels(wg1_sb, G1, 0, bank_a[0], i)
                if i == DC - 1:
                    m.then_inc(s_g1z, 1)

            def v_proj(a, half):
                if half == 0:
                    need(pe, s_q, H, a, 2)
                else:
                    need(pe, s_g1, 1, a, 1)
                for j in range(2):
                    for i in range(DC):
                        t0 = i * T + (2 * half + j) * P
                        m = pe.matmul(bank_a[1 - half][:, j * D:(j + 1) * D], xn_t[:, t0:t0 + P], wv_sb[:, i * D:(i + 1) * D],
                                      start=(i == 0), stop=(i == DC - 1))
                m.then_inc(s_vz, 1)

            def gate_proj(a, half):
                need(pe, s_g1, 1, a, 1)
                need(pe, s_v, 2, a, half + 1)
                for j in range(2):
                    t0 = (2 * half + j) * P
                    m = pe.matmul(bank_a[1 - half][:, j * D:(j + 1) * D], g1_t[:, t0:t0 + P], wg2_sb[:, :], start=True, stop=True)
                m.then_inc(s_gz, 1)

            def diagonal(a, h):
                need(pe, s_qk, 1, a, 1)
                need(pe, s_gate, 2, a, h + 1)
                pe.matmul(bank_a[1 - h][:, :], ones[:, :], qk[:, h * T:(h + 1) * T], start=True, stop=True).then_inc(s_dz, 1)

            def k_transposes(b):
                need(pe, s_up, 2 * H * LEVELS, b, 2 * H * LEVELS)
                need(pe, s_og, 2, b, 0)
                for c in range(TJ - 1):
                    for h in range(H):
                        n = c * H + h
                        m = pe.transpose(bank_b[n // 4][:, n % 4 * P:(n % 4 + 1) * P],
                                         chunk(kq[b.par], h, c, KEY), ident[:, :])
                m.then_inc(s_k7, 1)

            def key_values(b):
                need(pe, s_v, 2, b, 2)
                for c in range(TJ - 1):
                    for h in range(H):
                        n = c * H + h
                        if n % 4 == 0:
                            need(pe, s_kt, 2, b, n // 4 + 1)
                        if n == 4:
                            m.then_inc(s_kv, 1)
                        m = pe.matmul(bank_b[n // 4][:, n % 4 * P:(n % 4 + 1) * P], k_tok[:, n * P:(n + 1) * P],
                                      v_sb[b.par][:, n * P:(n + 1) * P], start=True, stop=True)
                m.then_inc(s_kv, 1)

            def outputs(b, half, between=None):
                need(pe, s_pick, 2 * LEVELS, b, 2 * LEVELS)
                need(pe, s_state, 5, b, 5)
                for c in (2 * half, 2 * half + 1):
                    for h in range(H):
                        dst = bank_b[half][:, c % 2 * D + h * P:c % 2 * D + (h + 1) * P]
                        t0 = h * T + c * P
                        if c > 0:
                            n = (c - 1) * H + h
                            pe.matmul(dst, chunk(kq[b.par], h, c, QUERY), state[:, n * P:(n + 1) * P], start=True, stop=False)
                        m = pe.matmul(dst, attn_t[b.par][:, t0:t0 + P], v_sb[b.par][:, c * D + h * P:c * D + (h + 1) * P],
                                      start=(c == 0), stop=True)
                        if (c % 2, h) == (1, H - 1):
                            m.then_inc(s_o, 1)
                        if between is not None:
                            between(2 * (c * H + h))
                            between(2 * (c * H + h) + 1)

            def o_transposes(c, i):
                if i == 0:
                    need(pe, s_aff, 1, c, 0)
                    need(pe, s_best, 1, c, 0)
                else:
                    need(pe, s_xn2t, DC, c, 0)
                for j in range(TJ):
                    need(pe, s_on, TJ, c, TJ if i else j + 1)
                    m = pe.transpose(bank_c[i][:, j * P:(j + 1) * P], tiles(o_sb)[:, j, i * P:(i + 1) * P], ident[:, :])
                m.then_inc(s_ot, 1)

            def out_proj(c, half, j):
                need(pe, s_ont, DC, c, DC)
                for i in range(DC):
                    t0 = i * T + (2 * half + j) * P
                    m = pe.matmul(bank_c[half][:, j * D:(j + 1) * D], o_t[:, t0:t0 + P], wo_sb[:, i * D:(i + 1) * D],
                                  start=(i == 0), stop=(i == DC - 1))
                if j == 1:
                    m.then_inc(s_y, 1)

            def xn2_transposes(c):
                need(pe, s_x1, 2, c, 2)
                for i in range(DC):
                    for j in range(TJ):
                        need(pe, s_xn2, TJ, c, TJ if i else j + 1)
                        m = pe.transpose(bank_c[i][:, j * P:(j + 1) * P], tiles(xn2)[:, j, i * P:(i + 1) * P], ident[:, :])
                    m.then_inc(s_t2, 1)

            def affinity(c, n):
                j, i = n // DC, n % DC
                if n == 0:
                    need(pe, s_xn2t, DC, c, DC)
                m = pe.matmul(bank_c[0][:, j * E:(j + 1) * E], xn2_t[:, i * T + j * P:i * T + (j + 1) * P],
                              cent_sb[:, i * E:(i + 1) * E], start=(i == 0), stop=(i == DC - 1))
                if n == DC * TJ - 1:
                    m.then_inc(s_affz, 1)

            def step(a, b, c, nxt):
                def of(s, f, *args):
                    if s is not None:
                        f(s, *args)

                if b is not None and isinstance(b.half, int) and number(b) == 0:
                    pe.wait_ge(s_wo, DC)
                    pe.wait_ge(s_small, 64)

                of(b, level, 0, 0)
                of(a, transposes, 0)
                of(a, transposes, 1)
                of(b, level, 0, 1)
                of(a, k_proj, 0, 0)
                of(b, level, 1, 0)
                of(a, k_proj, 0, 1)
                of(b, level, 1, 1)
                of(a, k_proj, 1, 0)
                of(b, level, 2, 0)
                of(a, k_proj, 1, 1)
                of(b, level, 2, 1)
                of(a, q_proj, 0, 0)
                of(b, level, 3, 0)
                of(a, q_proj, 0, 1)
                of(b, level, 3, 1)
                of(c, o_transposes, 0)
                of(c, o_transposes, 1)
                of(b, level, 4, 0)
                of(a, q_proj, 1, 0)
                of(b, level, 4, 1)
                of(c, out_proj, 0, 0)
                of(b, level, 5, 0)
                of(c, out_proj, 0, 1)
                of(b, level, 5, 1)
                of(c, out_proj, 1, 0)
                of(b, level, 6, 0)
                of(c, out_proj, 1, 1)
                of(b, level, 6, 1)
                of(a, q_proj, 1, 1)
                if b is None:
                    pe.wait_ge(s_wvg, 48)
                of(a, g1_proj, 0)
                of(b, k_transposes)
                of(a, g1_proj, 1)
                of(b, key_values)
                of(a, v_proj, 0)
                of(a, v_proj, 1)
                of(a, gate_proj, 0)
                if a is None:
                    of(b, outputs, 0)
                    of(b, outputs, 1)
                    of(c, xn2_transposes)
                    for n in range(DC * TJ):
                        of(c, affinity, n)
                    return
                of(c, xn2_transposes)
                of(a, gate_proj, 1)
                of(a, diagonal, 0)
                if b is not None:
                    outputs(b, 0, None if c is None else lambda n: affinity(c, n))
                of(a, diagonal, 1)
                of(b, outputs, 1)

            pe.wait_ge(s_const, 1)
            pe.wait_ge(s_wqk, 32)
            pipeline(pe, step)

            pe.wait_ge(s_r, 5)
            pe.wait_ge(s_const, 2)
            pe.matmul(bank_a[0][:, 0:WIDE], not_below, onehot, start=True, stop=True)
            pe.matmul(bank_a[1][:, 0:WIDE], ones[:, :], onehot, start=True, stop=True).then_inc(s_rank, 1)
            for g in range(4):
                pe.wait_ge(s_hot, g + 3)
                pe.wait_ge(s_hot_t, 1)
                for t in range(g * NT // 4, (g + 1) * NT // 4):
                    m = pe.matmul(bank_b[1][:, 0:3 * TS], lo_hot[:, t * P:(t + 1) * P], hi_hot[:, t * 3 * TS:(t + 1) * 3 * TS],
                                  start=(t == 0), stop=(t == NT - 1))
            m.then_inc(s_inv, 1)

            def z_transposes(t):
                p = t.par
                pe.wait_ge(s_rows[p], t.half * 16 + 16)
                need(pe, s_xl, DC, t, 0)
                for i in range(DC):
                    m = pe.transpose(bank_b[0][:, i * P:(i + 1) * P], gathered[p][:, i * P:(i + 1) * P], ident[:, :])
                m.then_inc(s_zt, 1)

            def up(t):
                need(pe, s_xl, DC, t, DC)
                for k in range(FC):
                    if k % 4 == 0:
                        need(pe, s_hb, 2, before(t, 1), k // 4 + 1)
                        need(pe, s_now, 2, t, k // 4 + 1)
                    for i in range(DC):
                        m = pe.matmul(bank_a[k // 4][:, k % 4 * P:(k % 4 + 1) * P], w1_now[:, i * F + k * P:i * F + (k + 1) * P],
                                      xl_t[t.par % 2][:, i * P:(i + 1) * P], start=(i == 0), stop=(i == DC - 1))
                    if k % 4 == 3:
                        m.then_inc(s_h, 1)

            def down(t):
                p = t.par % 2
                need(pe, s_yb, 1, before(t, 2), 1)
                for k in range(FC):
                    if k % 4 == 0:
                        need(pe, s_hr, 2, t, k // 4 + 1)
                        need(pe, s_hl, 2, t, k // 4 + 1)
                        need(pe, s_wh, 2, t, k // 4 + 1)
                        need(pe, s_wl[k // 4], 1, t, 1)
                    for n, (h, w) in enumerate(((h_low, w2_high), (h_high, w2_low), (h_high, w2_high))):
                        m = pe.matmul(bank_c[p][:, 0:D], h[:, k * P:(k + 1) * P], w[p][:, k * D:(k + 1) * D],
                                      start=(k == 0 and n == 0), stop=(k == FC - 1 and n == 2))
                m.then_inc(s_ye, 1)

            pe.wait_ge(s_idx, 3)
            pe.wait_ge(s_w1, 16 * E)
            z_transposes(Step(0, 0, SLOTS))
            z_transposes(Step(0, 1, SLOTS))
            up(Step(0, 0, SLOTS))
            pe.wait_ge(s_w2, 16 * E)

            def turn(t):
                if exists(before(t, -1)):
                    up(before(t, -1))
                if exists(before(t, -2)):
                    z_transposes(before(t, -2))
                down(t)

            rounds(pe, turn)

        @block.vector
        def _(dve):
            start_at_one(dve, [*s_stat.values(), *s_mom.values(), *s_shift.values(), s_f0, s_q, s_up, s_pick, s_state, s_og,
                               s_x1, s_at0, s_best, s_hb, s_wl[0], s_hl, s_yb, s_yo])
            def sums(n, src, js):
                for j in js:
                    dve.bn_stats(stat[n][:, j, :], tiles(src)[:, j]).then_inc(s_stat[n], 1)

            def moments(n, s):
                for j in range(TJ):
                    need_apart(dve, s_stat[n], TJ, s, j + 1)
                    dve.bn_aggr(mom[n][:, j, :], stat[n][:, j, :]).then_inc(s_mom[n], 1)

            def stats(n, src, s):
                sums(n, src, range(TJ))
                moments(n, s)

            def shifts(n, s):
                need(dve, s_rstd[n], 1, s, 1)
                dve.scalar_tensor_tensor(out=shift[n][:, :], in0=mom[n][:, :, 0], scalar=-1.0, in1=rstd[n][:, :],
                                         op0=ALU.mult, op1=ALU.mult).then_inc(s_shift[n], 1)

            def x_stats(a):
                dve.wait_ge(s_x[a.par], a.half * 16 + 16)
                stats("x", x_sb[a.par], a)

            def update(b, l, h):
                need(dve, s_lev, H * LEVELS, b, H * l + h + 1)
                if l > 0:
                    need(dve, s_tree, LEVELS, b, l)
                    need(dve, s_up, 2 * H * LEVELS, b, 2 * (H * (l - 1) + h + 1))
                for second in range(2):
                    half = updated(kq[b.par], h, l, second)
                    dve.tensor_tensor(half, half, factor(decay[b.par], h, l, second), ALU.mult).then_inc(s_up, 1)

            def pick(b, l):
                if l == 0:
                    need_apart(dve, s_at0, H, b, H)
                else:
                    need_apart(dve, s_pick, 2 * LEVELS, b, 2 * l)
                for odd in range(2):
                    m0 = (2 * l + odd) * PAIRS * HALF
                    mask = masks[:, m0:m0 + PAIRS * HALF].rearrange("p (m n h) -> p m n h", m=PAIRS, h=2 ** l)
                    scores = bank_l[l % 2][:, :].rearrange("p (m two s) -> p m two s", m=PAIRS, two=2)[:, :, odd, :]
                    dve.copy_predicated(picked(attn_t[b.par], l, odd), mask, scores.rearrange("p m (n h) -> p m n h", h=2 ** l)).then_inc(s_pick, 1)

            def attn_diagonal(a, h):
                need(dve, s_o, 2, before(a, 2), 2)
                need(dve, s_dz, H, a, h + 1)
                dve.tensor_tensor(attn_t[a.par][:, h * T:(h + 1) * T].rearrange("p (n t) -> p n t", t=P),
                                  bank_a[1 - h][:, :].rearrange("p (n t) -> p n t", t=P),
                                  ident[:, :].unsqueeze(1).broadcast_to([P, TJ, P]), ALU.mult).then_inc(s_at0, 1)

            def largest(c):
                need(dve, s_affz, 1, c, 1)
                need(dve, s_alpha, 1, c, 0)
                dve.tensor_reduce(aff_best[:, :], bank_c[0][:, 0:TJ * E].rearrange("p (j e) -> p j e", e=E), AX_X,
                                  ALU.max).then_inc(s_best, 1)

            def decays(a, h):
                need(dve, s_f, H, a, h + 1)
                f = tree(decay[a.par], 0)[:, h * T:(h + 1) * T]
                dve.scalar_tensor_tensor(out=f, in0=f, scalar=0.5, in1=f, op0=ALU.is_equal,
                                         op1=ALU.subtract).then_inc(s_f0, 1)

            def q_mult(a, h):
                need(dve, s_qs, H, a, h + 1)
                dve.tensor_tensor(q_raw[:, h * T:(h + 1) * T], bank_a[h][:, :], q_raw[:, h * T:(h + 1) * T],
                                  ALU.mult).then_inc(s_q, 1)

            def residual(c, half):
                need(dve, s_y, 2, c, half + 1)
                if half == 0:
                    dve.wait_ge(s_xres, number(c) * 16 + 16)
                    need(dve, s_base, 1, c, 0)
                w = slice(half * 512, half * 512 + 512)
                dve.tensor_tensor(x1[:, w], bank_c[half][:, :], x_res[:, w], ALU.add).then_inc(s_x1, 1)

            def states(b):
                need(dve, s_kv, 2, b, 1)
                f7 = tree(decay[b.par], LEVELS)
                dve.tensor_copy(state[:, 0:D], bank_b[0][:, 0:D]).then_inc(s_state, 1)
                for c in range(1, TJ - 1):
                    for h in range(H):
                        n = c * H + h
                        if h == 0:
                            need(dve, s_state, 5, b, 2 * c - 1)
                        if n == 4:
                            need(dve, s_kv, 2, b, 2)
                        dve.scalar_tensor_tensor(out=state[:, n * P:(n + 1) * P], in0=state[:, (n - H) * P:(n - H + 1) * P],
                                                 scalar=f7[:, h * TJ + c:h * TJ + c + 1],
                                                 in1=bank_b[n // 4][:, n % 4 * P:(n % 4 + 1) * P],
                                                 op0=ALU.mult, op1=ALU.add).then_inc(s_state, 1)

            def gating(b, i):
                if i == 0:
                    need(dve, s_gate, 2, b, 2)
                    need(dve, s_ot, DC, b, 0)
                need(dve, s_o, 2, b, i + 1)
                w = slice(i * 512, i * 512 + 512)
                dve.scalar_tensor_tensor(out=o_sb[:, w], in0=bank_b[i][:, :], scalar=QSCALE, in1=gate[b.par][:, w],
                                         op0=ALU.mult, op1=ALU.mult).then_inc(s_og, 1)

            def step(a, b, c, nxt):
                def of(s, f, *args):
                    if s is not None:
                        f(s, *args)

                def output(b, largest_of=None, diagonal_of=None):
                    of(diagonal_of, attn_diagonal, 0)
                    of(b, gating, 0)
                    if b is not None:
                        need(dve, s_og, 2, b, 1)
                        sums("o", o_sb, (0, 1))
                    of(largest_of, largest)
                    of(diagonal_of, attn_diagonal, 1)
                    of(b, gating, 1)

                def level(l):
                    of(b, update, l, 0)
                    if l > 0:
                        of(b, pick, l - 1)
                    of(b, update, l, 1)

                level(0)
                if c is not None:
                    need(dve, s_og, 2, c, 2)
                    sums("o", o_sb, (2, 3))
                    moments("o", c)
                level(1)
                if c is not None:
                    need(dve, s_on, TJ, c, 0)
                    shifts("o", c)
                level(2)
                level(3)
                of(a, decays, 0)
                level(4)
                of(a, q_mult, 0)
                level(5)
                of(a, decays, 1)
                level(6)
                of(b, pick, 6)
                if c is not None:
                    for half in range(2):
                        residual(c, half)
                        if a is None:
                            need(dve, s_x1, 2, c, half + 1)
                            sums("u", x1, (2 * half, 2 * half + 1))
                of(a, q_mult, 1)
                if c is not None:
                    if a is not None:
                        need(dve, s_x1, 2, c, 2)
                        sums("u", x1, range(TJ))
                    moments("u", c)
                if a is None:
                    of(b, states)
                    if c is not None:
                        need(dve, s_xn2, TJ, c, 0)
                        shifts("u", c)
                    of(b, output)
                    if c is not None:
                        need(dve, s_xn2, TJ, c, TJ)
                        stats("z", xn2, c)
                        need(dve, s_zn, TJ, c, 0)
                        shifts("z", c)
                        largest(c)
                    return
                if c is not None:
                    need(dve, s_xn2, TJ, c, 0)
                    shifts("u", c)
                of(nxt, x_stats)
                of(b, states)
                if c is not None:
                    need(dve, s_xn2, TJ, c, TJ)
                    stats("z", xn2, c)
                if nxt is not None:
                    need(dve, s_xn, TJ, nxt, 0)
                    shifts("x", nxt)
                if c is not None:
                    need(dve, s_zn, TJ, c, 0)
                    shifts("z", c)
                output(b, c, a)
                if b is None:
                    dve.wait_ge(s_mask, 1)
                    dve.tensor_copy(masks[:, :].rearrange("p (l m s) -> p l m s", m=PAIRS, s=HALF),
                                    mask_f.rearrange("p (l s) -> p l s", s=HALF).unsqueeze(2).broadcast_to([P, 2 * LEVELS, PAIRS, HALF])).then_inc(s_mask, 1)
                    dve.wait_ge(s_mask, 2)

            x_stats(Step(0, 0, 2))
            shifts("x", Step(0, 0, 2))
            dve.wait_ge(s_wo_in, 32)
            for i in range(DC):
                dve.tensor_scalar(wo_sb[:, i * D:(i + 1) * D], wo_sb[:, i * D:(i + 1) * D], norm_col[:, i:i + 1], None,
                                  ALU.mult).then_inc(s_wo, 1)
            pipeline(dve, step)

            done = 0

            def own(ins):
                nonlocal done
                done += 1
                ins.then_inc(s_r, 1)
                dve.wait_ge(s_r, done)

            def te(ap):
                return ap.rearrange("p (t e) -> p t e", e=E)

            def over_t(ap):
                return ap.unsqueeze(1).broadcast_to([P, NT, E])

            def over_e(ap):
                return ap.unsqueeze(2).broadcast_to([P, NT, E])

            dve.wait_ge(s_aff, NSEQ + 1)
            dve.wait_ge(s_zn, TJ * NSEQ + 1)
            dve.wait_ge(s_base, NSEQ + 1)
            own(dve.tensor_reduce(aff_max, te(aff[:, :]), AX_X, ALU.max))
            own(dve.tensor_tensor(te(is_max), te(aff[:, :]), over_e(aff_max), ALU.is_equal))
            own(dve.scalar_tensor_tensor(out=te(is_max), in0=te(is_max), scalar=-float(E), in1=over_t(iota_e[:, :]),
                                         op0=ALU.mult, op1=ALU.add))
            own(dve.tensor_reduce(first, te(is_max), AX_X, ALU.min))
            own(dve.scalar_tensor_tensor(out=te(onehot), in0=over_t(iota_e[:, :]), scalar=-float(E), in1=over_e(first),
                                         op0=ALU.add, op1=ALU.is_equal))
            own(dve.memset(small[:, 0:1], 0.0))
            dve.wait_ge(s_rank, 1)
            own(dve.tensor_copy(count_e.rearrange("p (e t) -> p t e", e=E), te(bank_a[1][:, 0:WIDE])))
            own(dve.tensor_tensor_scan(out=cum_e, data0=ones_wide(), data1=count_e, initial=0.0, op0=ALU.mult, op1=ALU.add))
            prior = small[:, 0:E]
            upto = small[:, 1:E + 1]
            n_e = small[:, 2 * E:3 * E]
            nt_e = small[:, 4 * E:5 * E]
            t_upto = small[:, 5 * E:6 * E]
            off = small[:, 6 * E:7 * E]
            own(dve.tensor_copy(upto, cum_e.rearrange("p (e t) -> p e t", e=E)[:, :, NT - 1]))
            own(dve.tensor_tensor(n_e, upto, prior, ALU.subtract))
            own(dve.tensor_scalar(ntile_i[:, 0:E], n_e, float(P - 1), None, ALU.add))
            own(dve.tensor_scalar(ntile_i[:, E:2 * E], ntile_i[:, 0:E], 7, None, ALU.arith_shift_right))
            own(dve.tensor_copy(nt_e, ntile_i[:, E:2 * E]))
            own(dve.tensor_tensor_scan(out=t_upto, data0=ones[:, 0:E], data1=nt_e, initial=0.0, op0=ALU.mult, op1=ALU.add))
            own(dve.tensor_tensor(off, t_upto, nt_e, ALU.subtract))
            own(dve.scalar_tensor_tensor(out=off, in0=off, scalar=float(P), in1=prior, op0=ALU.mult, op1=ALU.subtract))
            own(dve.tensor_tensor(te(place), te(bank_a[0][:, 0:WIDE]), cum_e.rearrange("p (e t) -> p t e", e=E), ALU.add))
            own(dve.tensor_tensor(te(place), te(place), over_t(off), ALU.add))
            own(dve.tensor_tensor(place, place, onehot, ALU.mult))
            own(dve.tensor_reduce(slot, te(place), AX_X, ALU.add))
            own(dve.tensor_copy(slot_i, slot))
            own(dve.tensor_scalar(hi_i, slot_i, 7, None, ALU.arith_shift_right))
            own(dve.tensor_scalar(lo_i, slot_i, P - 1, None, ALU.bitwise_and))
            own(dve.tensor_copy(hi_f, hi_i))
            own(dve.tensor_copy(lo_f, lo_i))
            dve.tensor_tensor(hot[:, :, 0, :], iota_t[:, :].unsqueeze(1).broadcast_to(wide), hi_f.unsqueeze(2).broadcast_to(wide),
                              ALU.is_equal).then_inc(s_hot, 1)
            dve.wait_ge(s_hot, 1)
            dve.tensor_scalar(hot[:, :, 1, :], hot[:, :, 0, :], iota_p[:, 0:1], None, ALU.mult).then_inc(s_hot, 1)
            dve.wait_ge(s_const, 2)
            lo3 = lo_hot.rearrange("p (t r) -> p t r", r=P)
            for g in range(4):
                n = NT // 4
                dve.tensor_tensor(lo3[:, g * n:(g + 1) * n], iota_r.unsqueeze(1).broadcast_to([P, n, P]),
                                  lo_f[:, g * n:(g + 1) * n].unsqueeze(2).broadcast_to([P, n, P]), ALU.is_equal).then_inc(s_hot, 1)
            own(dve.tensor_tensor(ge_f[:, 0:TS * (E - 1)].rearrange("p (s e) -> p s e", e=E - 1),
                                  iota_t[:, :].unsqueeze(2).broadcast_to([P, TS, E - 1]),
                                  t_upto[:, 0:E - 1].unsqueeze(1).broadcast_to([P, TS, E - 1]), ALU.is_ge))
            own(dve.tensor_reduce(texp_f, ge_f[:, 0:TS * (E - 1)].rearrange("p (s e) -> p s e", e=E - 1), AX_X, ALU.add))
            dve.tensor_copy(tile_expert[:, :], texp_f).then_inc(s_idx, 1)
            dve.wait_ge(s_inv, 1)
            own(dve.tensor_copy(slot_f[:, 0:3 * TS], bank_b[1][:, 0:3 * TS]))
            own(dve.scalar_tensor_tensor(out=slot_f[:, 3 * TS:4 * TS], in0=slot_f[:, 2 * TS:3 * TS], scalar=float(P),
                                         in1=slot_f[:, TS:2 * TS], op0=ALU.mult, op1=ALU.add))
            own(dve.tensor_scalar(slot_f[:, 0:TS], slot_f[:, 0:TS], -float(SKIP), float(SKIP), ALU.mult, ALU.add))
            dve.tensor_copy(take_idx[:, :], slot_f[:, 3 * TS:4 * TS]).then_inc(s_idx, 1)
            dve.tensor_tensor(put_idx[:, :], slot_f[:, 0:TS], slot_f[:, 3 * TS:4 * TS], ALU.add).then_inc(s_idx, 1)

            dve.wait_ge(s_idx, 3)
            dve.wait_ge(s_b2, 16)

            def bias_h(t, n):
                e = dve.value_load(expert_of(t), min_val=0, max_val=E - 1)
                need(dve, s_hl, 2, t, 0)
                need(dve, s_h, 2, t, n + 1)
                b = b1_col[:, bass.ds(e * FC + n * FC // 2, FC // 2)]
                dve.tensor_tensor(h_sb[:, n * 512:(n + 1) * 512].rearrange("p (k t) -> p k t", t=P),
                                  bank_a[n][:, :].rearrange("p (k t) -> p k t", t=P),
                                  b.unsqueeze(2).broadcast_to([P, FC // 2, P]), ALU.add).then_inc(s_hb, 1)

            def low_h(t):
                for n in range(2):
                    need(dve, s_hr, 2, t, n + 1)
                    w = slice(n * F // 2, (n + 1) * F // 2)
                    dve.scalar_tensor_tensor(out=h_low[:, w], in0=h_sb[:, w], scalar=0.0, in1=h_high[:, w],
                                             op0=ALU.max, op1=ALU.subtract).then_inc(s_hl, 1)

            def finish(t):
                p = t.par
                e = dve.value_load(expert_of(t), min_val=0, max_val=E - 1)
                need(dve, s_ye, 1, t, 1)
                need(dve, s_yo, 1, t, 0)
                dve.tensor_tensor(y_sb, bank_c[p % 2][:, 0:D], b2_sb[:, bass.ds(e * D, D)], ALU.add).then_inc(s_yb, 1)
                need(dve, s_yb, 1, t, 1)
                if not isinstance(t.half, int) or t.half > 0:
                    dve.wait_ge(s_out[p], t.half * 16)
                dve.scalar_tensor_tensor(out=y_out[p], in0=y_sb, scalar=gathered[p][:, 2 * D:2 * D + 1],
                                         in1=gathered[p][:, D:2 * D], op0=ALU.mult, op1=ALU.add).then_inc(s_yo, 1)

            def turn(t):
                one = before(t, -1) if exists(before(t, -1)) else None
                low_h(t)
                if one is not None:
                    bias_h(one, 0)
                if not isinstance(t.half, int) or number(t) > 0:
                    finish(before(t, 1))
                if one is not None:
                    bias_h(one, 1)
                    low_w2(dve, one, 0)

            for n in range(2):
                bias_h(Step(0, 0, SLOTS), n)
            low_w2(dve, Step(0, 0, SLOTS), 0)
            rounds(dve, turn)
            finish(Step(LAST, (TILES - 1) % SLOTS, SLOTS))


def kernel(**inputs):
    import concourse.bacc as bacc
    from concourse.bass_utils import run_bass_kernel_spmd

    def columns(a):
        n, d = a.shape
        return a.reshape(n, d // P, P).transpose(2, 0, 1).reshape(P, -1)

    def odd_reversed(a):
        a = a.reshape(-1, 2, P, a.shape[-1])
        return np.stack([a[:, 0], a[:, 1, ::-1]], axis=1)

    g = {k.replace("L0_", ""): np.asarray(v) for k, v in inputs.items()}
    E, F, D = g["ffn_w1"].shape
    arrays = {
        "x": odd_reversed(g["attn_x"]).reshape(g["attn_x"].shape), "wq": g["attn_wq"], "wk": g["attn_wk"], "wv": g["attn_wv"], "wo": g["attn_wo"],
        "wg1": g["attn_wg1"], "wg2": g["attn_wg2"], "norm_w": columns(g["attn_norm_w"][None]),
        "centroids": g["ffn_centroids"].reshape(E, D // P, P).transpose(2, 1, 0).reshape(P, -1),
        "ln_g": columns(g["ffn_ln_g"]), "ln_b": columns(g["ffn_ln_b"]),
        "w1": g["ffn_w1"].reshape(E, F, D // P, P).transpose(3, 0, 2, 1).reshape(P, -1),
        "b1": columns(g["ffn_b1"]),
        "w2": g["ffn_w2"].reshape(E, D, F // P, P).transpose(3, 0, 2, 1).reshape(P, -1),
        "b2": g["ffn_b2"],
    }
    arrays = {k: np.ascontiguousarray(v) for k, v in arrays.items()}
    nc = bacc.Bacc("TRN2", target_bir_lowering=False, num_devices=1)
    args = [nc.dram_tensor(k, v.shape, mybir.dt.from_np(v.dtype), kind="ExternalInput").ap() for k, v in arrays.items()]
    shape = g["attn_x"].shape
    out = nc.dram_tensor("out", (shape[0] * shape[1], shape[2]), F32, kind="ExternalOutput").ap()
    build_program(nc, *args, out)
    got = run_bass_kernel_spmd(nc, [arrays], core_ids=[0])
    return odd_reversed(got.results[0]["out"]).reshape(shape)
```
